# Optimizing a Trainium2 kernel written in Bass

```python
import numpy as np
import jax
import jax.numpy as jnp

def _softmax(x, axis=-1):
    return jax.nn.softmax(x, axis=axis)

def _gelu(x):
    return jax.nn.gelu(x, approximate=True)

def _silu(x):
    return jax.nn.silu(x)

def _sigmoid(x):
    return jax.nn.sigmoid(x)

def _layernorm(x, axis=-1, eps=1e-05):
    m = jnp.mean(x, axis=axis, keepdims=True)
    v = jnp.var(x, axis=axis, keepdims=True)
    return (x - m) / jnp.sqrt(v + eps)

def _scatter_add(tgt, idx, src, axis=0):
    return tgt.at[idx].add(src)

def _segment_sum(src, seg, n):
    return jax.ops.segment_sum(src, seg, n)
kernel_name = 'mk_gnn_preln_d4_gnn_r32_a97d9e'

def setup_inputs(seed: int=0):
    np.random.seed(seed)
    _w = jnp.asarray

    def _rec_inputs():
        import jax
        import jax.numpy as jnp
        _gk = jax.random.key(seed)
        x = -0.000202 + 1 * jax.random.normal(jax.random.fold_in(_gk, 1), (50000, 128), jnp.float32)
        src = jax.random.randint(jax.random.fold_in(_gk, 2), (50000,), 0, 50000, jnp.int32)
        dst = jnp.minimum((50000 * jax.random.uniform(jax.random.fold_in(_gk, 3), (50000,)) ** 2.0).astype(jnp.int32), 49999)
        _o = jnp.argsort(dst, stable=True)
        src = src[_o]
        dst = dst[_o]
        edge_attr_128 = -8.513e-05 + 0.999844 * jax.random.normal(jax.random.fold_in(_gk, 12), (50000, 128), jnp.float32)
        edge_attr_32 = -5.3897e-05 + 0.999841 * jax.random.normal(jax.random.fold_in(_gk, 13), (50000, 32), jnp.float32)
        edge_type_8 = jax.random.randint(jax.random.fold_in(_gk, 15), (50000,), 0, 8, jnp.int32)
        return (x, src, dst, edge_attr_128, edge_attr_32, edge_type_8)
    x, src, dst, edge_attr_128, edge_attr_32, edge_type_8 = _rec_inputs()

    def _L0_gnn_setup():
        import jax, jax.numpy as jnp
        import numpy as np
        RRELU_EVAL_SLOPE = (1.0 / 8.0 + 1.0 / 3.0) / 2.0
        key = jax.random.key(seed)
        ks = jax.random.split(key, 6)
        N, E, D, H = (50000, 20000, 128, 128)
        node_feats = jax.random.normal(ks[0], (N, D), dtype=jnp.float32)
        edge_feats = jax.random.normal(ks[1], (E, D), dtype=jnp.float32)
        src = jax.random.randint(ks[2], (E,), 0, N, dtype=jnp.int64)
        dst = jax.random.randint(ks[3], (E,), 0, N, dtype=jnp.int64)
        W1 = jax.random.normal(ks[4], (2 * D, H), dtype=jnp.float32) / np.sqrt(2 * D)
        b1 = jnp.zeros((H,), dtype=jnp.float32)
        W2 = jax.random.normal(ks[5], (D, H), dtype=jnp.float32) / np.sqrt(D)
        b2 = jnp.zeros((H,), dtype=jnp.float32)
        return {'node_feats': node_feats, 'edge_feats': edge_feats, 'src': src, 'dst': dst, 'W1': W1, 'b1': b1, 'W2': W2, 'b2': b2}
    _L0_gnn_all = _L0_gnn_setup()
    _L0_gnn_in = {k: v for k, v in _L0_gnn_all.items() if k in ('W1', 'b1', 'W2', 'b2')}
    del _L0_gnn_all

    def _L1_gnn_setup():
        import jax, jax.numpy as jnp
        import numpy as np
        DIM_H = 128
        HEADS = 8
        HEAD_DIM = DIM_H // HEADS
        N_NODES = 1250
        N_EDGES = 20000
        BN_EPS = 1e-05

        def _batchnorm(h, gamma, beta):
            mu = jnp.mean(h, axis=0)
            var = jnp.mean((h - mu) ** 2, axis=0)
            return (h - mu) * jax.lax.rsqrt(var + BN_EPS) * gamma + beta

        def _sparse_attn(x, edge_index, Wk, bk, Wv, bv, Wo, bo):
            N = x.shape[0]
            src, dst = (edge_index[0], edge_index[1])
            K = (x @ Wk.T + bk).reshape(N, HEADS, HEAD_DIM)
            V = (x @ Wv.T + bv).reshape(N, HEADS, HEAD_DIM)
            Q = x.reshape(N, HEADS, HEAD_DIM)
            scores = jnp.sum(K[src] * Q[dst], axis=-1) / np.sqrt(HEAD_DIM).astype(np.float32)
            m = jax.ops.segment_max(scores, dst, num_segments=N)
            e = jnp.exp(scores - m[dst])
            denom = jax.ops.segment_sum(e, dst, num_segments=N)
            attn = e / (denom[dst] + 1e-16)
            messages = V[src] * attn[:, :, None]
            out = jax.ops.segment_sum(messages, dst, num_segments=N)
            return out.reshape(N, DIM_H) @ Wo.T + bo
        key = jax.random.key(seed)
        ks = jax.random.split(key, 16)
        s = 0.05
        x = jax.random.normal(ks[0], (N_NODES, DIM_H), dtype=jnp.float32)
        edge_index = jax.random.randint(ks[1], (2, N_EDGES), 0, N_NODES, dtype=jnp.int64)
        p = lambda k, shp: jax.random.normal(k, shp, dtype=jnp.float32) * s
        return {'x': x, 'edge_index': edge_index, 'Wk': p(ks[2], (DIM_H, DIM_H)), 'bk': p(ks[3], (DIM_H,)), 'Wv': p(ks[4], (DIM_H, DIM_H)), 'bv': p(ks[5], (DIM_H,)), 'Wo': p(ks[6], (DIM_H, DIM_H)), 'bo': p(ks[7], (DIM_H,)), 'bn1_g': jnp.ones((DIM_H,), jnp.float32), 'bn1_b': jnp.zeros((DIM_H,), jnp.float32), 'W1': p(ks[8], (2 * DIM_H, DIM_H)), 'b1': p(ks[9], (2 * DIM_H,)), 'W2': p(ks[10], (DIM_H, 2 * DIM_H)), 'b2': p(ks[11], (DIM_H,)), 'bn2_g': jnp.ones((DIM_H,), jnp.float32), 'bn2_b': jnp.zeros((DIM_H,), jnp.float32)}
    _L1_gnn_all = _L1_gnn_setup()
    _L1_gnn_in = {k: v for k, v in _L1_gnn_all.items() if k in ('Wk', 'bk', 'Wv', 'bv', 'Wo', 'bo', 'bn1_g', 'bn1_b', 'W1', 'b1', 'W2', 'b2', 'bn2_g', 'bn2_b')}
    del _L1_gnn_all

    def _L2_gnn_setup():
        import jax, jax.numpy as jnp
        import numpy as np
        N_NODES = 50000
        N_EDGES = 25000
        D = 128
        E_DIM = 32
        LN_EPS = 1e-05

        def _layernorm(x, w, b):
            mu = jnp.mean(x, axis=-1, keepdims=True)
            var = jnp.mean(jnp.square(x - mu), axis=-1, keepdims=True)
            return (x - mu) * jax.lax.rsqrt(var + LN_EPS) * w + b
        key = jax.random.key(seed)
        ks = jax.random.split(key, 8)
        return {'node_attr': jax.random.normal(ks[0], (N_NODES, D), dtype=jnp.float32), 'edge_attr': jax.random.normal(ks[1], (N_EDGES, E_DIM), dtype=jnp.float32), 'edge_index': jax.random.randint(ks[2], (2, N_EDGES), 0, N_NODES, dtype=jnp.int64), 'W_node': jax.random.normal(ks[3], (D, D), dtype=jnp.float32), 'W_center_node': jax.random.normal(ks[4], (D, D), dtype=jnp.float32), 'W_concat_node': jax.random.normal(ks[5], (2 * D, D), dtype=jnp.float32), 'W_edge': jax.random.normal(ks[6], (E_DIM, D), dtype=jnp.float32), 'ln_weight': jnp.ones((D,), dtype=jnp.float32), 'ln_bias': jnp.zeros((D,), dtype=jnp.float32)}
    _L2_gnn_all = _L2_gnn_setup()
    _L2_gnn_in = {k: v for k, v in _L2_gnn_all.items() if k in ('W_node', 'W_center_node', 'W_concat_node', 'W_edge', 'ln_weight', 'ln_bias')}
    del _L2_gnn_all

    def _L3_gnn_setup():
        import jax, jax.numpy as jnp
        import numpy as np
        N_NODES = 50000
        N_EDGES = 18750
        IN_C = 128
        OUT_C = 128
        N_REL = 8
        key = jax.random.key(seed)
        k1, k2, k3, k4 = jax.random.split(key, 4)
        x = jax.random.normal(k1, (N_NODES, IN_C), dtype=jnp.float32)
        edge_index = jax.random.randint(k2, (2, N_EDGES), 0, N_NODES, dtype=jnp.int64)
        edge_type = jax.random.randint(k3, (N_EDGES,), 0, N_REL, dtype=jnp.int64)
        weight = jax.random.normal(k4, (N_REL, IN_C, OUT_C), dtype=jnp.float32)
        bias = jnp.zeros((OUT_C,), dtype=jnp.float32)
        return {'x': x, 'edge_index': edge_index, 'edge_type': edge_type, 'weight': weight, 'bias': bias}
    _L3_gnn_all = _L3_gnn_setup()
    _L3_gnn_in = {k: v for k, v in _L3_gnn_all.items() if k in ('weight', 'bias')}
    del _L3_gnn_all
    return {'x': x, 'src': src, 'dst': dst, 'edge_attr_128': edge_attr_128, 'edge_attr_32': edge_attr_32, 'edge_type_8': edge_type_8, 'L0_gnn_W1': _L0_gnn_in['W1'], 'L0_gnn_b1': _L0_gnn_in['b1'], 'L0_gnn_W2': _L0_gnn_in['W2'], 'L0_gnn_b2': _L0_gnn_in['b2'], 'L1_gnn_Wk': _L1_gnn_in['Wk'], 'L1_gnn_bk': _L1_gnn_in['bk'], 'L1_gnn_Wv': _L1_gnn_in['Wv'], 'L1_gnn_bv': _L1_gnn_in['bv'], 'L1_gnn_Wo': _L1_gnn_in['Wo'], 'L1_gnn_bo': _L1_gnn_in['bo'], 'L1_gnn_bn1_g': _L1_gnn_in['bn1_g'], 'L1_gnn_bn1_b': _L1_gnn_in['bn1_b'], 'L1_gnn_W1': _L1_gnn_in['W1'], 'L1_gnn_b1': _L1_gnn_in['b1'], 'L1_gnn_W2': _L1_gnn_in['W2'], 'L1_gnn_b2': _L1_gnn_in['b2'], 'L1_gnn_bn2_g': _L1_gnn_in['bn2_g'], 'L1_gnn_bn2_b': _L1_gnn_in['bn2_b'], 'L2_gnn_W_node': _L2_gnn_in['W_node'], 'L2_gnn_W_center_node': _L2_gnn_in['W_center_node'], 'L2_gnn_W_concat_node': _L2_gnn_in['W_concat_node'], 'L2_gnn_W_edge': _L2_gnn_in['W_edge'], 'L2_gnn_ln_weight': _L2_gnn_in['ln_weight'], 'L2_gnn_ln_bias': _L2_gnn_in['ln_bias'], 'L3_gnn_weight': _L3_gnn_in['weight'], 'L3_gnn_bias': _L3_gnn_in['bias']}

def reference(x, src, dst, edge_attr_128, edge_attr_32, edge_type_8, L0_gnn_W1, L0_gnn_b1, L0_gnn_W2, L0_gnn_b2, L1_gnn_Wk, L1_gnn_bk, L1_gnn_Wv, L1_gnn_bv, L1_gnn_Wo, L1_gnn_bo, L1_gnn_bn1_g, L1_gnn_bn1_b, L1_gnn_W1, L1_gnn_b1, L1_gnn_W2, L1_gnn_b2, L1_gnn_bn2_g, L1_gnn_bn2_b, L2_gnn_W_node, L2_gnn_W_center_node, L2_gnn_W_concat_node, L2_gnn_W_edge, L2_gnn_ln_weight, L2_gnn_ln_bias, L3_gnn_weight, L3_gnn_bias):
    import jax
    import jax.numpy as jnp

    def _L0_gnn_ref(node_feats, edge_feats, src, dst, W1, b1, W2, b2):
        import jax, jax.numpy as jnp
        import numpy as np
        RRELU_EVAL_SLOPE = (1.0 / 8.0 + 1.0 / 3.0) / 2.0
        N = node_feats.shape[0]
        msg_inp = jnp.concatenate([node_feats[src], edge_feats], axis=-1)
        msg = msg_inp @ W1 + b1
        msg_sum = jax.ops.segment_sum(msg, dst, num_segments=N)
        deg = jax.ops.segment_sum(jnp.ones((dst.shape[0],), msg.dtype), dst, num_segments=N)
        node_msg = msg_sum / jnp.maximum(deg, 1.0)[:, None]
        out = node_msg + (node_msg @ W2 + b2)
        return jnp.where(out >= 0, out, RRELU_EVAL_SLOPE * out)

    def _L1_gnn_ref(x, edge_index, Wk, bk, Wv, bv, Wo, bo, bn1_g, bn1_b, W1, b1, W2, b2, bn2_g, bn2_b):
        import jax, jax.numpy as jnp
        import numpy as np
        DIM_H = 128
        HEADS = 8
        HEAD_DIM = DIM_H // HEADS
        N_NODES = 1250
        N_EDGES = 20000
        BN_EPS = 1e-05

        def _batchnorm(h, gamma, beta):
            mu = jnp.mean(h, axis=0)
            var = jnp.mean((h - mu) ** 2, axis=0)
            return (h - mu) * jax.lax.rsqrt(var + BN_EPS) * gamma + beta

        def _sparse_attn(x, edge_index, Wk, bk, Wv, bv, Wo, bo):
            N = x.shape[0]
            src, dst = (edge_index[0], edge_index[1])
            K = (x @ Wk.T + bk).reshape(N, HEADS, HEAD_DIM)
            V = (x @ Wv.T + bv).reshape(N, HEADS, HEAD_DIM)
            Q = x.reshape(N, HEADS, HEAD_DIM)
            scores = jnp.sum(K[src] * Q[dst], axis=-1) / np.sqrt(HEAD_DIM).astype(np.float32)
            m = jax.ops.segment_max(scores, dst, num_segments=N)
            e = jnp.exp(scores - m[dst])
            denom = jax.ops.segment_sum(e, dst, num_segments=N)
            attn = e / (denom[dst] + 1e-16)
            messages = V[src] * attn[:, :, None]
            out = jax.ops.segment_sum(messages, dst, num_segments=N)
            return out.reshape(N, DIM_H) @ Wo.T + bo
        h_attn = _sparse_attn(x, edge_index, Wk, bk, Wv, bv, Wo, bo)
        h = _batchnorm(x + h_attn, bn1_g, bn1_b)
        ff = jax.nn.relu(h @ W1.T + b1) @ W2.T + b2
        h = _batchnorm(h + ff, bn2_g, bn2_b)
        return h

    def _L2_gnn_ref(node_attr, edge_attr, edge_index, W_node, W_center_node, W_concat_node, W_edge, ln_weight, ln_bias):
        import jax, jax.numpy as jnp
        import numpy as np
        N_NODES = 50000
        N_EDGES = 25000
        D = 128
        E_DIM = 32
        LN_EPS = 1e-05

        def _layernorm(x, w, b):
            mu = jnp.mean(x, axis=-1, keepdims=True)
            var = jnp.mean(jnp.square(x - mu), axis=-1, keepdims=True)
            return (x - mu) * jax.lax.rsqrt(var + LN_EPS) * w + b
        edge_center = edge_index[0]
        edge_neigh = edge_index[1]
        num_nodes = node_attr.shape[0]
        proj_node = node_attr @ W_node
        proj_edge = proj_node[edge_neigh]
        proj_radial = edge_attr @ W_edge
        m_node = jax.ops.segment_sum(proj_edge * proj_radial, edge_center, num_segments=num_nodes)
        proj_center_node = node_attr @ W_center_node
        cat = jnp.concatenate([proj_center_node, m_node], axis=-1)
        h_node = _layernorm(cat @ W_concat_node, ln_weight, ln_bias)
        return h_node

    def _L3_gnn_ref(x, edge_index, edge_type, weight, bias):
        import jax, jax.numpy as jnp
        import numpy as np
        N_NODES = 50000
        N_EDGES = 18750
        IN_C = 128
        OUT_C = 128
        N_REL = 8
        N = x.shape[0]
        src = edge_index[0]
        dst = edge_index[1]
        out = jnp.zeros((N, weight.shape[2]), dtype=x.dtype)
        for r in range(weight.shape[0]):
            rel_mask = (edge_type == r).astype(x.dtype)
            transformed = x @ weight[r]
            msgs = transformed[src] * rel_mask[:, None]
            sums = jax.ops.segment_sum(msgs, dst, num_segments=N)
            counts = jax.ops.segment_sum(rel_mask, dst, num_segments=N)
            mean = jnp.where(counts[:, None] > 0, sums / jnp.maximum(counts, 1.0)[:, None], 0.0)
            out = out + mean
        return out + bias
    edge_index = jnp.stack([src, dst])
    h = jnp.maximum(_layernorm(x, axis=-1), 0.0)
    x = x + _L0_gnn_ref(h, edge_attr_128, src, dst, L0_gnn_W1, L0_gnn_b1, L0_gnn_W2, L0_gnn_b2)
    h = jnp.maximum(_layernorm(x, axis=-1), 0.0)
    x = x + _L1_gnn_ref(h, edge_index, L1_gnn_Wk, L1_gnn_bk, L1_gnn_Wv, L1_gnn_bv, L1_gnn_Wo, L1_gnn_bo, L1_gnn_bn1_g, L1_gnn_bn1_b, L1_gnn_W1, L1_gnn_b1, L1_gnn_W2, L1_gnn_b2, L1_gnn_bn2_g, L1_gnn_bn2_b)
    h = jnp.maximum(_layernorm(x, axis=-1), 0.0)
    x = x + _L2_gnn_ref(h, edge_attr_32, edge_index, L2_gnn_W_node, L2_gnn_W_center_node, L2_gnn_W_concat_node, L2_gnn_W_edge, L2_gnn_ln_weight, L2_gnn_ln_bias)
    h = jnp.maximum(_layernorm(x, axis=-1), 0.0)
    x = x + _L3_gnn_ref(h, edge_index, edge_type_8, L3_gnn_weight, L3_gnn_bias)
    return x

_drawn_inputs = setup_inputs


def setup_inputs(seed=0):
    import zlib

    import numpy as np

    out = dict(_drawn_inputs(seed))
    spreads = {'L0_gnn_b1': (0.0, 0.1),
     'L0_gnn_b2': (0.0, 0.1),
     'L1_gnn_bn1_g': (1.0, 0.2),
     'L1_gnn_bn1_b': (0.0, 0.8),
     'L1_gnn_bn2_g': (1.0, 0.2),
     'L1_gnn_bn2_b': (0.0, 0.1),
     'L2_gnn_ln_weight': (1.0, 0.2),
     'L2_gnn_ln_bias': (0.0, 0.1),
     'L3_gnn_bias': (0.0, 0.696)}
    factors = {'L1_gnn_Wk': 7.024,
     'L1_gnn_bk': 8.0,
     'L1_gnn_bv': 4.92,
     'L1_gnn_bo': 8.0,
     'L1_gnn_b1': 6.725,
     'L1_gnn_b2': 8.0}
    for name, (base, spread) in spreads.items():
        noise = np.random.default_rng([zlib.crc32(name.encode()), seed]).standard_normal(out[name].shape)
        drawn = base * np.exp(spread * noise) if base else spread * noise
        out[name] = jnp.asarray(drawn.astype(out[name].dtype))
    for name, factor in factors.items():
        out[name] = (out[name] * factor).astype(out[name].dtype)
    return out
```

```python
from contextlib import ExitStack

import numpy as np

import concourse.bass as bass
from concourse import mybir

ALU = mybir.AluOpType
ACT = mybir.ActivationFunctionType
F32 = mybir.dt.float32
BF16 = mybir.dt.bfloat16
I32 = mybir.dt.int32

P = 128
D = 128
TILES = 4
ROWS = TILES * P
HEADS = 8
HEAD_DIM = D // HEADS
RELS = 8
EDGE_DIM = 32
EPS = 1e-5
SLOPE = (1.0 / 8.0 + 1.0 / 3.0) / 2.0
FAR = float(1 << 22)
LOW = 1e30
PEEL = 4


def steps_of(rows):
    s = rows // ROWS + 1
    return s + s % 2


class Sizes:
    def __init__(self, nodes, edges):
        self.nodes = nodes
        self.steps = steps_of(max(nodes, edges))
        self.rows = self.steps * ROWS


def run_steps(eng, body, steps, lag):
    for i in range(PEEL):
        body(i, i % 2)
    with eng.Fori(PEEL, steps - 2, 2) as i:
        body(i, 0)
        body(i + 1, 1)
    for i in range(steps - 2, steps + lag):
        body(i, i % 2)


def live(j, steps):
    return not isinstance(j, int) or 0 <= j < steps


def after(eng, sem, j, per=1):
    if isinstance(j, int) and j < 0:
        return
    eng.wait_ge(sem, (j + 1) * per)


def landed(eng, sems, j, u, dmas):
    if isinstance(j, int):
        if j >= 0:
            eng.wait_ge(sems[u], (j // 2 + 1) * 16 * dmas)
    else:
        eng.wait_ge(sems[u], (j - u) * (8 * dmas) + 16 * dmas)


def rows_of(table, i):
    return table.rearrange("(s p t) d -> s p (t d)", p=P, t=TILES)[bass.ds(i, 1), :, :].rearrange(
        "s p c -> (s p) c")


def cols_of(table, i):
    return table[:, bass.ds(i * ROWS, ROWS)]


def flat(tile):
    return tile.rearrange("p t c -> p (t c)")


def spread(cols, n):
    return cols.unsqueeze(2).broadcast_to([cols.shape[0], cols.shape[1], n])


class Phase:

    def __init__(self, nc, name):
        self.nc, self.name, self.ctx, self.sems = nc, name, ExitStack(), []

    def sb(self, name, shape, dt=F32):
        return self.ctx.enter_context(self.nc.sbuf_tensor(f"{self.name}_{name}", shape, dt))

    def two(self, name, shape, dt=F32):
        return [self.sb(f"{name}{u}", shape, dt) for u in range(2)]

    def ps(self, name, shape=(P, TILES, P)):
        return self.ctx.enter_context(self.nc.psum_tensor(f"{self.name}_{name}", list(shape), F32))

    def sem(self, name):
        self.sems.append(self.nc.alloc_semaphore(f"{self.name}_{name}"))
        return self.sems[-1]

    def sem2(self, name):
        return [self.sem(f"{name}{u}") for u in range(2)]

    def __enter__(self):
        return self

    def __exit__(self, *a):
        self.ctx.__exit__(*a)
        if a[0] is None:
            self.nc.clear_and_free_semaphores(self.sems)
            self.nc.all_engine_barrier()


class Norm:

    def __init__(self, ph, name):
        self.stats = ph.two(name + "_stats", [P, TILES, 6])
        self.moments = ph.two(name + "_moments", [P, TILES, 2])
        self.std = ph.two(name + "_std", [P, TILES])
        self.rstd = ph.two(name + "_rstd", [P, TILES])
        self.shift = ph.two(name + "_shift", [P, TILES])
        self.turn = ph.sem(name + "_turn")
        self.stats_done = ph.sem(name + "_stats_done")
        self.moments_done = ph.sem(name + "_moments_done")
        self.std_done = ph.sem(name + "_std_done")
        self.rstd_done = ph.sem(name + "_rstd_done")
        self.shift_done = ph.sem(name + "_shift_done")

    def moments_of(self, dve, x, i, u):
        for t in range(TILES):
            last = dve.bn_stats(self.stats[u][:, t, :], x[:, t, :])
        last.then_inc(self.stats_done, 1)
        after(dve, self.stats_done, i)
        after(dve, self.std_done, i - 2)
        dve.sem_inc(self.turn, 1)
        for t in range(TILES):
            last = dve.bn_aggr(self.moments[u][:, t, :], self.stats[u][:, t, :])
        last.then_inc(self.moments_done, 1)

    def std_of(self, act, eps, i, u):
        after(act, self.moments_done, i)
        after(act, self.rstd_done, i - 2)
        act.activation(self.std[u][:, :], self.moments[u][:, :, 1], ACT.Sqrt, bias=eps).then_inc(self.std_done, 1)

    def scale_of(self, dve, i, u, used):
        after(dve, self.std_done, i)
        after(dve, used, i - 2)
        dve.reciprocal(self.rstd[u][:, :], self.std[u][:, :]).then_inc(self.rstd_done, 1)
        after(dve, self.rstd_done, i)
        dve.scalar_tensor_tensor(self.shift[u][:, :], self.moments[u][:, :, 0], -1.0, self.rstd[u][:, :],
                                 ALU.mult, ALU.mult).then_inc(self.shift_done, 1)

    def apply(self, act, out, x, func, i, u):
        after(act, self.shift_done, i)
        for t in range(TILES):
            last = act.activation(out[:, t, :], x[:, t, :], func, bias=self.shift[u][:, t:t + 1],
                                  scale=self.rstd[u][:, t:t + 1])
        return last


class Kept:

    def __init__(self, nc, ctx, size):
        def tile(name, shape, dt=F32):
            return ctx.enter_context(nc.sbuf_tensor(name, shape, dt))

        self.ident = tile("ident", [D, D])
        self.w1_node = tile("w1_node", [D, D])
        self.w1_edge = tile("w1_edge", [D, D])
        self.w2_plus_one = tile("w2_plus_one", [D, D])
        self.wk = tile("wk", [D, D])
        self.wv = tile("wv", [D, D])
        self.wo = tile("wo", [D, D])
        self.w_node = tile("w_node", [D, D])
        self.w_center_cat = tile("w_center_cat", [D, D])
        self.w_cat_sum = tile("w_cat_sum", [D, D])
        self.ff1 = tile("ff1", [D, 2, D])
        self.ff2 = tile("ff2", [D, 2, D])
        self.rel_w = tile("rel_w", [D, RELS, D])
        self.w_edge = tile("w_edge", [EDGE_DIM, D])
        self.b1 = tile("b1", [D, 1])
        self.bk = tile("bk", [D, 1])
        self.bv = tile("bv", [D, 1])
        self.bo = tile("bo", [D, 1])
        self.ff_b2 = tile("ff_b2", [D, 1])
        self.eps = tile("eps", [D, 1])
        self.tiny = tile("tiny", [D, 1])
        self.bn1_scale = tile("bn1_scale", [D, 1])
        self.bn1_shift = tile("bn1_shift", [D, 1])
        self.bn2_scale = tile("bn2_scale", [D, 1])
        self.bn2_shift = tile("bn2_shift", [D, 1])
        self.ff_b1 = tile("ff_b1", [D, 2])
        self.bn = tile("bn", [D, 4])
        self.ones_row = tile("ones_row", [1, P], BF16)
        self.head_rows = tile("head_rows", [HEADS, D])
        self.head_cols = tile("head_cols", [D, HEADS])
        self.b2_rep = tile("b2_rep", [P, TILES, D])
        self.rel_b_rep = tile("rel_b_rep", [P, TILES, D])
        self.ln_w_rep = tile("ln_w_rep", [P, TILES, D])
        self.ln_b_rep = tile("ln_b_rep", [P, TILES, D])
        self.place = tile("place", [P, TILES])
        self.dump_row = tile("dump_row", [P, TILES])
        self.place_row = tile("place_row", [P, ROWS])
        self.bn_stats1 = tile("bn_stats1", [D, size.steps, 6])
        self.bn_stats2 = tile("bn_stats2", [D, size.steps, 6])


def build(nc, size, a, out, scratch):
    with ExitStack() as ctx:
        k = Kept(nc, ctx, size)

        prepare(nc, size, a, scratch, k)
        mean_edges(nc, size, a, scratch, k)
        mean_nodes(nc, size, a, scratch, k)
        attention_edges(nc, size, a, scratch, k)
        attention_nodes(nc, size, scratch, k)
        finish_batchnorm(nc, size, k.bn_stats1, k.bn[:, 0:2], k.bn1_scale, k.bn1_shift, k, "bn1")
        feed_forward(nc, size, scratch, k)
        finish_batchnorm(nc, size, k.bn_stats2, k.bn[:, 2:4], k.bn2_scale, k.bn2_shift, k, "bn2")
        second_norm_nodes(nc, size, scratch, k)
        gated_edges(nc, size, a, scratch, k)
        gated_nodes(nc, size, scratch, k)
        relation_edges(nc, size, a, scratch, k)
        relation_nodes(nc, size, scratch, out, k)


def prepare(nc, size, a, scratch, k):
    S = size.steps
    with Phase(nc, "prep") as ph:
        weights_in = ph.sem("weights_in")
        lists_in = ph.sem("lists_in")
        stored = ph.sem("stored")
        consts = ph.sem("consts")
        chain = ph.sem("chain")
        rel_sums_ready = ph.sem("rel_sums_ready")
        flipped = ph.sem("flipped")
        tables_done = ph.sem("tables_done")
        zero_ready = ph.sem("zero_ready")

        w2 = ph.sb("w2", [D, D])
        w_center_t = ph.sb("w_center_t", [D, D])
        w_cat_node = ph.sb("w_cat_node", [D, D])
        raw = ph.sb("raw", [S, 4, ROWS], I32)
        row_lists = ph.sb("row_lists", [P, 2, S * TILES], I32)
        head_iota = ph.sb("head_iota", [HEADS, D], I32)
        head_iota_c = ph.sb("head_iota_c", [D, HEADS], I32)
        place_i = ph.sb("place_i", [P, TILES], I32)
        place_row_i = ph.sb("place_row_i", [P, ROWS], I32)
        edge_i = ph.sb("edge_i", [S, ROWS], I32)
        zero = ph.sb("zero", [P, ROWS])
        edge_at = ph.sb("edge_at", [S, ROWS])
        first = ph.sb("first", [S, ROWS])
        last = ph.sb("last", [S, ROWS])
        col_tab = ph.sb("col_tab", [S, 2, ROWS], BF16)
        drop = ph.sb("drop", [S, ROWS])
        inv_deg = ph.sb("inv_deg", [S, ROWS])
        inv_rel = ph.sb("inv_rel", [S, ROWS])
        one_rel = ph.sb("one_rel", [S, ROWS])
        none = ph.sb("none", [S, ROWS])
        work = ph.sb("work", [S, ROWS])
        work2 = ph.sb("work2", [S, ROWS])
        counts = ph.sb("counts", [S, RELS, ROWS])
        starts = ph.sb("starts", [S, RELS, ROWS])
        ends = ph.sb("ends", [S, RELS, ROWS])
        totals = ph.sb("totals", [S, 3, 32])
        totals_t = ph.sb("totals_t", [32, S])
        carried = ph.sb("carried", [32, 3, S + 1])
        carry = ph.sb("carry", [S, 3, 32])
        row_tab = ph.sb("row_tab", [P, S, 12], I32)
        ps_a = ph.ps("a")
        ps_b = ph.ps("b")
        block = ph.ctx.enter_context(nc.Block())

        @block.sync
        def _(sp):
            for tile, src in (
                (k.w1_node, a["L0_W1"][0:D, :]), (k.w1_edge, a["L0_W1"][D:2 * D, :]), (w2, a["L0_W2"]),
                (k.wk, a["L1_WkT"]), (k.wv, a["L1_WvT"]), (k.wo, a["L1_WoT"]), (k.w_node, a["L2_W_node"]),
                (w_center_t, a["L2_W_centerT"]), (w_cat_node, a["L2_W_cat"][0:D, :]),
                (k.w_cat_sum, a["L2_W_cat"][D:2 * D, :]), (k.w_edge, a["L2_W_edge"]),
                (k.b1, a["L0_b1"]), (k.bk, a["L1_bk"]), (k.bv, a["L1_bv"]), (k.bo, a["L1_bo"]),
                (k.ff_b1, a["L1_b1"]), (k.ff_b2, a["L1_b2"]), (k.bn, a["L1_bn"]),
            ):
                sp.dma_start(tile[:, :], src[:, :]).then_inc(weights_in, 16)
            sp.dma_start(k.ff1[:, :, :], a["L1_W1T"].rearrange("d (h n) -> d h n", h=2)).then_inc(weights_in, 16)
            sp.dma_start(k.ff2[:, :, :], a["L1_W2T"].rearrange("(h d) n -> d h n", h=2)).then_inc(weights_in, 16)
            sp.dma_start(k.rel_w[:, :, :], a["L3_W"].rearrange("r d n -> d r n")).then_inc(weights_in, 16)
            for tile, src in ((k.b2_rep, a["L0_b2"]), (k.ln_w_rep, a["L2_ln_w"]), (k.ln_b_rep, a["L2_ln_b"]),
                              (k.rel_b_rep, a["L3_b"])):
                for t in range(TILES):
                    sp.dma_start(tile[:, t, :], src[0, :].partition_broadcast(P)).then_inc(weights_in, 16)
            for n in range(4):
                sp.dma_start(raw[:, n, :], a["edge_lin"][n, :, :]).then_inc(lists_in, 16)
            sp.dma_start(row_lists[:, :, :], a["edge_rows"][:, :, :]).then_inc(lists_in, 16)
            sp.wait_ge(zero_ready, 1)
            sp.dma_start(scratch["agg"].rearrange("(p r) d -> p (r d)", p=P).rearrange("p (s c) -> p s c", c=ROWS),
                         zero[:, :].unsqueeze(1).broadcast_to([P, S, ROWS])).then_inc(stored, 16)
            sp.dma_start(scratch["sum"][size.rows:size.rows + ROWS, :].rearrange("(p r) d -> p (r d)", p=P),
                         zero[:, :]).then_inc(stored, 16)
            sp.wait_ge(tables_done, 1)
            sp.dma_start(scratch["col_tab"], col_tab[:, :, :]).then_inc(stored, 16)
            sp.dma_start(scratch["drop"], drop[:, :]).then_inc(stored, 16)
            sp.dma_start(scratch["row_tab"], row_tab[:, :, :]).then_inc(stored, 16)
            sp.wait_ge(stored, 5 * 16)
            sp.wait_ge(weights_in, 16 * (21 + 4 * TILES))

        @block.gpsimd
        def _(pool):
            pool.memset(zero[:, :], 0.0).then_inc(zero_ready, 1)
            pool.memset(k.ident[:, :], 0.0).then_inc(consts, 1)
            pool.wait_ge(consts, 1)
            pool.affine_select(out=k.ident[:, :], in_=k.ident[:, :], compare_op=ALU.not_equal, fill=1.0, base=0,
                               pattern=[[-1, P]], channel_multiplier=1).then_inc(consts, 1)
            pool.memset(k.ones_row[:, :], 1.0).then_inc(consts, 1)
            pool.memset(k.eps[:, :], EPS).then_inc(consts, 1)
            pool.memset(k.tiny[:, :], 1e-16).then_inc(consts, 1)
            pool.iota(head_iota[:, :], [[1, D]], base=0, channel_multiplier=-HEAD_DIM).then_inc(consts, 1)
            pool.iota(head_iota_c[:, :], [[-HEAD_DIM, HEADS]], base=0, channel_multiplier=1).then_inc(consts, 1)
            pool.iota(place_i[:, :], [[P, TILES]], base=1, channel_multiplier=1).then_inc(consts, 1)
            pool.iota(place_row_i[:, :], [[1, ROWS]], base=1, channel_multiplier=0).then_inc(consts, 1)
            pool.iota(edge_i[:, :], [[1, ROWS]], base=0, channel_multiplier=ROWS).then_inc(consts, 1)

        @block.tensor
        def _(pe):
            pe.wait_ge(weights_in, 16 * (21 + 4 * TILES))
            pe.wait_ge(consts, 10)
            pe.matmul(ps_a[:, 0, :], w_center_t[:, :], w_cat_node[:, :], start=True, stop=True).then_inc(flipped, 1)
            for n in range(2):
                pe.wait_ge(rel_sums_ready, 2 * n + 1)
                pe.transpose(ps_a[0:32, 1, 0:S], totals[:, n, :], k.ident[0:S, 0:S]).then_inc(flipped, 1)
                if n == 1:
                    pe.transpose(ps_a[0:32, 2, 0:S], totals[:, 2, :], k.ident[0:S, 0:S]).then_inc(flipped, 1)
                pe.wait_ge(rel_sums_ready, 2 * n + 2)
                if n == 0:
                    pe.transpose(ps_b[0:S, 0, 0:32], carried[:, 0, 0:S], k.ident[0:32, 0:32]).then_inc(flipped, 1)
                else:
                    pe.transpose(ps_b[0:S, 1, 0:32], carried[:, 1, 0:S], k.ident[0:32, 0:32]).then_inc(flipped, 1)
                    pe.transpose(ps_b[0:S, 2, 0:32], carried[:, 2, 1:S + 1], k.ident[0:32, 0:32]).then_inc(flipped, 1)
            pe.wait_ge(rel_sums_ready, 5)
            for t in range(TILES):
                pe.transpose(ps_a[:, t, 0:S], inv_deg[:, t * P:(t + 1) * P], k.ident[0:S, 0:S])
                last_one = pe.transpose(ps_b[:, t, 0:S], inv_rel[:, t * P:(t + 1) * P], k.ident[0:S, 0:S])
            last_one.then_inc(flipped, 1)

        @block.vector
        def _(dve):
            count = [0]

            def done(ins):
                count[0] += 1
                ins.then_inc(chain, 1)
                dve.wait_ge(chain, count[0])

            dve.wait_ge(consts, 10)
            dve.wait_ge(weights_in, 16 * (21 + 4 * TILES))
            dve.tensor_tensor(k.w2_plus_one[:, :], w2[:, :], k.ident[:, :], ALU.add)
            dve.tensor_copy(k.place[:, :], place_i[:, :])
            dve.tensor_scalar(k.dump_row[:, :], place_i[:, :], float(size.rows - 1), None, ALU.add)
            dve.tensor_copy(k.place_row[:, :], place_row_i[:, :])
            dve.tensor_copy(edge_at[:, :], edge_i[:, :])
            dve.memset(totals[:, :, :], 0.0)
            dve.memset(none[:, :], 0.0)
            dve.memset(carried[:, :, :], 0.0)
            dve.tensor_scalar(k.head_rows[:, :], head_iota[:, :], 0.0, None, ALU.is_ge)
            done(dve.tensor_scalar(k.head_cols[:, :], head_iota_c[:, :], 0.0, HEAD_DIM ** -0.5, ALU.is_ge, ALU.mult))
            dve.scalar_tensor_tensor(k.head_rows[:, :], head_iota[:, :], float(HEAD_DIM), k.head_rows[:, :],
                                     ALU.is_lt, ALU.mult)
            dve.scalar_tensor_tensor(k.head_cols[:, :], head_iota_c[:, :], float(HEAD_DIM), k.head_cols[:, :],
                                     ALU.is_lt, ALU.mult)
            dve.wait_ge(flipped, 1)
            dve.tensor_copy(k.w_center_cat[:, :], ps_a[:, 0, :])

            dve.wait_ge(lists_in, 5 * 16)
            dve.tensor_tensor(first[:, :], raw[:, 0, :], raw[:, 1, :], ALU.not_equal)
            dve.tensor_tensor(last[:, :], raw[:, 0, :], raw[:, 2, :], ALU.not_equal)
            done(dve.tensor_copy(col_tab[:, 1, :], raw[:, 3, :]))
            dve.tensor_scalar(col_tab[:, 0, :], first[:, :], -1.0, 1.0, ALU.mult, ALU.add)
            dve.tensor_scalar(drop[:, :], first[:, :], -LOW, None, ALU.mult)
            scat = row_tab[:, :, 0:TILES]
            there = row_lists[:, 0, :].rearrange("p (s t) -> p s t", t=TILES)
            nxt = row_lists[:, 1, :].rearrange("p (s t) -> p s t", t=TILES)
            done(dve.tensor_tensor(scat, there, nxt, ALU.is_equal))
            done(dve.scalar_tensor_tensor(scat, scat, FAR, there, ALU.mult, ALU.add))
            done(dve.tensor_tensor(work[:, :], first[:, :], edge_at[:, :], ALU.mult))
            done(dve.tensor_tensor_scan(inv_deg[:, :], work[:, :], work[:, :], 0.0, ALU.max, ALU.max))
            done(dve.tensor_copy(totals[:, 0, RELS:RELS + 1], inv_deg[:, ROWS - 1:ROWS]))
            for r in range(RELS):
                done(dve.tensor_scalar(work[:, :], raw[:, 3, :], float(r), None, ALU.is_equal))
                done(dve.tensor_tensor_scan(counts[:, r, :], work[:, :], none[:, :], 0.0, ALU.add, ALU.add))
                done(dve.tensor_copy(totals[:, 0, r:r + 1], counts[:, r, ROWS - 1:ROWS]))
            dve.sem_inc(rel_sums_ready, 1)
            dve.wait_ge(flipped, 2)
            done(dve.tensor_copy(totals_t[:, 0:S], ps_a[0:32, 1, 0:S]))
            done(dve.tensor_tensor_scan(carried[:, 0, 1:S], totals_t[:, 0:S - 1], carried[:, 2, 0:S - 1], 0.0,
                                        ALU.add, ALU.add))
            dve.sem_inc(rel_sums_ready, 1)
            dve.wait_ge(flipped, 3)
            done(dve.tensor_copy(carry[:, 0, :], ps_b[0:S, 0, 0:32]))
            for r in range(RELS):
                done(dve.tensor_scalar(counts[:, r, :], counts[:, r, :], carry[:, 0, r:r + 1], None, ALU.add))
                done(dve.tensor_scalar(one_rel[:, :], raw[:, 3, :], float(r), None, ALU.is_equal))
                done(dve.tensor_tensor(work[:, :], counts[:, r, :], one_rel[:, :], ALU.subtract))
                done(dve.tensor_tensor(work[:, :], work[:, :], first[:, :], ALU.mult))
                done(dve.tensor_tensor_scan(starts[:, r, :], work[:, :], work[:, :], 0.0, ALU.max, ALU.max))
                done(dve.tensor_copy(totals[:, 1, r:r + 1], starts[:, r, ROWS - 1:ROWS]))
                done(dve.scalar_tensor_tensor(work[:, :], counts[:, r, :], -FAR, last[:, :], ALU.add, ALU.mult))
                done(dve.tensor_tensor_scan(ends[:, r, ::-1], work[:, ::-1], work[:, ::-1], 0.0, ALU.min, ALU.min))
                done(dve.tensor_copy(totals[:, 2, r:r + 1], ends[:, r, 0:1]))
            done(dve.tensor_copy(totals[:, 1, RELS:RELS + 1], totals[:, 0, RELS:RELS + 1]))
            dve.sem_inc(rel_sums_ready, 1)
            dve.wait_ge(flipped, 5)
            done(dve.tensor_copy(totals_t[:, 0:S], ps_a[0:32, 1, 0:S]))
            done(dve.tensor_tensor_scan(carried[:, 1, 1:S], totals_t[:, 0:S - 1], totals_t[:, 0:S - 1], 0.0,
                                        ALU.max, ALU.max))
            done(dve.tensor_copy(totals_t[:, 0:S], ps_a[0:32, 2, 0:S]))
            done(dve.tensor_tensor_scan(carried[:, 2, 1:S][:, ::-1], totals_t[:, 1:S][:, ::-1],
                                        totals_t[:, 1:S][:, ::-1], 0.0, ALU.min, ALU.min))
            dve.sem_inc(rel_sums_ready, 1)
            dve.wait_ge(flipped, 7)
            done(dve.tensor_copy(carry[:, 1:3, :], ps_b[0:S, 1:3, 0:32]))
            done(dve.memset(inv_rel[:, :], 0.0))
            for r in range(RELS):
                done(dve.tensor_scalar(work[:, :], starts[:, r, :], carry[:, 1, r:r + 1], None, ALU.max))
                done(dve.scalar_tensor_tensor(work2[:, :], ends[:, r, :], carry[:, 2, r:r + 1], work[:, :],
                                              ALU.min, ALU.subtract))
                done(dve.tensor_scalar(work2[:, :], work2[:, :], FAR, None, ALU.add))
                done(dve.tensor_scalar(one_rel[:, :], raw[:, 3, :], float(r), None, ALU.is_equal))
                done(dve.tensor_tensor(work2[:, :], work2[:, :], one_rel[:, :], ALU.mult))
                done(dve.tensor_tensor(inv_rel[:, :], inv_rel[:, :], work2[:, :], ALU.add))
            done(dve.reciprocal(inv_rel[:, :], inv_rel[:, :]))
            done(dve.tensor_scalar(inv_deg[:, :], inv_deg[:, :], carry[:, 1, RELS:RELS + 1], None, ALU.max))
            done(dve.scalar_tensor_tensor(inv_deg[:, :], edge_at[:, :], 1.0, inv_deg[:, :], ALU.add, ALU.subtract))
            done(dve.reciprocal(inv_deg[:, :], inv_deg[:, :]))
            dve.sem_inc(rel_sums_ready, 1)
            dve.wait_ge(flipped, 8)
            for t in range(TILES):
                dve.tensor_copy(row_tab[:, :, 4 + t].bitcast(F32), ps_a[:, t, 0:S])
                end = dve.tensor_copy(row_tab[:, :, 8 + t].bitcast(F32), ps_b[:, t, 0:S])
            done(end)
            dve.sem_inc(tables_done, 1)


def gather(pool, tile, table, idx, col, sem):
    for t in range(TILES):
        pool.indirect_dma_start(out=tile[:, t, :], out_offset=None, in_=table,
                                in_offset=bass.IndirectOffsetOnAxis(ap=idx[:, col + t:col + t + 1], axis=0)
                                ).then_inc(sem, 16)


def scatter(pool, table, tile, idx, bound, sem):
    for t in range(TILES):
        pool.indirect_dma_start(out=table, out_offset=bass.IndirectOffsetOnAxis(ap=idx[:, t:t + 1], axis=0),
                                in_=tile[:, t, :], in_offset=None, bounds_check=bound,
                                oob_is_err=False).then_inc(sem, 16)


def mean_edges(nc, size, a, scratch, k):
    S = size.steps
    with Phase(nc, "e0") as ph:
        idx, idx_in = ph.two("idx", [P, 8], I32), ph.sem2("idx_in")
        edge, edge_in = ph.two("edge", [D, ROWS]), ph.sem2("edge_in")
        col, col_in = ph.two("col", [1, 2, ROWS], BF16), ph.sem2("col_in")
        row, row_in = ph.two("row", [P, 12], I32), ph.sem2("row_in")
        x, x_in = ph.two("x", [P, TILES, D]), ph.sem2("x_in")
        h, h_ready = ph.two("h", [P, TILES, D]), ph.sem("h_ready")
        ht, ht_ready = ph.two("ht", [D, TILES, P]), ph.sem("ht_ready")
        msg, msg_ready = ph.two("msg", [D, ROWS]), ph.sem("msg_ready")
        run, run_ready = ph.two("run", [D, ROWS]), ph.sem("run_ready")
        res, res_ready = ph.two("res", [P, TILES, D]), ph.sem("res_ready")
        scattered = ph.sem2("scattered")
        pool_turn = ph.sem("pool_turn")
        turned = ph.sem("turned")
        msg_done = ph.sem("msg_done")
        keep_done = ph.sem("keep_done")
        out_done = ph.sem("out_done")
        norm = Norm(ph, "norm")
        ps_t = [ph.ps(f"t{u}") for u in range(2)]
        ps_m = [ph.ps(f"m{u}") for u in range(2)]
        ps_k = [ph.ps(f"k{u}") for u in range(2)]
        ps_r = [ph.ps(f"r{u}") for u in range(2)]
        block = ph.ctx.enter_context(nc.Block())

        @block.sync
        def _(sp):
            def body(i, u):
                if live(i, S):
                    landed(sp, x_in, i - 2, u, TILES)
                    sp.dma_start(idx[u][:, :], a["idx"][:, bass.ds(i * 8, 8)]).then_inc(idx_in[u], 16)
                    after(sp, msg_done, i - 2)
                    sp.dma_start(edge[u][:, :], cols_of(a["edge128T"], i)).then_inc(edge_in[u], 16)
                    after(sp, keep_done, i - 2)
                    sp.dma_start(flat(col[u][:, :, :]), scratch["col_tab"].rearrange("s a c -> s (a c)")[bass.ds(i, 1), :]
                                 ).then_inc(col_in[u], 16)
                j, v = i - 1, 1 - u
                if live(j, S):
                    landed(sp, scattered, j - 2, v, TILES)
                    sp.dma_start(row[v][:, :], scratch["row_tab"].rearrange("p s c -> p (s c)")[:, bass.ds(j * 12, 12)]
                                 ).then_inc(row_in[v], 16)
            run_steps(sp, body, S, 1)

        @block.gpsimd
        def _(pool):
            def body(i, u):
                if live(i, S):
                    landed(pool, idx_in, i, u, 1)
                    after(pool, h_ready, i - 2)
                    pool.sem_inc(pool_turn, 1)
                    gather(pool, x[u], a["x"], idx[u], 0, x_in[u])
                j = i - 2
                if live(j, S):
                    after(pool, res_ready, j)
                    pool.sem_inc(pool_turn, 1)
                    scatter(pool, scratch["agg"], res[u], row[u], size.rows - 1, scattered[u])
            run_steps(pool, body, S, 2)
            for u in range(2):
                pool.wait_ge(scattered[u], 16 * TILES * (S // 2))

        @block.vector
        def _(dve):
            def body(i, u):
                j, v = i - 1, 1 - u
                if live(i, S):
                    landed(dve, x_in, i, u, TILES)
                    norm.moments_of(dve, x[u], i, u)
                if live(j, S):
                    after(dve, msg_ready, j)
                    after(dve, keep_done, j)
                    after(dve, out_done, j - 2)
                    after(dve, run_ready, j - 1)
                    before = 0.0 if isinstance(j, int) and j == 0 else run[1 - v][:, ROWS - 1:ROWS]
                    dve.tensor_tensor_scan(run[v][:, :], flat(ps_k[v][:, :, :]), msg[v][:, :], before, ALU.mult,
                                           ALU.add).then_inc(run_ready, 1)
                if live(i, S):
                    norm.scale_of(dve, i, u, h_ready)
                if live(j, S):
                    after(dve, out_done, j)
                    landed(dve, row_in, j, v, 1)
                    landed(dve, scattered, j - 2, v, TILES)
                    dve.tensor_tensor(res[v][:, :, :], ps_r[v][:, :, :], spread(row[v][:, 4:8].bitcast(F32), D),
                                      ALU.mult).then_inc(res_ready, 1)
            run_steps(dve, body, S, 1)

        @block.scalar
        def _(act):
            def body(i, u):
                j, v = i - 1, 1 - u
                if live(j, S):
                    after(act, msg_done, j)
                    after(act, run_ready, j - 2)
                    act.activation(msg[v][:, :], flat(ps_m[v][:, :, :]), ACT.Identity, bias=k.b1[:, :]
                                   ).then_inc(msg_ready, 1)
                if live(i, S):
                    norm.std_of(act, k.eps[:, :], i, u)
                    after(act, turned, i - 2)
                    norm.apply(act, h[u], x[u], ACT.Relu, i, u).then_inc(h_ready, 1)
                    after(act, turned, i)
                    after(act, msg_done, i - 2)
                    act.activation(ht[u][:, :, :], ps_t[u][:, :, :], ACT.Copy).then_inc(ht_ready, 1)
            run_steps(act, body, S, 1)

        @block.tensor
        def _(pe):
            def body(i, u):
                j, v = i - 1, 1 - u
                if live(j, S):
                    after(pe, ht_ready, j)
                    landed(pe, edge_in, j, v, 1)
                    after(pe, msg_ready, j - 2)
                    pe.matmul(flat(ps_m[v][:, :, :]), k.w1_edge[:, :], edge[v][:, :], start=True, stop=False)
                    pe.matmul(flat(ps_m[v][:, :, :]), k.w1_node[:, :], flat(ht[v][:, :, :]), start=False, stop=True
                              ).then_inc(msg_done, 1)
                    landed(pe, col_in, j, v, 1)
                    after(pe, run_ready, j - 2)
                    pe.matmul(flat(ps_k[v][:, :, :]), k.ones_row[:, :], col[v][:, 0, :], start=True, stop=True
                              ).then_inc(keep_done, 1)
                if live(i, S):
                    after(pe, h_ready, i)
                    after(pe, ht_ready, i - 2)
                    for t in range(TILES):
                        ins = pe.transpose(ps_t[u][:, t, :], h[u][:, t, :], k.ident[:, :])
                    ins.then_inc(turned, 1)
                if live(j, S):
                    after(pe, run_ready, j)
                    after(pe, res_ready, j - 2)
                    for t in range(TILES):
                        ins = pe.matmul(ps_r[v][:, t, :], run[v][:, t * P:(t + 1) * P], k.w2_plus_one[:, :],
                                        start=True, stop=True)
                    ins.then_inc(out_done, 1)
            run_steps(pe, body, S, 1)


def mean_nodes(nc, size, a, scratch, k):
    S = size.steps
    with Phase(nc, "n0") as ph:
        x, x_in = ph.two("x", [P, TILES, D]), ph.sem2("x_in")
        agg, agg_in = ph.two("agg", [P, TILES, D]), ph.sem2("agg_in")
        biased, biased_ready = ph.two("biased", [P, TILES, D]), ph.sem("biased_ready")
        leaky, leaky_ready = ph.two("leaky", [P, TILES, D]), ph.sem("leaky_ready")
        x1, x1_ready, x1_out = ph.two("x1", [P, TILES, D]), ph.sem("x1_ready"), ph.sem2("x1_out")
        h1, h1_ready, h1_out = ph.two("h1", [P, TILES, D]), ph.sem("h1_ready"), ph.sem2("h1_out")
        norm = Norm(ph, "norm")
        block = ph.ctx.enter_context(nc.Block())

        @block.sync
        def _(sp):
            def body(i, u):
                if live(i, S):
                    after(sp, biased_ready, i - 2)
                    sp.dma_start(flat(agg[u][:, :, :]), rows_of(scratch["agg"], i)).then_inc(agg_in[u], 16)
                    after(sp, x1_ready, i - 2)
                    sp.dma_start(flat(x[u][:, :, :]), rows_of(a["x"], i)).then_inc(x_in[u], 16)
                j, v = i - 1, 1 - u
                if live(j, S):
                    after(sp, x1_ready, j)
                    sp.dma_start(rows_of(scratch["x1"], j), flat(x1[v][:, :, :])).then_inc(x1_out[v], 16)
                if live(i - 2, S):
                    after(sp, h1_ready, i - 2)
                    sp.dma_start(rows_of(scratch["h1"], i - 2), flat(h1[u][:, :, :])).then_inc(h1_out[u], 16)
            run_steps(sp, body, S, 2)
            for s in (*x1_out, *h1_out):
                sp.wait_ge(s, 16 * (S // 2))

        @block.vector
        def _(dve):
            def body(i, u):
                if live(i, S):
                    landed(dve, agg_in, i, u, 1)
                    after(dve, leaky_ready, i - 2)
                    dve.tensor_tensor(biased[u][:, :, :], agg[u][:, :, :], k.b2_rep[:, :, :], ALU.add
                                      ).then_inc(biased_ready, 1)
                    after(dve, biased_ready, i)
                    after(dve, x1_ready, i - 2)
                    dve.scalar_tensor_tensor(leaky[u][:, :, :], biased[u][:, :, :], SLOPE, biased[u][:, :, :],
                                             ALU.mult, ALU.max).then_inc(leaky_ready, 1)
                    after(dve, leaky_ready, i)
                    landed(dve, x_in, i, u, 1)
                    landed(dve, x1_out, i - 2, u, 1)
                    after(dve, h1_ready, i - 2)
                    dve.tensor_tensor(x1[u][:, :, :], leaky[u][:, :, :], x[u][:, :, :], ALU.add).then_inc(x1_ready, 1)
                    after(dve, x1_ready, i)
                    norm.moments_of(dve, x1[u], i, u)
                if live(i - 1, S):
                    norm.scale_of(dve, i - 1, 1 - u, h1_ready)
            run_steps(dve, body, S, 1)

        @block.scalar
        def _(act):
            def body(i, u):
                if live(i, S):
                    norm.std_of(act, k.eps[:, :], i, u)
                j, v = i - 1, 1 - u
                if live(j, S):
                    landed(act, h1_out, j - 2, v, 1)
                    norm.apply(act, h1[v], x1[v], ACT.Relu, j, v).then_inc(h1_ready, 1)
            run_steps(act, body, S, 1)


def attention_edges(nc, size, a, scratch, k):
    S = size.steps
    with Phase(nc, "e1") as ph:
        idx, idx_in = ph.two("idx", [P, 8], I32), ph.sem2("idx_in")
        drop, drop_in = ph.two("drop", [HEADS, ROWS]), ph.sem2("drop_in")
        row, row_in = ph.two("row", [P, 12], I32), ph.sem2("row_in")
        hs, hs_in = ph.two("hs", [P, TILES, D]), ph.sem2("hs_in")
        hd, hd_in = ph.two("hd", [P, TILES, D]), ph.sem2("hd_in")
        hst, hst_ready = ph.two("hst", [D, ROWS]), ph.sem("hst_ready")
        hdt, hdt_ready = ph.two("hdt", [D, ROWS]), ph.sem("hdt_ready")
        kq, kq_ready = ph.two("kq", [D, ROWS]), ph.sem("kq_ready")
        top, top_ready = ph.two("top", [HEADS, ROWS + 1]), ph.sem("top_ready")
        fall, fall_ready = ph.two("fall", [HEADS, ROWS]), ph.sem("fall_ready")
        arg, arg_ready = ph.two("arg", [HEADS, 2, ROWS]), ph.sem("arg_ready")
        ex, ex_ready = ph.two("ex", [HEADS, 2, ROWS]), ph.sem("ex_ready")
        den, den_ready = ph.two("den", [HEADS, ROWS]), ph.sem("den_ready")
        safe_den, safe_ready = ph.two("safe_den", [HEADS, ROWS]), ph.sem("safe_ready")
        inv_den, inv_ready = ph.two("inv_den", [HEADS, ROWS]), ph.sem("inv_ready")
        v, v_ready = ph.two("v", [D, ROWS]), ph.sem("v_ready")
        pv, pv_ready = ph.two("pv", [D, ROWS]), ph.sem("pv_ready")
        run, run_ready = ph.two("run", [D, ROWS]), ph.sem("run_ready")
        att, att_ready = ph.two("att", [D, ROWS]), ph.sem("att_ready")
        res, res_ready = ph.two("res", [P, TILES, D]), ph.sem("res_ready")
        scattered = ph.sem2("scattered")
        pool_turn = ph.sem("pool_turn")
        hs_turned = ph.sem("hs_turned")
        hd_turned = ph.sem("hd_turned")
        k_done = ph.sem("k_done")
        score_done = ph.sem("score_done")
        v_done = ph.sem("v_done")
        spread_done = ph.sem("spread_done")
        inv_spread = ph.sem("inv_spread")
        out_done = ph.sem("out_done")
        carry_set = ph.sem("carry_set")
        ps_hs, ps_hd, ps_k, ps_vr = ph.ps("hs"), ph.ps("hd"), ph.ps("k"), ph.ps("vr")
        ps_s = ph.ps("s", (HEADS, ROWS))
        ps_p, ps_d, ps_i = ph.ps("p"), ph.ps("d"), ph.ps("i")
        block = ph.ctx.enter_context(nc.Block())

        @block.sync
        def _(sp):
            def body(i, u):
                if live(i, S):
                    landed(sp, hs_in, i - 2, u, TILES)
                    landed(sp, hd_in, i - 2, u, TILES)
                    sp.dma_start(idx[u][:, :], a["idx"][:, bass.ds(i * 8, 8)]).then_inc(idx_in[u], 16)
                    after(sp, arg_ready, i - 2)
                    sp.dma_start(drop[u][:, :], scratch["drop"][bass.ds(i, 1), :].rearrange(
                        "a c -> (a c)").partition_broadcast(HEADS)).then_inc(drop_in[u], 16)
                j, w = i - 1, 1 - u
                if live(j, S):
                    landed(sp, scattered, j - 2, w, TILES)
                    sp.dma_start(row[w][:, :], scratch["row_tab"].rearrange("p s c -> p (s c)")[:, bass.ds(j * 12, 12)]
                                 ).then_inc(row_in[w], 16)
            run_steps(sp, body, S, 1)

        @block.gpsimd
        def _(pool):
            def body(i, u):
                if live(i, S):
                    landed(pool, idx_in, i, u, 1)
                    after(pool, hs_turned, i - 2)
                    pool.sem_inc(pool_turn, 1)
                    gather(pool, hs[u], scratch["h1"], idx[u], 0, hs_in[u])
                    after(pool, hd_turned, i - 2)
                    pool.sem_inc(pool_turn, 1)
                    gather(pool, hd[u], scratch["h1"], idx[u], TILES, hd_in[u])
                j = i - 2
                if live(j, S):
                    landed(pool, row_in, j, u, 1)
                    after(pool, res_ready, j)
                    pool.sem_inc(pool_turn, 1)
                    scatter(pool, scratch["agg"], res[u], row[u], size.rows - 1, scattered[u])
            run_steps(pool, body, S, 2)
            for u in range(2):
                pool.wait_ge(scattered[u], 16 * TILES * (S // 2))

        @block.vector
        def _(dve):
            dve.memset(top[0][:, 0:1], 0.0).then_inc(carry_set, 1)

            def body(i, u):
                j, w = i - 1, 1 - u
                if live(j, S):
                    after(dve, ex_ready, j)
                    after(dve, safe_ready, j - 2)
                    after(dve, den_ready, j - 1)
                    before = 0.0 if isinstance(j, int) and j == 0 else den[1 - w][:, ROWS - 1:ROWS]
                    dve.tensor_tensor_scan(den[w][:, :], ex[w][:, 1, :], ex[w][:, 0, :], before, ALU.mult, ALU.add
                                           ).then_inc(den_ready, 1)
                    after(dve, v_ready, j)
                    after(dve, spread_done, j)
                    after(dve, run_ready, j - 2)
                    dve.tensor_tensor(pv[w][:, :], v[w][:, :], flat(ps_p[:, :, :]), ALU.mult).then_inc(pv_ready, 1)
                    after(dve, pv_ready, j)
                    after(dve, att_ready, j - 2)
                    after(dve, run_ready, j - 1)
                    before = 0.0 if isinstance(j, int) and j == 0 else run[1 - w][:, ROWS - 1:ROWS]
                    dve.tensor_tensor_scan(run[w][:, :], flat(ps_d[:, :, :]), pv[w][:, :], before, ALU.mult, ALU.add
                                           ).then_inc(run_ready, 1)
                    after(dve, safe_ready, j)
                    after(dve, inv_spread, j - 2)
                    dve.reciprocal(inv_den[w][:, :], safe_den[w][:, :]).then_inc(inv_ready, 1)
                if live(i, S):
                    after(dve, k_done, i)
                    after(dve, hdt_ready, i)
                    after(dve, score_done, i - 2)
                    dve.scalar_tensor_tensor(kq[u][:, :], flat(ps_k[:, :, :]), k.bk[:, :], hdt[u][:, :], ALU.add,
                                             ALU.mult).then_inc(kq_ready, 1)
                if live(j, S):
                    after(dve, inv_spread, j)
                    after(dve, run_ready, j)
                    after(dve, out_done, j - 2)
                    dve.tensor_tensor(att[w][:, :], run[w][:, :], flat(ps_i[:, :, :]), ALU.mult
                                      ).then_inc(att_ready, 1)
                if live(i, S):
                    after(dve, score_done, i)
                    landed(dve, drop_in, i, u, 1)
                    after(dve, arg_ready, i - 1)
                    if isinstance(i, int) and i == 0:
                        dve.wait_ge(carry_set, 1)
                        before = 0.0
                    else:
                        before = top[1 - u][:, ROWS:ROWS + 1]
                        dve.tensor_copy(top[u][:, 0:1], before).then_inc(carry_set, 1)
                        after(dve, carry_set, i)
                    dve.tensor_tensor_scan(top[u][:, 1:ROWS + 1], drop[u][:, :], ps_s[:, :], before, ALU.add, ALU.max
                                           ).then_inc(top_ready, 1)
                    after(dve, top_ready, i)
                    after(dve, ex_ready, i - 2)
                    dve.tensor_tensor(arg[u][:, 0, :], ps_s[:, :], top[u][:, 1:ROWS + 1], ALU.subtract)
                    dve.tensor_tensor(fall[u][:, :], top[u][:, 0:ROWS], top[u][:, 1:ROWS + 1], ALU.subtract
                                      ).then_inc(fall_ready, 1)
                    after(dve, fall_ready, i)
                    dve.tensor_tensor(arg[u][:, 1, :], fall[u][:, :], drop[u][:, :], ALU.add).then_inc(arg_ready, 1)
            run_steps(dve, body, S, 1)

        @block.scalar
        def _(act):
            def body(i, u):
                j, w = i - 1, 1 - u
                if live(j, S):
                    after(act, v_done, j)
                    after(act, pv_ready, j - 2)
                    act.activation(v[w][:, :], flat(ps_vr[:, :, :]), ACT.Identity, bias=k.bv[:, :]
                                   ).then_inc(v_ready, 1)
                if live(i, S):
                    after(act, hs_turned, i)
                    after(act, v_done, i - 2)
                    act.activation(hst[u][:, :], flat(ps_hs[:, :, :]), ACT.Copy).then_inc(hst_ready, 1)
                    after(act, hd_turned, i)
                    after(act, kq_ready, i - 2)
                    act.activation(hdt[u][:, :], flat(ps_hd[:, :, :]), ACT.Copy).then_inc(hdt_ready, 1)
                if live(j, S):
                    after(act, den_ready, j)
                    after(act, inv_ready, j - 2)
                    act.activation(safe_den[w][:, :], den[w][:, :], ACT.Identity, bias=k.tiny[0:HEADS, :]
                                   ).then_inc(safe_ready, 1)
                    after(act, out_done, j)
                    landed(act, scattered, j - 2, w, TILES)
                    act.activation(res[w][:, :, :], ps_vr[:, :, :], ACT.Copy).then_inc(res_ready, 1)
                if live(i, S):
                    after(act, arg_ready, i)
                    after(act, den_ready, i - 2)
                    after(act, spread_done, i - 2)
                    act.activation(ex[u][:, :, :], arg[u][:, :, :], ACT.Exp).then_inc(ex_ready, 1)
            run_steps(act, body, S, 1)

        @block.tensor
        def _(pe):
            def body(i, u):
                j, w = i - 1, 1 - u
                if live(j, S):
                    after(pe, res_ready, j - 1)
                    pe.matmul(flat(ps_vr[:, :, :]), k.wv[:, :], hst[w][:, :], start=True, stop=True
                              ).then_inc(v_done, 1)
                    after(pe, ex_ready, j)
                    after(pe, run_ready, j - 1)
                    pe.matmul(flat(ps_p[:, :, :]), k.head_rows[:, :], ex[w][:, 0, :], start=True, stop=True)
                    pe.matmul(flat(ps_d[:, :, :]), k.head_rows[:, :], ex[w][:, 1, :], start=True, stop=True
                              ).then_inc(spread_done, 1)
                if live(i, S):
                    landed(pe, hs_in, i, u, TILES)
                    after(pe, hst_ready, i - 1)
                    for t in range(TILES):
                        ins = pe.transpose(ps_hs[:, t, :], hs[u][:, t, :], k.ident[:, :])
                    ins.then_inc(hs_turned, 1)
                    landed(pe, hd_in, i, u, TILES)
                    after(pe, hdt_ready, i - 1)
                    for t in range(TILES):
                        ins = pe.transpose(ps_hd[:, t, :], hd[u][:, t, :], k.ident[:, :])
                    ins.then_inc(hd_turned, 1)
                    after(pe, hst_ready, i)
                    after(pe, kq_ready, i - 1)
                    pe.matmul(flat(ps_k[:, :, :]), k.wk[:, :], hst[u][:, :], start=True, stop=True).then_inc(k_done, 1)
                if live(j, S):
                    after(pe, inv_ready, j)
                    after(pe, att_ready, j - 1)
                    pe.matmul(flat(ps_i[:, :, :]), k.head_rows[:, :], inv_den[w][:, :], start=True, stop=True
                              ).then_inc(inv_spread, 1)
                if live(i, S):
                    after(pe, kq_ready, i)
                    after(pe, arg_ready, i - 1)
                    pe.matmul(ps_s[:, :], k.head_cols[:, :], kq[u][:, :], start=True, stop=True
                              ).then_inc(score_done, 1)
                if live(j, S):
                    after(pe, att_ready, j)
                    after(pe, v_ready, j)
                    for t in range(TILES):
                        ins = pe.matmul(ps_vr[:, t, :], att[w][:, t * P:(t + 1) * P], k.wo[:, :], start=True,
                                        stop=True)
                    ins.then_inc(out_done, 1)
            run_steps(pe, body, S, 1)


def valid_columns(size, tile, i):
    if not isinstance(i, int) or (i + 1) * ROWS <= size.nodes:
        return tile[:, :, :]
    per = (size.nodes - i * ROWS) // TILES
    return tile[:, :, 0:per] if per > 0 else None


def attention_nodes(nc, size, scratch, k):
    S = size.steps
    with Phase(nc, "n1") as ph:
        h1, h1_in = ph.two("h1", [P, TILES, D]), ph.sem2("h1_in")
        agg, agg_in = ph.two("agg", [P, TILES, D]), ph.sem2("agg_in")
        total, total_ready = ph.two("total", [P, TILES, D]), ph.sem("total_ready")
        tt, tt_ready, tt_out = ph.two("tt", [D, TILES, P]), ph.sem("tt_ready"), ph.sem2("tt_out")
        turned = ph.sem("turned")
        stats_done = ph.sem("stats_done")
        ps_t = [ph.ps(f"t{u}") for u in range(2)]
        block = ph.ctx.enter_context(nc.Block())

        @block.sync
        def _(sp):
            def body(i, u):
                if live(i, S):
                    after(sp, total_ready, i - 2)
                    sp.dma_start(flat(agg[u][:, :, :]), rows_of(scratch["agg"], i)).then_inc(agg_in[u], 16)
                    sp.dma_start(flat(h1[u][:, :, :]), rows_of(scratch["h1"], i)).then_inc(h1_in[u], 16)
                j, w = i - 1, 1 - u
                if live(j, S):
                    after(sp, tt_ready, j)
                    sp.dma_start(cols_of(scratch["tt"], j), flat(tt[w][:, :, :])).then_inc(tt_out[w], 16)
            run_steps(sp, body, S, 1)
            for s in tt_out:
                sp.wait_ge(s, 16 * (S // 2))

        @block.vector
        def _(dve):
            def body(i, u):
                if live(i, S):
                    landed(dve, agg_in, i, u, 1)
                    landed(dve, h1_in, i, u, 1)
                    after(dve, turned, i - 2)
                    dve.tensor_tensor(total[u][:, :, :], agg[u][:, :, :], h1[u][:, :, :], ALU.add
                                      ).then_inc(total_ready, 1)
                j, w = i - 1, 1 - u
                if live(j, S):
                    after(dve, tt_ready, j)
                    cols = valid_columns(size, tt[w], j)
                    if cols is not None:
                        dve.bn_stats(k.bn_stats1[:, bass.ds(j, 1), :].rearrange("p a c -> p (a c)"), cols
                                     ).then_inc(stats_done, 1)
            run_steps(dve, body, S, 1)

        @block.tensor
        def _(pe):
            def body(i, u):
                if live(i, S):
                    after(pe, total_ready, i)
                    after(pe, tt_ready, i - 2)
                    for t in range(TILES):
                        ins = pe.transpose(ps_t[u][:, t, :], total[u][:, t, :], k.ident[:, :])
                    ins.then_inc(turned, 1)
            run_steps(pe, body, S, 0)

        @block.scalar
        def _(act):
            def body(i, u):
                if live(i, S):
                    after(act, turned, i)
                    landed(act, tt_out, i - 2, u, 1)
                    after(act, stats_done, i - 2)
                    act.activation(tt[u][:, :, :], ps_t[u][:, :, :], ACT.Identity, bias=k.bo[:, :]
                                   ).then_inc(tt_ready, 1)
            run_steps(act, body, S, 0)


def finish_batchnorm(nc, size, stats, gb, scale, shift, k, name):
    used = -(-size.nodes // ROWS)
    with Phase(nc, name) as ph:
        mv = ph.sb("mv", [D, 2])
        std = ph.sb("std", [D, 1])
        step = ph.sem("step")
        std_done = ph.sem("std_done")
        block = ph.ctx.enter_context(nc.Block())

        @block.vector
        def _(dve):
            dve.bn_aggr(mv[:, :], stats[:, 0:used, :].rearrange("p s c -> p (s c)")).then_inc(step, 1)
            dve.wait_ge(std_done, 1)
            dve.reciprocal(scale[:, :], std[:, :]).then_inc(step, 1)
            dve.wait_ge(step, 2)
            dve.tensor_tensor(scale[:, :], scale[:, :], gb[:, 0:1], ALU.mult).then_inc(step, 1)
            dve.wait_ge(step, 3)
            dve.tensor_tensor(shift[:, :], mv[:, 0:1], scale[:, :], ALU.mult).then_inc(step, 1)
            dve.wait_ge(step, 4)
            dve.tensor_tensor(shift[:, :], gb[:, 1:2], shift[:, :], ALU.subtract).then_inc(step, 1)

        @block.scalar
        def _(act):
            act.wait_ge(step, 1)
            act.activation(std[:, :], mv[:, 1:2], ACT.Sqrt, bias=k.eps[:, :]).then_inc(std_done, 1)


def feed_forward(nc, size, scratch, k):
    S = size.steps
    with Phase(nc, "ff") as ph:
        tt, tt_in = ph.two("tt", [D, ROWS]), ph.sem2("tt_in")
        hb, hb_ready = ph.two("hb", [D, TILES, P]), ph.sem("hb_ready")
        mid, mid_ready = ph.two("mid", [D, 2, ROWS]), ph.sem("mid_ready")
        ut, ut_ready, ut_out = ph.two("ut", [D, TILES, P]), ph.sem("ut_ready"), ph.sem2("ut_out")
        up_done, down_done, stats_done = ph.sem("up_done"), ph.sem("down_done"), ph.sem("stats_done")
        ps_m = [[ph.ps(f"m{u}{n}", (D, ROWS)) for n in range(2)] for u in range(2)]
        ps_u = [ph.ps(f"u{u}") for u in range(2)]
        block = ph.ctx.enter_context(nc.Block())

        @block.sync
        def _(sp):
            def body(i, u):
                if live(i, S):
                    after(sp, hb_ready, i - 2)
                    sp.dma_start(tt[u][:, :], cols_of(scratch["tt"], i)).then_inc(tt_in[u], 16)
                if live(i - 2, S):
                    after(sp, ut_ready, i - 2)
                    sp.dma_start(cols_of(scratch["ut"], i - 2), flat(ut[u][:, :, :])).then_inc(ut_out[u], 16)
            run_steps(sp, body, S, 2)
            for s in ut_out:
                sp.wait_ge(s, 16 * (S // 2))

        @block.scalar
        def _(act):
            def body(i, u):
                if live(i, S):
                    landed(act, tt_in, i, u, 1)
                    after(act, up_done, i - 2)
                    after(act, ut_ready, i - 2)
                    act.activation(flat(hb[u][:, :, :]), tt[u][:, :], ACT.Identity, bias=k.bn1_shift[:, :],
                                   scale=k.bn1_scale[:, :]).then_inc(hb_ready, 1)
                j, w = i - 1, 1 - u
                if live(j, S):
                    after(act, down_done, j - 2)
                    after(act, up_done, j)
                    for n in range(2):
                        ins = act.activation(mid[w][:, n, :], ps_m[w][n][:, :], ACT.Relu, bias=k.ff_b1[:, n:n + 1])
                    ins.then_inc(mid_ready, 1)
            run_steps(act, body, S, 1)

        @block.tensor
        def _(pe):
            def body(i, u):
                if live(i, S):
                    after(pe, hb_ready, i)
                    after(pe, mid_ready, i - 2)
                    for n in range(2):
                        ins = pe.matmul(ps_m[u][n][:, :], k.ff1[:, n, :], flat(hb[u][:, :, :]), start=True, stop=True)
                    ins.then_inc(up_done, 1)
                j, w = i - 1, 1 - u
                if live(j, S):
                    after(pe, mid_ready, j)
                    after(pe, ut_ready, j - 2)
                    for n in range(2):
                        ins = pe.matmul(flat(ps_u[w][:, :, :]), k.ff2[:, n, :], mid[w][:, n, :], start=(n == 0),
                                        stop=(n == 1))
                    ins.then_inc(down_done, 1)
            run_steps(pe, body, S, 1)

        @block.vector
        def _(dve):
            def body(i, u):
                j, w = i - 1, 1 - u
                if live(j, S):
                    after(dve, down_done, j)
                    landed(dve, ut_out, j - 2, w, 1)
                    after(dve, hb_ready, j)
                    after(dve, stats_done, j - 2)
                    dve.scalar_tensor_tensor(ut[w][:, :, :], ps_u[w][:, :, :], k.ff_b2[:, :], hb[w][:, :, :], ALU.add,
                                             ALU.add).then_inc(ut_ready, 1)
                    after(dve, ut_ready, j)
                    cols = valid_columns(size, ut[w], j)
                    if cols is not None:
                        dve.bn_stats(k.bn_stats2[:, bass.ds(j, 1), :].rearrange("p a c -> p (a c)"), cols
                                     ).then_inc(stats_done, 1)
            run_steps(dve, body, S, 1)


def second_norm_nodes(nc, size, scratch, k):
    S = size.steps
    with Phase(nc, "n3") as ph:
        ut, ut_in = ph.two("ut", [D, ROWS]), ph.sem2("ut_in")
        x1, x1_in = ph.two("x1", [P, TILES, D]), ph.sem2("x1_in")
        vt, vt_ready = ph.two("vt", [D, ROWS]), ph.sem("vt_ready")
        x2, x2_ready, x2_out = ph.two("x2", [P, TILES, D]), ph.sem("x2_ready"), ph.sem2("x2_out")
        h2, h2_ready, h2_out = ph.two("h2", [P, TILES, D]), ph.sem("h2_ready"), ph.sem2("h2_out")
        h2t, h2t_ready = ph.two("h2t", [D, TILES, P]), ph.sem("h2t_ready")
        own, own_ready, own_out = ph.two("own", [P, TILES, D]), ph.sem("own_ready"), ph.sem2("own_out")
        pool_turn = ph.sem("pool_turn")
        turned_back, h2_turned, own_done = ph.sem("turned_back"), ph.sem("h2_turned"), ph.sem("own_done")
        norm = Norm(ph, "norm")
        ps_v = [ph.ps(f"v{u}") for u in range(2)]
        ps_h = [ph.ps(f"h{u}") for u in range(2)]
        ps_o = [ph.ps(f"o{u}") for u in range(2)]
        block = ph.ctx.enter_context(nc.Block())

        @block.sync
        def _(sp):
            def body(i, u):
                if live(i, S):
                    after(sp, vt_ready, i - 2)
                    sp.dma_start(ut[u][:, :], cols_of(scratch["ut"], i)).then_inc(ut_in[u], 16)
                    after(sp, x2_ready, i - 2)
                    sp.dma_start(flat(x1[u][:, :, :]), rows_of(scratch["x1"], i)).then_inc(x1_in[u], 16)
                j, w = i - 1, 1 - u
                if live(j, S):
                    after(sp, x2_ready, j)
                    sp.dma_start(rows_of(scratch["x2"], j), flat(x2[w][:, :, :])).then_inc(x2_out[w], 16)
                if live(i - 2, S):
                    after(sp, h2_ready, i - 2)
                    sp.dma_start(rows_of(scratch["h2"], i - 2), flat(h2[u][:, :, :])).then_inc(h2_out[u], 16)
            run_steps(sp, body, S, 2)
            for s in (*x2_out, *h2_out):
                sp.wait_ge(s, 16 * (S // 2))

        @block.gpsimd
        def _(pool):
            def body(i, u):
                if live(i - 2, S):
                    after(pool, own_ready, i - 2)
                    pool.sem_inc(pool_turn, 1)
                    pool.dma_start(rows_of(scratch["sum"][0:size.rows, :], i - 2), flat(own[u][:, :, :])
                                   ).then_inc(own_out[u], 16)
            run_steps(pool, body, S, 2)
            for s in own_out:
                pool.wait_ge(s, 16 * (S // 2))

        @block.scalar
        def _(act):
            def body(i, u):
                if live(i, S):
                    landed(act, ut_in, i, u, 1)
                    after(act, turned_back, i - 2)
                    act.activation(vt[u][:, :], ut[u][:, :], ACT.Identity, bias=k.bn2_shift[:, :],
                                   scale=k.bn2_scale[:, :]).then_inc(vt_ready, 1)
                j, w = i - 1, 1 - u
                if live(j, S):
                    landed(act, h2_out, j - 2, w, 1)
                    after(act, h2_turned, j - 2)
                    norm.apply(act, h2[w], x2[w], ACT.Relu, j, w).then_inc(h2_ready, 1)
                if live(i, S):
                    norm.std_of(act, k.eps[:, :], i, u)
                if live(j, S):
                    after(act, h2_turned, j)
                    after(act, own_done, j - 2)
                    act.activation(h2t[w][:, :, :], ps_h[w][:, :, :], ACT.Copy).then_inc(h2t_ready, 1)
            run_steps(act, body, S, 1)

        @block.tensor
        def _(pe):
            def body(i, u):
                if live(i, S):
                    after(pe, vt_ready, i)
                    after(pe, x2_ready, i - 2)
                    for t in range(TILES):
                        ins = pe.transpose(ps_v[u][:, t, :], vt[u][:, t * P:(t + 1) * P], k.ident[:, :])
                    ins.then_inc(turned_back, 1)
                j, w = i - 1, 1 - u
                if live(j, S):
                    after(pe, h2_ready, j)
                    after(pe, h2t_ready, j - 2)
                    for t in range(TILES):
                        ins = pe.transpose(ps_h[w][:, t, :], h2[w][:, t, :], k.ident[:, :])
                    ins.then_inc(h2_turned, 1)
                if live(i - 2, S):
                    after(pe, h2t_ready, i - 2)
                    after(pe, own_ready, i - 4)
                    for t in range(TILES):
                        ins = pe.matmul(ps_o[u][:, t, :], h2t[u][:, t, :], k.w_center_cat[:, :], start=True, stop=True)
                    ins.then_inc(own_done, 1)
            run_steps(pe, body, S, 2)

        @block.vector
        def _(dve):
            def body(i, u):
                if live(i, S):
                    after(dve, turned_back, i)
                    landed(dve, x1_in, i, u, 1)
                    landed(dve, x2_out, i - 2, u, 1)
                    after(dve, h2_ready, i - 2)
                    dve.tensor_tensor(x2[u][:, :, :], ps_v[u][:, :, :], x1[u][:, :, :], ALU.add).then_inc(x2_ready, 1)
                    after(dve, x2_ready, i)
                    norm.moments_of(dve, x2[u], i, u)
                if live(i - 2, S):
                    after(dve, own_done, i - 2)
                    landed(dve, own_out, i - 4, u, 1)
                    dve.tensor_copy(own[u][:, :, :], ps_o[u][:, :, :]).then_inc(own_ready, 1)
                if live(i, S):
                    norm.scale_of(dve, i, u, h2_ready)
            run_steps(dve, body, S, 2)


def gated_edges(nc, size, a, scratch, k):
    S = size.steps
    with Phase(nc, "e2") as ph:
        idx, idx_in = ph.two("idx", [P, 8], I32), ph.sem2("idx_in")
        edge, edge_in = ph.two("edge", [EDGE_DIM, ROWS]), ph.sem2("edge_in")
        keys, keys_in = ph.two("keys", [P, ROWS], I32), ph.sem2("keys_in")
        mine, mine_ready = ph.two("mine", [P, TILES]), ph.sem("mine_ready")
        keys_f, keys_ready = ph.two("keys_f", [P, ROWS]), ph.sem("keys_ready")
        hd, hd_in = ph.two("hd", [P, TILES, D]), ph.sem2("hd_in")
        hdt, hdt_ready = ph.two("hdt", [D, TILES, P]), ph.sem("hdt_ready")
        gate, gate_ready = ph.two("gate", [P, TILES, D]), ph.sem("gate_ready")
        msg, msg_ready = ph.two("msg", [P, TILES, D]), ph.sem("msg_ready")
        same, same_ready = ph.two("same", [P, TILES, ROWS]), ph.sem("same_ready")
        spare = ph.sb("spare", [P, ROWS])
        last_place, last_ready = ph.two("last_place", [P, TILES]), ph.sem("last_ready")
        chosen, chosen_ready = ph.two("chosen", [P, TILES]), ph.sem("chosen_ready")
        gap, gap_ready = ph.two("gap", [P, TILES]), ph.sem("gap_ready")
        target, target_ready = ph.two("target", [P, TILES], I32), ph.sem("target_ready")
        sums, sums_ready = ph.two("sums", [D, TILES, P]), ph.sem("sums_ready")
        res, res_ready = ph.two("res", [P, TILES, D]), ph.sem("res_ready")
        added = ph.sem2("added")
        pool_turn, sp_turn, dve_turn = ph.sem("pool_turn"), ph.sem("sp_turn"), ph.sem("dve_turn")
        turned, proj_done, gate_done = ph.sem("turned"), ph.sem("proj_done"), ph.sem("gate_done")
        sums_done, out_done = ph.sem("sums_done"), ph.sem("out_done")
        ps_t = [ph.ps(f"t{u}") for u in range(2)]
        ps_p, ps_g = ph.ps("p"), ph.ps("g")
        ps_s = [ph.ps(f"s{u}") for u in range(2)]
        ps_r = [ph.ps(f"r{u}") for u in range(2)]
        block = ph.ctx.enter_context(nc.Block())

        @block.sync
        def _(sp):
            def body(i, u):
                if live(i, S):
                    landed(sp, hd_in, i - 2, u, TILES)
                    sp.sem_inc(sp_turn, 1)
                    after(sp, mine_ready, i - 2)
                    sp.dma_start(idx[u][:, :], a["idx"][:, bass.ds(i * 8, 8)]).then_inc(idx_in[u], 16)
                    after(sp, gate_done, i - 2)
                    sp.dma_start(edge[u][:, :], cols_of(a["edge32T"], i)).then_inc(edge_in[u], 16)
                    after(sp, keys_ready, i - 2)
                    sp.dma_start(keys[u][:, :], a["src_lin"][bass.ds(i, 1), :].rearrange(
                        "a c -> (a c)").partition_broadcast(P)).then_inc(keys_in[u], 16)
            run_steps(sp, body, S, 0)

        @block.gpsimd
        def _(pool):
            def body(i, u):
                if live(i, S):
                    landed(pool, idx_in, i, u, 1)
                    after(pool, turned, i - 2)
                    pool.sem_inc(pool_turn, 1)
                    gather(pool, hd[u], scratch["h2"], idx[u], TILES, hd_in[u])
                j = i - 2
                if live(j, S):
                    after(pool, target_ready, j)
                    after(pool, res_ready, j)
                    landed(pool, added, j - 1, 1 - u, TILES)
                    pool.sem_inc(pool_turn, 1)
                    for t in range(TILES):
                        pool.indirect_dma_start(out=scratch["sum"], out_offset=bass.IndirectOffsetOnAxis(
                            ap=target[u][:, t:t + 1], axis=0), in_=res[u][:, t, :], in_offset=None,
                            compute_op=ALU.add).then_inc(added[u], 16)
            run_steps(pool, body, S, 2)
            for u in range(2):
                pool.wait_ge(added[u], 16 * TILES * (S // 2))

        @block.vector
        def _(dve):
            def body(i, u):
                j, w = i - 1, 1 - u
                if live(i, S):
                    landed(dve, idx_in, i, u, 1)
                    after(dve, gap_ready, i - 2)
                    dve.tensor_copy(mine[u][:, :], idx[u][:, 0:TILES]).then_inc(mine_ready, 1)
                    landed(dve, keys_in, i, u, 1)
                    after(dve, same_ready, i - 2)
                    dve.tensor_copy(keys_f[u][:, :], keys[u][:, :]).then_inc(keys_ready, 1)
                    after(dve, mine_ready, i)
                    after(dve, keys_ready, i)
                    after(dve, sums_done, i - 2)
                    for t in range(TILES):
                        ins = dve.tensor_scalar(same[u][:, t, :], keys_f[u][:, :], mine[u][:, t:t + 1], None,
                                                ALU.is_equal)
                    ins.then_inc(same_ready, 1)
                if live(j, S):
                    after(dve, proj_done, j)
                    after(dve, gate_ready, j)
                    after(dve, sums_done, j - 2)
                    dve.tensor_tensor(msg[w][:, :, :], ps_p[:, :, :], gate[w][:, :, :], ALU.mult
                                      ).then_inc(msg_ready, 1)
                if live(i, S):
                    after(dve, same_ready, i)
                    for t in range(TILES):
                        if t:
                            after(dve, last_ready, i * TILES + t - 1)
                        elif not isinstance(i, int) or i:
                            after(dve, last_ready, i * TILES - 1)
                        dve.sem_inc(dve_turn, 1)
                        dve.tensor_tensor_reduce(spare[:, :], same[u][:, t, :], k.place_row[:, :], 1.0, 0.0, ALU.mult,
                                                 ALU.max, last_place[u][:, t:t + 1]).then_inc(last_ready, 1)
                    after(dve, last_ready, i * TILES + TILES - 1)
                    dve.tensor_tensor(gap[u][:, :], mine[u][:, :], k.dump_row[:, :], ALU.subtract)
                    dve.tensor_tensor(chosen[u][:, :], last_place[u][:, :], k.place[:, :], ALU.is_equal
                                      ).then_inc(chosen_ready, 1)
                    after(dve, chosen_ready, i)
                    dve.tensor_tensor(gap[u][:, :], gap[u][:, :], chosen[u][:, :], ALU.mult).then_inc(gap_ready, 1)
                    after(dve, gap_ready, i)
                    landed(dve, added, i - 2, u, TILES)
                    dve.tensor_tensor(target[u][:, :], gap[u][:, :], k.dump_row[:, :], ALU.add
                                      ).then_inc(target_ready, 1)
            run_steps(dve, body, S, 1)

        @block.scalar
        def _(act):
            def body(i, u):
                j, w = i - 1, 1 - u
                if live(j, S):
                    after(act, gate_done, j)
                    after(act, msg_ready, j - 2)
                    act.activation(gate[w][:, :, :], ps_g[:, :, :], ACT.Copy).then_inc(gate_ready, 1)
                if live(i, S):
                    after(act, turned, i)
                    after(act, proj_done, i - 2)
                    act.activation(hdt[u][:, :, :], ps_t[u][:, :, :], ACT.Copy).then_inc(hdt_ready, 1)
                if live(j, S):
                    after(act, sums_done, j)
                    after(act, out_done, j - 2)
                    act.activation(sums[w][:, :, :], ps_s[w][:, :, :], ACT.Copy).then_inc(sums_ready, 1)
                    after(act, out_done, j)
                    landed(act, added, j - 2, w, TILES)
                    act.activation(res[w][:, :, :], ps_r[w][:, :, :], ACT.Copy).then_inc(res_ready, 1)
            run_steps(act, body, S, 1)

        @block.tensor
        def _(pe):
            def body(i, u):
                j, w = i - 1, 1 - u
                if live(j, S):
                    landed(pe, edge_in, j, w, 1)
                    after(pe, gate_ready, j - 1)
                    for t in range(TILES):
                        ins = pe.matmul(ps_g[:, t, :], edge[w][:, t * P:(t + 1) * P], k.w_edge[:, :], start=True,
                                        stop=True)
                    ins.then_inc(gate_done, 1)
                    after(pe, hdt_ready, j)
                    after(pe, msg_ready, j - 1)
                    for t in range(TILES):
                        ins = pe.matmul(ps_p[:, t, :], hdt[w][:, t, :], k.w_node[:, :], start=True, stop=True)
                    ins.then_inc(proj_done, 1)
                if live(i, S):
                    landed(pe, hd_in, i, u, TILES)
                    after(pe, hdt_ready, i - 2)
                    for t in range(TILES):
                        ins = pe.transpose(ps_t[u][:, t, :], hd[u][:, t, :], k.ident[:, :])
                    ins.then_inc(turned, 1)
                if live(j, S):
                    after(pe, msg_ready, j)
                    after(pe, same_ready, j)
                    after(pe, sums_ready, j - 2)
                    for t in range(TILES):
                        ins = pe.matmul(flat(ps_s[w][:, :, :]), msg[w][:, t, :], same[w][:, t, :], start=(t == 0),
                                        stop=(t == TILES - 1))
                    ins.then_inc(sums_done, 1)
                    after(pe, sums_ready, j)
                    after(pe, res_ready, j - 2)
                    for t in range(TILES):
                        ins = pe.matmul(ps_r[w][:, t, :], sums[w][:, t, :], k.w_cat_sum[:, :], start=True, stop=True)
                    ins.then_inc(out_done, 1)
            run_steps(pe, body, S, 1)


def gated_nodes(nc, size, scratch, k):
    S = size.steps
    with Phase(nc, "n4") as ph:
        z, z_in = ph.two("z", [P, TILES, D]), ph.sem2("z_in")
        x2, x2_in = ph.two("x2", [P, TILES, D]), ph.sem2("x2_in")
        zn, zn_ready = ph.two("zn", [P, TILES, D]), ph.sem("zn_ready")
        zw, zw_ready = ph.two("zw", [P, TILES, D]), ph.sem("zw_ready")
        xb, xb_ready = ph.two("xb", [P, TILES, D]), ph.sem("xb_ready")
        x3, x3_ready, x3_out = ph.two("x3", [P, TILES, D]), ph.sem("x3_ready"), ph.sem2("x3_out")
        h3, h3_ready, h3_out = ph.two("h3", [P, TILES, D]), ph.sem("h3_ready"), ph.sem2("h3_out")
        pool_turn = ph.sem("pool_turn")
        first, second = Norm(ph, "first"), Norm(ph, "second")
        block = ph.ctx.enter_context(nc.Block())

        @block.sync
        def _(sp):
            def body(i, u):
                if live(i, S):
                    after(sp, zn_ready, i - 2)
                    sp.dma_start(flat(z[u][:, :, :]), rows_of(scratch["sum"][0:size.rows, :], i)).then_inc(z_in[u], 16)
                    after(sp, xb_ready, i - 2)
                    sp.dma_start(flat(x2[u][:, :, :]), rows_of(scratch["x2"], i)).then_inc(x2_in[u], 16)
                if live(i - 2, S):
                    after(sp, x3_ready, i - 2)
                    sp.dma_start(rows_of(scratch["x3"], i - 2), flat(x3[u][:, :, :])).then_inc(x3_out[u], 16)
                    after(sp, h3_ready, i - 2)
                    sp.dma_start(rows_of(scratch["h3"], i - 2), flat(h3[u][:, :, :])).then_inc(h3_out[u], 16)
            run_steps(sp, body, S, 2)
            for s in (*x3_out, *h3_out):
                sp.wait_ge(s, 16 * (S // 2))

        @block.gpsimd
        def _(pool):
            def body(i, u):
                if live(i, S):
                    landed(pool, x2_in, i, u, 1)
                    after(pool, x3_ready, i - 2)
                    pool.sem_inc(pool_turn, 1)
                    pool.tensor_tensor(xb[u][:, :, :], x2[u][:, :, :], k.ln_b_rep[:, :, :], ALU.add
                                       ).then_inc(xb_ready, 1)
            run_steps(pool, body, S, 0)

        @block.vector
        def _(dve):
            def body(i, u):
                j, w = i - 1, 1 - u
                if live(i, S):
                    landed(dve, z_in, i, u, 1)
                    first.moments_of(dve, z[u], i, u)
                if live(j, S):
                    after(dve, zn_ready, j)
                    after(dve, x3_ready, j - 2)
                    dve.tensor_tensor(zw[w][:, :, :], zn[w][:, :, :], k.ln_w_rep[:, :, :], ALU.mult
                                      ).then_inc(zw_ready, 1)
                    after(dve, zw_ready, j)
                    after(dve, xb_ready, j)
                    landed(dve, x3_out, j - 2, w, 1)
                    after(dve, h3_ready, j - 2)
                    dve.tensor_tensor(x3[w][:, :, :], zw[w][:, :, :], xb[w][:, :, :], ALU.add).then_inc(x3_ready, 1)
                if live(i, S):
                    first.scale_of(dve, i, u, zn_ready)
                if live(j, S):
                    after(dve, x3_ready, j)
                    second.moments_of(dve, x3[w], j, w)
                if live(i - 2, S):
                    second.scale_of(dve, i - 2, u, h3_ready)
            run_steps(dve, body, S, 2)

        @block.scalar
        def _(act):
            def body(i, u):
                if live(i, S):
                    first.std_of(act, k.eps[:, :], i, u)
                    after(act, zw_ready, i - 2)
                    first.apply(act, zn[u], z[u], ACT.Identity, i, u).then_inc(zn_ready, 1)
                if live(i - 1, S):
                    second.std_of(act, k.eps[:, :], i - 1, 1 - u)
                if live(i - 2, S):
                    landed(act, h3_out, i - 4, u, 1)
                    second.apply(act, h3[u], x3[u], ACT.Relu, i - 2, u).then_inc(h3_ready, 1)
            run_steps(act, body, S, 2)


def relation_edges(nc, size, a, scratch, k):
    S = size.steps
    with Phase(nc, "e3") as ph:
        idx, idx_in = ph.two("idx", [P, 8], I32), ph.sem2("idx_in")
        col, col_in = ph.two("col", [1, 2, ROWS], BF16), ph.sem2("col_in")
        row, row_in = ph.two("row", [P, 12], I32), ph.sem2("row_in")
        again, again_in = ph.two("again", [P, 12], I32), ph.sem2("again_in")
        hs, hs_in = ph.two("hs", [P, TILES, D]), ph.sem2("hs_in")
        part, part_ready = ph.two("part", [P, TILES, D]), ph.sem("part_ready")
        hst, hst_ready = ph.two("hst", [D, ROWS]), ph.sem("hst_ready")
        by_rel, by_rel_ready = ph.two("by_rel", [D, RELS, ROWS]), ph.sem("by_rel_ready")
        msg, msg_ready = ph.two("msg", [D, ROWS]), ph.sem("msg_ready")
        run, run_ready = ph.two("run", [D, ROWS]), ph.sem("run_ready")
        res, res_ready = ph.two("res", [P, TILES, D]), ph.sem("res_ready")
        scattered = ph.sem2("scattered")
        pool_turn = ph.sem("pool_turn")
        turned, type_done, keep_done = ph.sem("turned"), ph.sem("type_done"), ph.sem("keep_done")
        msg_done, out_done = ph.sem("msg_done"), ph.sem("out_done")
        ps_t, ps_y, ps_k = ph.ps("t"), ph.ps("y"), [ph.ps(f"k{u}") for u in range(2)]
        ps_m = [ph.ps(f"m{u}") for u in range(2)]
        ps_r = [ph.ps(f"r{u}") for u in range(2)]
        block = ph.ctx.enter_context(nc.Block())

        @block.sync
        def _(sp):
            def body(i, u):
                if live(i, S):
                    landed(sp, hs_in, i - 2, u, TILES)
                    sp.dma_start(idx[u][:, :], a["idx"][:, bass.ds(i * 8, 8)]).then_inc(idx_in[u], 16)
                    after(sp, keep_done, i - 2)
                    after(sp, type_done, i - 2)
                    sp.dma_start(flat(col[u][:, :, :]), scratch["col_tab"].rearrange("s a c -> s (a c)")[bass.ds(i, 1), :]
                                 ).then_inc(col_in[u], 16)
                    after(sp, part_ready, i - 2)
                    sp.dma_start(row[u][:, :], scratch["row_tab"].rearrange("p s c -> p (s c)")[:, bass.ds(i * 12, 12)]
                                 ).then_inc(row_in[u], 16)
                j, w = i - 1, 1 - u
                if live(j, S):
                    landed(sp, scattered, j - 2, w, TILES)
                    sp.dma_start(again[w][:, :], scratch["row_tab"].rearrange("p s c -> p (s c)")[:, bass.ds(j * 12, 12)]
                                 ).then_inc(again_in[w], 16)
            run_steps(sp, body, S, 1)

        @block.gpsimd
        def _(pool):
            def body(i, u):
                if live(i, S):
                    landed(pool, idx_in, i, u, 1)
                    after(pool, part_ready, i - 2)
                    pool.sem_inc(pool_turn, 1)
                    gather(pool, hs[u], scratch["h3"], idx[u], 0, hs_in[u])
                j = i - 2
                if live(j, S):
                    landed(pool, again_in, j, u, 1)
                    after(pool, res_ready, j)
                    pool.sem_inc(pool_turn, 1)
                    scatter(pool, scratch["agg"], res[u], again[u], size.rows - 1, scattered[u])
            run_steps(pool, body, S, 2)
            for u in range(2):
                pool.wait_ge(scattered[u], 16 * TILES * (S // 2))

        @block.vector
        def _(dve):
            def body(i, u):
                j, w = i - 1, 1 - u
                if live(i, S):
                    landed(dve, hs_in, i, u, TILES)
                    landed(dve, row_in, i, u, 1)
                    after(dve, turned, i - 2)
                    dve.tensor_tensor(part[u][:, :, :], hs[u][:, :, :], spread(row[u][:, 8:12].bitcast(F32), D),
                                      ALU.mult).then_inc(part_ready, 1)
                if live(j, S):
                    after(dve, msg_ready, j)
                    after(dve, keep_done, j)
                    after(dve, out_done, j - 2)
                    after(dve, run_ready, j - 1)
                    before = 0.0 if isinstance(j, int) and j == 0 else run[1 - w][:, ROWS - 1:ROWS]
                    dve.tensor_tensor_scan(run[w][:, :], flat(ps_k[w][:, :, :]), msg[w][:, :], before, ALU.mult,
                                           ALU.add).then_inc(run_ready, 1)
                if live(i, S):
                    after(dve, hst_ready, i)
                    after(dve, type_done, i)
                    after(dve, msg_done, i - 2)
                    for r in range(RELS):
                        ins = dve.scalar_tensor_tensor(by_rel[u][:, r, :], flat(ps_y[:, :, :]), float(r), hst[u][:, :],
                                                       ALU.is_equal, ALU.mult)
                    ins.then_inc(by_rel_ready, 1)
            run_steps(dve, body, S, 1)

        @block.scalar
        def _(act):
            def body(i, u):
                j, w = i - 1, 1 - u
                if live(i, S):
                    after(act, turned, i)
                    after(act, by_rel_ready, i - 2)
                    act.activation(hst[u][:, :], flat(ps_t[:, :, :]), ACT.Copy).then_inc(hst_ready, 1)
                if live(j, S):
                    after(act, msg_done, j)
                    after(act, run_ready, j - 2)
                    act.activation(msg[w][:, :], flat(ps_m[w][:, :, :]), ACT.Copy).then_inc(msg_ready, 1)
                    after(act, out_done, j)
                    landed(act, scattered, j - 2, w, TILES)
                    act.activation(res[w][:, :, :], ps_r[w][:, :, :], ACT.Copy).then_inc(res_ready, 1)
            run_steps(act, body, S, 1)

        @block.tensor
        def _(pe):
            def body(i, u):
                j, w = i - 1, 1 - u
                if live(i, S):
                    landed(pe, col_in, i, u, 1)
                    after(pe, by_rel_ready, i - 1)
                    pe.matmul(flat(ps_y[:, :, :]), k.ones_row[:, :], col[u][:, 1, :], start=True, stop=True
                              ).then_inc(type_done, 1)
                    after(pe, run_ready, i - 2)
                    pe.matmul(flat(ps_k[u][:, :, :]), k.ones_row[:, :], col[u][:, 0, :], start=True, stop=True
                              ).then_inc(keep_done, 1)
                    after(pe, part_ready, i)
                    after(pe, hst_ready, i - 1)
                    for t in range(TILES):
                        ins = pe.transpose(ps_t[:, t, :], part[u][:, t, :], k.ident[:, :])
                    ins.then_inc(turned, 1)
                if live(j, S):
                    after(pe, by_rel_ready, j)
                    after(pe, msg_ready, j - 2)
                    for r in range(RELS):
                        ins = pe.matmul(flat(ps_m[w][:, :, :]), k.rel_w[:, r, :], by_rel[w][:, r, :], start=(r == 0),
                                        stop=(r == RELS - 1))
                    ins.then_inc(msg_done, 1)
                    after(pe, run_ready, j)
                    after(pe, res_ready, j - 2)
                    for t in range(TILES):
                        ins = pe.transpose(ps_r[w][:, t, :], run[w][:, t * P:(t + 1) * P], k.ident[:, :])
                    ins.then_inc(out_done, 1)
            run_steps(pe, body, S, 1)


def relation_nodes(nc, size, scratch, out, k):
    S = size.steps
    with Phase(nc, "n5") as ph:
        x3, x3_in = ph.two("x3", [P, TILES, D]), ph.sem2("x3_in")
        agg, agg_in = ph.two("agg", [P, TILES, D]), ph.sem2("agg_in")
        xb, xb_ready = ph.two("xb", [P, TILES, D]), ph.sem("xb_ready")
        res, res_ready, res_out = ph.two("res", [P, TILES, D]), ph.sem("res_ready"), ph.sem2("res_out")
        block = ph.ctx.enter_context(nc.Block())

        @block.sync
        def _(sp):
            def body(i, u):
                if live(i, S):
                    after(sp, xb_ready, i - 2)
                    sp.dma_start(flat(x3[u][:, :, :]), rows_of(scratch["x3"], i)).then_inc(x3_in[u], 16)
                    after(sp, res_ready, i - 2)
                    sp.dma_start(flat(agg[u][:, :, :]), rows_of(scratch["agg"], i)).then_inc(agg_in[u], 16)
                j, w = i - 1, 1 - u
                if live(j, S):
                    after(sp, res_ready, j)
                    sp.dma_start(rows_of(out, j), flat(res[w][:, :, :])).then_inc(res_out[w], 16)
            run_steps(sp, body, S, 1)
            for s in res_out:
                sp.wait_ge(s, 16 * (S // 2))

        @block.vector
        def _(dve):
            def body(i, u):
                if live(i, S):
                    landed(dve, x3_in, i, u, 1)
                    after(dve, res_ready, i - 2)
                    dve.tensor_tensor(xb[u][:, :, :], x3[u][:, :, :], k.rel_b_rep[:, :, :], ALU.add
                                      ).then_inc(xb_ready, 1)
                    after(dve, xb_ready, i)
                    landed(dve, agg_in, i, u, 1)
                    landed(dve, res_out, i - 2, u, 1)
                    dve.tensor_tensor(res[u][:, :, :], xb[u][:, :, :], agg[u][:, :, :], ALU.add
                                      ).then_inc(res_ready, 1)
            run_steps(dve, body, S, 0)


def padded(a, rows, fill):
    out = np.full((rows, *a.shape[1:]), fill, a.dtype)
    out[:a.shape[0]] = a
    return out


def kernel(**inputs):
    from concourse import bacc
    from concourse.bass_utils import run_bass_kernel_spmd

    g = {n: np.asarray(v) for n, v in inputs.items()}
    nodes, edges = g["x"].shape[0], g["src"].shape[0]
    size = Sizes(nodes, edges)
    S, R = size.steps, size.rows
    i32 = np.int32

    src = padded(g["src"].astype(i32, copy=False), R, nodes)
    dst = padded(g["dst"].astype(i32, copy=False), R, nodes)
    kind = padded(g["edge_type_8"].astype(i32, copy=False), R, 0)
    before = np.concatenate([np.full(1, -1, i32), dst[:-1]])
    behind = np.concatenate([dst[1:], np.full(1, -1, i32)])

    def by_place(v):
        return v.reshape(S, TILES, P).transpose(2, 0, 1)

    col = lambda v: v.reshape(-1, 1)
    row = lambda v: v.reshape(1, -1)
    arrays = {
        "x": padded(g["x"], R, 0),
        "edge128T": padded(g["edge_attr_128"], R, 0).T,
        "edge32T": padded(g["edge_attr_32"], R, 0).T,
        "idx": np.concatenate([by_place(src), by_place(dst)], axis=2).reshape(P, S * 2 * TILES),
        "edge_lin": np.stack([v.reshape(S, ROWS) for v in (dst, before, behind, kind)]),
        "src_lin": src.reshape(S, ROWS),
        "edge_rows": np.stack([by_place(dst).reshape(P, -1), by_place(behind).reshape(P, -1)], axis=1),
        "L0_W1": g["L0_gnn_W1"], "L0_W2": g["L0_gnn_W2"], "L0_b1": col(g["L0_gnn_b1"]), "L0_b2": row(g["L0_gnn_b2"]),
        "L1_WkT": g["L1_gnn_Wk"].T, "L1_WvT": g["L1_gnn_Wv"].T, "L1_WoT": g["L1_gnn_Wo"].T,
        "L1_bk": col(g["L1_gnn_bk"]), "L1_bv": col(g["L1_gnn_bv"]), "L1_bo": col(g["L1_gnn_bo"]),
        "L1_W1T": g["L1_gnn_W1"].T, "L1_W2T": g["L1_gnn_W2"].T,
        "L1_b1": g["L1_gnn_b1"].reshape(2, D).T, "L1_b2": col(g["L1_gnn_b2"]),
        "L1_bn": np.stack([g["L1_gnn_bn1_g"], g["L1_gnn_bn1_b"], g["L1_gnn_bn2_g"], g["L1_gnn_bn2_b"]], axis=1),
        "L2_W_node": g["L2_gnn_W_node"], "L2_W_centerT": g["L2_gnn_W_center_node"].T,
        "L2_W_cat": g["L2_gnn_W_concat_node"], "L2_W_edge": g["L2_gnn_W_edge"],
        "L2_ln_w": row(g["L2_gnn_ln_weight"]), "L2_ln_b": row(g["L2_gnn_ln_bias"]),
        "L3_W": g["L3_gnn_weight"], "L3_b": row(g["L3_gnn_bias"]),
    }
    arrays = {n: np.ascontiguousarray(v) for n, v in arrays.items()}

    nc = bacc.Bacc("TRN2", target_bir_lowering=False, num_devices=1)
    a = {n: nc.dram_tensor(n, v.shape, mybir.dt.from_np(v.dtype), kind="ExternalInput").ap() for n, v in arrays.items()}
    out = nc.dram_tensor("out", (R, D), F32, kind="ExternalOutput").ap()

    def table(name, shape, dt=F32):
        return nc.dram_tensor(f"{name}_table", shape, dt).ap()

    scratch = {n: table(n, (R, D)) for n in ("agg", "x1", "h1", "x2", "h2", "x3", "h3")}
    scratch["sum"] = table("sum", (R + ROWS, D))
    scratch["tt"] = table("tt", (D, R))
    scratch["ut"] = table("ut", (D, R))
    scratch["col_tab"] = table("col_tab", (S, 2, ROWS), BF16)
    scratch["drop"] = table("drop", (S, ROWS))
    scratch["row_tab"] = table("row_tab", (P, S, 12), I32)
    build(nc, size, a, out, scratch)
    r = run_bass_kernel_spmd(nc, [arrays], core_ids=[0])
    return r.results[0]["out"][:nodes]
```

```python
from contextlib import ExitStack

import numpy as np

import concourse.bass as bass
from concourse import mybir

ALU = mybir.AluOpType
ACT = mybir.ActivationFunctionType
F32 = mybir.dt.float32
BF16 = mybir.dt.bfloat16
I32 = mybir.dt.int32

P = 128
D = 128
TILES = 4
ROWS = TILES * P
HEADS = 8
HEAD_DIM = D // HEADS
RELS = 8
EDGE_DIM = 32
EPS = 1e-5
SLOPE = (1.0 / 8.0 + 1.0 / 3.0) / 2.0
FAR = float(1 << 22)
LOW = 1e30
PEEL = 8
UNROLL = 4
SLOTS = 4
ENDING = 2


def steps_of(rows):
    s = rows // ROWS + 1
    return max(PEEL + UNROLL, -(-(s - ENDING) // UNROLL) * UNROLL) + ENDING


class Sizes:
    def __init__(self, nodes, edges):
        self.nodes = nodes
        self.steps = steps_of(max(nodes, edges))
        self.rows = self.steps * ROWS


def run_steps(eng, body, steps, lag):
    for i in range(PEEL):
        body(i, i % UNROLL)
    with eng.Fori(PEEL, steps - ENDING - UNROLL + 1, UNROLL) as i:
        for u in range(UNROLL):
            body(i + u, u)
    for i in range(steps - ENDING, steps + lag):
        body(i, i % UNROLL)


def live(j, steps):
    return not isinstance(j, int) or 0 <= j < steps


def begun(j):
    return not isinstance(j, int) or j >= 0


def moved(j, u, dmas=1):
    return (j - u % SLOTS) * (16 * dmas // SLOTS) + 16 * dmas


def all_moved(steps, u, dmas=1):
    return len(range(u, steps, SLOTS)) * 16 * dmas


def at(slots, u):
    return slots[u % len(slots)]


def rows_of(table, i):
    return table.rearrange("(s p t) d -> s p (t d)", p=P, t=TILES)[bass.ds(i, 1), :, :].rearrange(
        "s p c -> (s p) c")


def cols_of(table, i):
    return table[:, bass.ds(i * ROWS, ROWS)]


def idx_of(a, i):
    return a["idx"][:, bass.ds(i * 2 * TILES, 2 * TILES)]


def row_values_of(scratch, i):
    return scratch["row_tab"].rearrange("p s c -> p (s c)")[:, bass.ds(i * 3 * TILES, 3 * TILES)]


def col_values_of(scratch, i):
    return scratch["col_tab"].rearrange("s a c -> s (a c)")[bass.ds(i, 1), :]


def flat(tile):
    return tile[:, :, :].rearrange("p t c -> p (t c)")


def spread(cols, n):
    return cols.unsqueeze(2).broadcast_to([cols.shape[0], cols.shape[1], n])


class Phase:

    def __init__(self, nc, name):
        self.nc, self.name, self.ctx, self.sems = nc, name, ExitStack(), []

    def sb(self, name, shape, dt=F32):
        return self.ctx.enter_context(self.nc.sbuf_tensor(f"{self.name}_{name}", shape, dt))

    def slots(self, n, name, shape, dt=F32):
        return [self.sb(f"{name}{u}", shape, dt) for u in range(n)]

    def ps(self, name, shape=(P, TILES, P)):
        return self.ctx.enter_context(self.nc.psum_tensor(f"{self.name}_{name}", list(shape), F32))

    def banks(self, name):
        return [self.ps(f"{name}{u}") for u in range(2)]

    def sem(self, name):
        self.sems.append(self.nc.alloc_semaphore(f"{self.name}_{name}"))
        return self.sems[-1]

    def dma_sems(self, name, n=SLOTS):
        return [self.sem(f"{name}{u}") for u in range(n)]

    def loaded(self, name, shape, dt=F32):
        return self.slots(4, name, shape, dt), self.dma_sems(name + "_in")

    def made(self, name, shape, n=2, dt=F32):
        return self.slots(n, name, shape, dt), self.sem(name + "_ready")

    def __enter__(self):
        return self

    def __exit__(self, *a):
        self.ctx.__exit__(*a)
        if a[0] is None:
            self.nc.clear_and_free_semaphores(self.sems)
            self.nc.all_engine_barrier()


class Norm:

    def __init__(self, ph, name):
        self.stats, self.stats_done = ph.made(name + "_stats", [P, TILES, 6])
        self.moments, self.moments_done = ph.made(name + "_moments", [P, TILES, 2], 4)
        self.std, self.std_done = ph.made(name + "_std", [P, TILES], 4)
        self.rstd, self.rstd_done = ph.made(name + "_rstd", [P, TILES], 4)
        self.shift, self.shift_done = ph.made(name + "_shift", [P, TILES], 4)
        self.turn = ph.sem(name + "_turn")

    def moments_of(self, dve, x, i, u):
        for t in range(TILES):
            last = dve.bn_stats(at(self.stats, u)[:, t, :], x[:, t, :])
        last.then_inc(self.stats_done, 1)
        dve.wait_ge(self.stats_done, i + 1)
        if begun(i - 4):
            dve.wait_ge(self.shift_done, i - 3)
        dve.sem_inc(self.turn, 1)
        for t in range(TILES):
            last = dve.bn_aggr(at(self.moments, u)[:, t, :], at(self.stats, u)[:, t, :])
        last.then_inc(self.moments_done, 1)

    def std_of(self, act, k, i, u):
        act.wait_ge(self.moments_done, i + 1)
        if begun(i - 4):
            act.wait_ge(self.rstd_done, i - 3)
        act.activation(at(self.std, u)[:, :], at(self.moments, u)[:, :, 1], ACT.Sqrt, bias=k.eps[:, :]
                       ).then_inc(self.std_done, 1)

    def scale_of(self, dve, i, u, used):
        dve.wait_ge(self.std_done, i + 1)
        if begun(i - 4):
            dve.wait_ge(used, i - 3)
        dve.reciprocal(at(self.rstd, u)[:, :], at(self.std, u)[:, :]).then_inc(self.rstd_done, 1)
        dve.wait_ge(self.rstd_done, i + 1)
        dve.scalar_tensor_tensor(at(self.shift, u)[:, :], at(self.moments, u)[:, :, 0], -1.0, at(self.rstd, u)[:, :],
                                 ALU.mult, ALU.mult).then_inc(self.shift_done, 1)

    def apply(self, act, out, x, func, i, u):
        act.wait_ge(self.shift_done, i + 1)
        for t in range(TILES):
            last = act.activation(out[:, t, :], x[:, t, :], func, bias=at(self.shift, u)[:, t:t + 1],
                                  scale=at(self.rstd, u)[:, t:t + 1])
        return last


class Kept:

    def __init__(self, nc, ctx, size):
        def tile(name, shape, dt=F32):
            return ctx.enter_context(nc.sbuf_tensor(name, shape, dt))

        self.ident = tile("ident", [D, D])
        self.w1_node = tile("w1_node", [D, D])
        self.w1_edge = tile("w1_edge", [D, D])
        self.w2_plus_one = tile("w2_plus_one", [D, D])
        self.wk = tile("wk", [D, D])
        self.wv = tile("wv", [D, D])
        self.wo = tile("wo", [D, D])
        self.w_node = tile("w_node", [D, D])
        self.w_center_cat = tile("w_center_cat", [D, D])
        self.w_cat_sum = tile("w_cat_sum", [D, D])
        self.ff1 = tile("ff1", [D, 2, D])
        self.ff2 = tile("ff2", [D, 2, D])
        self.rel_w = tile("rel_w", [D, RELS, D])
        self.w_edge = tile("w_edge", [EDGE_DIM, D])
        self.b1 = tile("b1", [D, 1])
        self.bk = tile("bk", [D, 1])
        self.bv = tile("bv", [D, 1])
        self.bo = tile("bo", [D, 1])
        self.ff_b2 = tile("ff_b2", [D, 1])
        self.eps = tile("eps", [D, 1])
        self.tiny = tile("tiny", [D, 1])
        self.bn1_scale = tile("bn1_scale", [D, 1])
        self.bn1_shift = tile("bn1_shift", [D, 1])
        self.bn2_scale = tile("bn2_scale", [D, 1])
        self.bn2_shift = tile("bn2_shift", [D, 1])
        self.ff_b1 = tile("ff_b1", [D, 2])
        self.bn = tile("bn", [D, 4])
        self.ones_row = tile("ones_row", [1, P], BF16)
        self.heads = tile("heads", [D, D])
        self.b2_rep = tile("b2_rep", [P, TILES, D])
        self.rel_b_rep = tile("rel_b_rep", [P, TILES, D])
        self.ln_w_rep = tile("ln_w_rep", [P, TILES, D])
        self.ln_b_rep = tile("ln_b_rep", [P, TILES, D])
        self.place = tile("place", [P, TILES])
        self.dump_row = tile("dump_row", [P, TILES])
        self.place_row = tile("place_row", [P, ROWS])
        self.bn_stats1 = tile("bn_stats1", [D, size.steps, 6])
        self.bn_stats2 = tile("bn_stats2", [D, size.steps, 6])


def build(nc, size, a, out, scratch):
    with ExitStack() as ctx:
        k = Kept(nc, ctx, size)

        prepare(nc, size, a, scratch, k)
        mean_edges(nc, size, a, scratch, k)
        mean_nodes(nc, size, a, scratch, k)
        attention_edges(nc, size, a, scratch, k)
        attention_nodes(nc, size, scratch, k)
        feed_forward(nc, size, scratch, k)
        second_norm_nodes(nc, size, scratch, k)
        gated_edges(nc, size, a, scratch, k)
        gated_nodes(nc, size, scratch, k)
        relation_edges(nc, size, a, scratch, k)
        relation_nodes(nc, size, scratch, out, k)


def prepare(nc, size, a, scratch, k):
    S = size.steps
    with Phase(nc, "prep") as ph:
        weights_in = ph.sem("weights_in")
        lists_in = ph.sem("lists_in")
        stored = ph.sem("stored")
        consts = ph.sem("consts")
        chain = ph.sem("chain")
        rel_sums_ready = ph.sem("rel_sums_ready")
        flipped = ph.sem("flipped")
        tables_done = ph.sem("tables_done")
        zero_ready = ph.sem("zero_ready")

        w2 = ph.sb("w2", [D, D])
        w_center_t = ph.sb("w_center_t", [D, D])
        w_cat_node = ph.sb("w_cat_node", [D, D])
        raw = ph.sb("raw", [S, 4, ROWS], I32)
        row_lists = ph.sb("row_lists", [P, 2, S * TILES], I32)
        offset_i = ph.sb("offset_i", [D, HEADS, HEAD_DIM], I32)
        at_least = ph.sb("at_least", [D, D])
        place_i = ph.sb("place_i", [P, TILES], I32)
        place_row_i = ph.sb("place_row_i", [P, ROWS], I32)
        edge_i = ph.sb("edge_i", [S, ROWS], I32)
        zero = ph.sb("zero", [P, ROWS])
        edge_at = ph.sb("edge_at", [S, ROWS])
        first = ph.sb("first", [S, ROWS])
        last = ph.sb("last", [S, ROWS])
        col_tab = ph.sb("col_tab", [S, 3, ROWS], BF16)
        inv_deg = ph.sb("inv_deg", [S, ROWS])
        inv_rel = ph.sb("inv_rel", [S, ROWS])
        one_rel = ph.sb("one_rel", [S, ROWS])
        none = ph.sb("none", [S, ROWS])
        work = ph.sb("work", [S, ROWS])
        work2 = ph.sb("work2", [S, ROWS])
        counts = ph.sb("counts", [S, RELS, ROWS])
        starts = ph.sb("starts", [S, RELS, ROWS])
        ends = ph.sb("ends", [S, RELS, ROWS])
        totals = ph.sb("totals", [S, 3, 32])
        totals_t = ph.sb("totals_t", [32, S])
        carried = ph.sb("carried", [32, 3, S + 1])
        carry = ph.sb("carry", [S, 3, 32])
        row_tab = ph.sb("row_tab", [P, S, 12], I32)
        ps_a = ph.ps("a")
        ps_b = ph.ps("b")
        block = ph.ctx.enter_context(nc.Block())

        @block.sync
        def _(sp):
            for tile, src in (
                (k.w1_node, a["L0_W1"][0:D, :]), (k.w1_edge, a["L0_W1"][D:2 * D, :]), (w2, a["L0_W2"]),
                (k.wk, a["L1_WkT"]), (k.wv, a["L1_WvT"]), (k.wo, a["L1_WoT"]), (k.w_node, a["L2_W_node"]),
                (w_center_t, a["L2_W_centerT"]), (w_cat_node, a["L2_W_cat"][0:D, :]),
                (k.w_cat_sum, a["L2_W_cat"][D:2 * D, :]), (k.w_edge, a["L2_W_edge"]),
                (k.b1, a["L0_b1"]), (k.bk, a["L1_bk"]), (k.bv, a["L1_bv"]), (k.bo, a["L1_bo"]),
                (k.ff_b1, a["L1_b1"]), (k.ff_b2, a["L1_b2"]), (k.bn, a["L1_bn"]),
            ):
                sp.dma_start(tile[:, :], src[:, :]).then_inc(weights_in, 16)
            sp.dma_start(k.ff1[:, :, :], a["L1_W1T"].rearrange("d (h n) -> d h n", h=2)).then_inc(weights_in, 16)
            sp.dma_start(k.ff2[:, :, :], a["L1_W2T"].rearrange("(h d) n -> d h n", h=2)).then_inc(weights_in, 16)
            sp.dma_start(k.rel_w[:, :, :], a["L3_W"].rearrange("r d n -> d r n")).then_inc(weights_in, 16)
            for tile, src in ((k.b2_rep, a["L0_b2"]), (k.ln_w_rep, a["L2_ln_w"]), (k.ln_b_rep, a["L2_ln_b"]),
                              (k.rel_b_rep, a["L3_b"])):
                for t in range(TILES):
                    sp.dma_start(tile[:, t, :], src[0, :].partition_broadcast(P)).then_inc(weights_in, 16)
            for n in range(4):
                sp.dma_start(raw[:, n, :], a["edge_lin"][n, :, :]).then_inc(lists_in, 16)
            sp.dma_start(row_lists[:, :, :], a["edge_rows"][:, :, :]).then_inc(lists_in, 16)
            sp.wait_ge(zero_ready, 1)
            sp.dma_start(scratch["agg"].rearrange("(p r) d -> p (r d)", p=P).rearrange("p (s c) -> p s c", c=ROWS),
                         zero[:, :].unsqueeze(1).broadcast_to([P, S, ROWS])).then_inc(stored, 16)
            sp.dma_start(scratch["sum"][size.rows:size.rows + ROWS, :].rearrange("(p r) d -> p (r d)", p=P),
                         zero[:, :]).then_inc(stored, 16)
            sp.wait_ge(tables_done, 1)
            sp.dma_start(scratch["col_tab"], col_tab[:, :, :]).then_inc(stored, 16)
            sp.dma_start(scratch["row_tab"], row_tab[:, :, :]).then_inc(stored, 16)
            sp.wait_ge(stored, 4 * 16)
            sp.wait_ge(weights_in, 16 * (21 + 4 * TILES))

        @block.gpsimd
        def _(pool):
            pool.memset(zero[:, :], 0.0).then_inc(zero_ready, 1)
            pool.memset(k.ident[:, :], 0.0).then_inc(consts, 1)
            pool.wait_ge(consts, 1)
            pool.affine_select(out=k.ident[:, :], in_=k.ident[:, :], compare_op=ALU.not_equal, fill=1.0, base=0,
                               pattern=[[-1, P]], channel_multiplier=1).then_inc(consts, 1)
            pool.memset(k.ones_row[:, :], 1.0).then_inc(consts, 1)
            pool.memset(k.eps[:, :], EPS).then_inc(consts, 1)
            pool.memset(k.tiny[:, :], 1e-16).then_inc(consts, 1)
            pool.iota(offset_i[:, :, :], [[-HEAD_DIM, HEADS], [0, HEAD_DIM]], base=0, channel_multiplier=1
                      ).then_inc(consts, 1)
            pool.iota(place_i[:, :], [[P, TILES]], base=1, channel_multiplier=1).then_inc(consts, 1)
            pool.iota(place_row_i[:, :], [[1, ROWS]], base=1, channel_multiplier=0).then_inc(consts, 1)
            pool.iota(edge_i[:, :], [[1, ROWS]], base=0, channel_multiplier=ROWS).then_inc(consts, 1)

        @block.tensor
        def _(pe):
            pe.wait_ge(weights_in, 16 * (21 + 4 * TILES))
            pe.wait_ge(consts, 9)
            pe.matmul(ps_a[:, 0, :], w_center_t[:, :], w_cat_node[:, :], start=True, stop=True).then_inc(flipped, 1)
            for n in range(2):
                pe.wait_ge(rel_sums_ready, 2 * n + 1)
                pe.transpose(ps_a[0:32, 1, 0:S], totals[:, n, :], k.ident[0:S, 0:S]).then_inc(flipped, 1)
                if n == 1:
                    pe.transpose(ps_a[0:32, 2, 0:S], totals[:, 2, :], k.ident[0:S, 0:S]).then_inc(flipped, 1)
                pe.wait_ge(rel_sums_ready, 2 * n + 2)
                if n == 0:
                    pe.transpose(ps_b[0:S, 0, 0:32], carried[:, 0, 0:S], k.ident[0:32, 0:32]).then_inc(flipped, 1)
                else:
                    pe.transpose(ps_b[0:S, 1, 0:32], carried[:, 1, 0:S], k.ident[0:32, 0:32]).then_inc(flipped, 1)
                    pe.transpose(ps_b[0:S, 2, 0:32], carried[:, 2, 1:S + 1], k.ident[0:32, 0:32]).then_inc(flipped, 1)
            pe.wait_ge(rel_sums_ready, 5)
            for t in range(TILES):
                pe.transpose(ps_a[:, t, 0:S], inv_deg[:, t * P:(t + 1) * P], k.ident[0:S, 0:S])
                last_one = pe.transpose(ps_b[:, t, 0:S], inv_rel[:, t * P:(t + 1) * P], k.ident[0:S, 0:S])
            last_one.then_inc(flipped, 1)

        @block.vector
        def _(dve):
            count = [0]

            def done(ins):
                count[0] += 1
                ins.then_inc(chain, 1)
                dve.wait_ge(chain, count[0])

            dve.wait_ge(consts, 9)
            dve.wait_ge(weights_in, 16 * (21 + 4 * TILES))
            dve.tensor_tensor(k.w2_plus_one[:, :], w2[:, :], k.ident[:, :], ALU.add)
            dve.tensor_copy(k.place[:, :], place_i[:, :])
            dve.tensor_scalar(k.dump_row[:, :], place_i[:, :], float(size.rows - 1), None, ALU.add)
            dve.tensor_copy(k.place_row[:, :], place_row_i[:, :])
            dve.tensor_copy(edge_at[:, :], edge_i[:, :])
            dve.memset(totals[:, :, :], 0.0)
            dve.memset(none[:, :], 0.0)
            dve.memset(carried[:, :, :], 0.0)
            done(dve.tensor_scalar(at_least[:, :], flat(offset_i), 0.0, HEAD_DIM ** -0.5, ALU.is_ge, ALU.mult))
            dve.scalar_tensor_tensor(k.heads[:, :], flat(offset_i), float(HEAD_DIM), at_least[:, :],
                                     ALU.is_lt, ALU.mult)
            dve.wait_ge(flipped, 1)
            dve.tensor_copy(k.w_center_cat[:, :], ps_a[:, 0, :])

            dve.wait_ge(lists_in, 5 * 16)
            dve.tensor_tensor(first[:, :], raw[:, 0, :], raw[:, 1, :], ALU.not_equal)
            dve.tensor_tensor(last[:, :], raw[:, 0, :], raw[:, 2, :], ALU.not_equal)
            done(dve.tensor_copy(col_tab[:, 1, :], raw[:, 3, :]))
            dve.tensor_scalar(col_tab[:, 0, :], first[:, :], -1.0, 1.0, ALU.mult, ALU.add)
            dve.tensor_scalar(col_tab[:, 2, :], first[:, :], -LOW, None, ALU.mult)
            scat = row_tab[:, :, 0:TILES]
            there = row_lists[:, 0, :].rearrange("p (s t) -> p s t", t=TILES)
            nxt = row_lists[:, 1, :].rearrange("p (s t) -> p s t", t=TILES)
            done(dve.tensor_tensor(scat, there, nxt, ALU.is_equal))
            done(dve.scalar_tensor_tensor(scat, scat, FAR, there, ALU.mult, ALU.add))
            done(dve.tensor_tensor(work[:, :], first[:, :], edge_at[:, :], ALU.mult))
            done(dve.tensor_tensor_scan(inv_deg[:, :], work[:, :], work[:, :], 0.0, ALU.max, ALU.max))
            done(dve.tensor_copy(totals[:, 0, RELS:RELS + 1], inv_deg[:, ROWS - 1:ROWS]))
            for r in range(RELS):
                done(dve.tensor_scalar(work[:, :], raw[:, 3, :], float(r), None, ALU.is_equal))
                done(dve.tensor_tensor_scan(counts[:, r, :], work[:, :], none[:, :], 0.0, ALU.add, ALU.add))
                done(dve.tensor_copy(totals[:, 0, r:r + 1], counts[:, r, ROWS - 1:ROWS]))
            dve.sem_inc(rel_sums_ready, 1)
            dve.wait_ge(flipped, 2)
            done(dve.tensor_copy(totals_t[:, 0:S], ps_a[0:32, 1, 0:S]))
            done(dve.tensor_tensor_scan(carried[:, 0, 1:S], totals_t[:, 0:S - 1], carried[:, 2, 0:S - 1], 0.0,
                                        ALU.add, ALU.add))
            dve.sem_inc(rel_sums_ready, 1)
            dve.wait_ge(flipped, 3)
            done(dve.tensor_copy(carry[:, 0, :], ps_b[0:S, 0, 0:32]))
            for r in range(RELS):
                done(dve.tensor_scalar(counts[:, r, :], counts[:, r, :], carry[:, 0, r:r + 1], None, ALU.add))
                done(dve.tensor_scalar(one_rel[:, :], raw[:, 3, :], float(r), None, ALU.is_equal))
                done(dve.tensor_tensor(work[:, :], counts[:, r, :], one_rel[:, :], ALU.subtract))
                done(dve.tensor_tensor(work[:, :], work[:, :], first[:, :], ALU.mult))
                done(dve.tensor_tensor_scan(starts[:, r, :], work[:, :], work[:, :], 0.0, ALU.max, ALU.max))
                done(dve.tensor_copy(totals[:, 1, r:r + 1], starts[:, r, ROWS - 1:ROWS]))
                done(dve.scalar_tensor_tensor(work[:, :], counts[:, r, :], -FAR, last[:, :], ALU.add, ALU.mult))
                done(dve.tensor_tensor_scan(ends[:, r, ::-1], work[:, ::-1], work[:, ::-1], 0.0, ALU.min, ALU.min))
                done(dve.tensor_copy(totals[:, 2, r:r + 1], ends[:, r, 0:1]))
            done(dve.tensor_copy(totals[:, 1, RELS:RELS + 1], totals[:, 0, RELS:RELS + 1]))
            dve.sem_inc(rel_sums_ready, 1)
            dve.wait_ge(flipped, 5)
            done(dve.tensor_copy(totals_t[:, 0:S], ps_a[0:32, 1, 0:S]))
            done(dve.tensor_tensor_scan(carried[:, 1, 1:S], totals_t[:, 0:S - 1], totals_t[:, 0:S - 1], 0.0,
                                        ALU.max, ALU.max))
            done(dve.tensor_copy(totals_t[:, 0:S], ps_a[0:32, 2, 0:S]))
            done(dve.tensor_tensor_scan(carried[:, 2, 1:S][:, ::-1], totals_t[:, 1:S][:, ::-1],
                                        totals_t[:, 1:S][:, ::-1], 0.0, ALU.min, ALU.min))
            dve.sem_inc(rel_sums_ready, 1)
            dve.wait_ge(flipped, 7)
            done(dve.tensor_copy(carry[:, 1:3, :], ps_b[0:S, 1:3, 0:32]))
            done(dve.memset(inv_rel[:, :], 0.0))
            for r in range(RELS):
                done(dve.tensor_scalar(work[:, :], starts[:, r, :], carry[:, 1, r:r + 1], None, ALU.max))
                done(dve.scalar_tensor_tensor(work2[:, :], ends[:, r, :], carry[:, 2, r:r + 1], work[:, :],
                                              ALU.min, ALU.subtract))
                done(dve.tensor_scalar(work2[:, :], work2[:, :], FAR, None, ALU.add))
                done(dve.tensor_scalar(one_rel[:, :], raw[:, 3, :], float(r), None, ALU.is_equal))
                done(dve.tensor_tensor(work2[:, :], work2[:, :], one_rel[:, :], ALU.mult))
                done(dve.tensor_tensor(inv_rel[:, :], inv_rel[:, :], work2[:, :], ALU.add))
            done(dve.reciprocal(inv_rel[:, :], inv_rel[:, :]))
            done(dve.tensor_scalar(inv_deg[:, :], inv_deg[:, :], carry[:, 1, RELS:RELS + 1], None, ALU.max))
            done(dve.scalar_tensor_tensor(inv_deg[:, :], edge_at[:, :], 1.0, inv_deg[:, :], ALU.add, ALU.subtract))
            done(dve.reciprocal(inv_deg[:, :], inv_deg[:, :]))
            dve.sem_inc(rel_sums_ready, 1)
            dve.wait_ge(flipped, 8)
            for t in range(TILES):
                dve.tensor_copy(row_tab[:, :, 4 + t].bitcast(F32), ps_a[:, t, 0:S])
                end = dve.tensor_copy(row_tab[:, :, 8 + t].bitcast(F32), ps_b[:, t, 0:S])
            done(end)
            dve.sem_inc(tables_done, 1)


def gather(pool, tile, table, idx, col, sem):
    for t in range(TILES):
        pool.indirect_dma_start(out=tile[:, t, :], out_offset=None, in_=table,
                                in_offset=bass.IndirectOffsetOnAxis(ap=idx[:, col + t:col + t + 1], axis=0)
                                ).then_inc(sem, 16)


def scatter(pool, table, tile, idx, bound, sem):
    for t in range(TILES):
        pool.indirect_dma_start(out=table, out_offset=bass.IndirectOffsetOnAxis(ap=idx[:, t:t + 1], axis=0),
                                in_=tile[:, t, :], in_offset=None, bounds_check=bound,
                                oob_is_err=False).then_inc(sem, 16)


def mean_edges(nc, size, a, scratch, k):
    S = size.steps
    with Phase(nc, "e0") as ph:
        idx, idx_in = ph.loaded("idx", [P, 2 * TILES], I32)
        edge, edge_in = ph.loaded("edge", [D, ROWS])
        col, col_in = ph.loaded("col", [1, 3, ROWS], BF16)
        row, row_in = ph.loaded("row", [P, 3 * TILES], I32)
        x, x_in = ph.loaded("x", [P, TILES, D])
        h, h_ready = ph.made("h", [P, TILES, D])
        ht, ht_ready = ph.made("ht", [D, TILES, P])
        msg, msg_ready = ph.made("msg", [D, ROWS])
        run, run_ready = ph.made("run", [D, ROWS])
        res, res_ready = ph.made("res", [P, TILES, D], 4)
        scattered = ph.dma_sems("scattered")
        pool_turn = ph.sem("pool_turn")
        turned, msg_done = ph.sem("turned"), ph.sem("msg_done")
        keep_done, out_done = ph.sem("keep_done"), ph.sem("out_done")
        norm = Norm(ph, "norm")
        ps_t, ps_m, ps_k, ps_r = ph.banks("t"), ph.banks("m"), ph.banks("k"), ph.banks("r")
        block = ph.ctx.enter_context(nc.Block())

        @block.sync
        def _(sp):
            def body(i, u):
                if live(i, S):
                    if begun(i - 4):
                        sp.wait_ge(at(x_in, u), moved(i - 4, u, TILES))
                    sp.dma_start(at(idx, u)[:, :], idx_of(a, i)).then_inc(at(idx_in, u), 16)
                    if begun(i - 4):
                        sp.wait_ge(msg_done, i - 3)
                    sp.dma_start(at(edge, u)[:, :], cols_of(a["edge128T"], i)).then_inc(at(edge_in, u), 16)
                    if begun(i - 4):
                        sp.wait_ge(keep_done, i - 3)
                    sp.dma_start(flat(at(col, u)), col_values_of(scratch, i)).then_inc(at(col_in, u), 16)
                j = i - 1
                if live(j, S):
                    if begun(j - 4):
                        sp.wait_ge(at(scattered, u - 1), moved(j - 4, u - 1, TILES))
                    sp.dma_start(at(row, u - 1)[:, :], row_values_of(scratch, j)).then_inc(at(row_in, u - 1), 16)
            run_steps(sp, body, S, 1)

        @block.gpsimd
        def _(pool):
            def body(i, u):
                if live(i, S):
                    pool.wait_ge(at(idx_in, u), moved(i, u))
                    if begun(i - 4):
                        pool.wait_ge(h_ready, i - 3)
                    pool.sem_inc(pool_turn, 1)
                    gather(pool, at(x, u), a["x"], at(idx, u), 0, at(x_in, u))
                j = i - 4
                if live(j, S):
                    pool.wait_ge(res_ready, j + 1)
                    pool.sem_inc(pool_turn, 1)
                    scatter(pool, scratch["agg"], at(res, u), at(row, u), size.rows - 1, at(scattered, u))
            run_steps(pool, body, S, 4)
            for u in range(SLOTS):
                pool.wait_ge(scattered[u], all_moved(S, u, TILES))

        @block.vector
        def _(dve):
            def body(i, u):
                if live(i, S):
                    dve.wait_ge(at(x_in, u), moved(i, u, TILES))
                    norm.moments_of(dve, at(x, u), i, u)
                j = i - 2
                if live(j, S):
                    dve.wait_ge(out_done, j + 1)
                    dve.wait_ge(at(row_in, u - 2), moved(j, u - 2))
                    if begun(j - 4):
                        dve.wait_ge(at(scattered, u - 2), moved(j - 4, u - 2, TILES))
                    dve.tensor_tensor(at(res, u - 2)[:, :, :], at(ps_r, u)[:, :, :],
                                      spread(at(row, u - 2)[:, TILES:2 * TILES].bitcast(F32), D), ALU.mult
                                      ).then_inc(res_ready, 1)
                if live(i, S):
                    norm.scale_of(dve, i, u, h_ready)
                j = i - 1
                if live(j, S):
                    dve.wait_ge(msg_ready, j + 1)
                    dve.wait_ge(keep_done, j + 1)
                    if begun(j - 2):
                        dve.wait_ge(out_done, j - 1)
                    if begun(j - 1):
                        dve.wait_ge(run_ready, j)
                    before = 0.0 if isinstance(j, int) and j == 0 else at(run, u)[:, ROWS - 1:ROWS]
                    dve.tensor_tensor_scan(at(run, u - 1)[:, :], flat(at(ps_k, u - 1)), at(msg, u - 1)[:, :], before,
                                           ALU.mult, ALU.add).then_inc(run_ready, 1)
            run_steps(dve, body, S, 2)

        @block.scalar
        def _(act):
            def body(i, u):
                j = i - 1
                if live(j, S):
                    act.wait_ge(msg_done, j + 1)
                    if begun(j - 2):
                        act.wait_ge(run_ready, j - 1)
                    act.activation(at(msg, u - 1)[:, :], flat(at(ps_m, u - 1)), ACT.Identity, bias=k.b1[:, :]
                                   ).then_inc(msg_ready, 1)
                if live(i, S):
                    norm.std_of(act, k, i, u)
                    if begun(i - 2):
                        act.wait_ge(turned, i - 1)
                    norm.apply(act, at(h, u), at(x, u), ACT.Relu, i, u).then_inc(h_ready, 1)
                    act.wait_ge(turned, i + 1)
                    if begun(i - 2):
                        act.wait_ge(msg_done, i - 1)
                    act.activation(at(ht, u)[:, :, :], at(ps_t, u)[:, :, :], ACT.Copy).then_inc(ht_ready, 1)
            run_steps(act, body, S, 1)

        @block.tensor
        def _(pe):
            def body(i, u):
                j = i - 2
                if live(j, S):
                    pe.wait_ge(run_ready, j + 1)
                    if begun(j - 2):
                        pe.wait_ge(res_ready, j - 1)
                    for t in range(TILES):
                        ins = pe.matmul(at(ps_r, u)[:, t, :], at(run, u)[:, t * P:(t + 1) * P], k.w2_plus_one[:, :],
                                        start=True, stop=True)
                    ins.then_inc(out_done, 1)
                j = i - 1
                if live(j, S):
                    pe.wait_ge(at(edge_in, u - 1), moved(j, u - 1))
                    if begun(j - 2):
                        pe.wait_ge(msg_ready, j - 1)
                    pe.matmul(flat(at(ps_m, u - 1)), k.w1_edge[:, :], at(edge, u - 1)[:, :], start=True, stop=False)
                    pe.wait_ge(ht_ready, j + 1)
                    pe.matmul(flat(at(ps_m, u - 1)), k.w1_node[:, :], flat(at(ht, u - 1)), start=False, stop=True
                              ).then_inc(msg_done, 1)
                    pe.wait_ge(at(col_in, u - 1), moved(j, u - 1))
                    if begun(j - 2):
                        pe.wait_ge(run_ready, j - 1)
                    pe.matmul(flat(at(ps_k, u - 1)), k.ones_row[:, :], at(col, u - 1)[:, 0, :], start=True, stop=True
                              ).then_inc(keep_done, 1)
                if live(i, S):
                    pe.wait_ge(h_ready, i + 1)
                    if begun(i - 2):
                        pe.wait_ge(ht_ready, i - 1)
                    for t in range(TILES):
                        ins = pe.transpose(at(ps_t, u)[:, t, :], at(h, u)[:, t, :], k.ident[:, :])
                    ins.then_inc(turned, 1)
            run_steps(pe, body, S, 2)


def mean_nodes(nc, size, a, scratch, k):
    S = size.steps
    with Phase(nc, "n0") as ph:
        x, x_in = ph.loaded("x", [P, TILES, D])
        agg, agg_in = ph.loaded("agg", [P, TILES, D])
        biased, biased_ready = ph.made("biased", [P, TILES, D], 4)
        leaky, leaky_ready = ph.made("leaky", [P, TILES, D])
        x1, x1_ready = ph.made("x1", [P, TILES, D], 4)
        h1, h1_ready = ph.made("h1", [P, TILES, D], 4)
        x1_out, h1_out = ph.dma_sems("x1_out"), ph.dma_sems("h1_out")
        pool_turn = ph.sem("pool_turn")
        norm = Norm(ph, "norm")
        block = ph.ctx.enter_context(nc.Block())

        @block.sync
        def _(sp):
            def body(i, u):
                if live(i, S):
                    if begun(i - 4):
                        sp.wait_ge(biased_ready, i - 3)
                    sp.dma_start(flat(at(agg, u)), rows_of(scratch["agg"], i)).then_inc(at(agg_in, u), 16)
                    if begun(i - 4):
                        sp.wait_ge(x1_ready, i - 3)
                    sp.dma_start(flat(at(x, u)), rows_of(a["x"], i)).then_inc(at(x_in, u), 16)
            run_steps(sp, body, S, 0)

        @block.gpsimd
        def _(pool):
            def body(i, u):
                if live(i, S):
                    pool.wait_ge(at(agg_in, u), moved(i, u))
                    if begun(i - 4):
                        pool.wait_ge(leaky_ready, i - 3)
                    pool.sem_inc(pool_turn, 1)
                    pool.tensor_tensor(at(biased, u)[:, :, :], at(agg, u)[:, :, :], k.b2_rep[:, :, :], ALU.add
                                       ).then_inc(biased_ready, 1)
            run_steps(pool, body, S, 0)

        @block.vector
        def _(dve):
            def body(i, u):
                if live(i, S):
                    dve.wait_ge(biased_ready, i + 1)
                    if begun(i - 2):
                        dve.wait_ge(x1_ready, i - 1)
                    dve.scalar_tensor_tensor(at(leaky, u)[:, :, :], at(biased, u)[:, :, :], SLOPE,
                                             at(biased, u)[:, :, :], ALU.mult, ALU.max).then_inc(leaky_ready, 1)
                if live(i - 1, S):
                    norm.scale_of(dve, i - 1, u - 1, h1_ready)
                if live(i, S):
                    dve.wait_ge(leaky_ready, i + 1)
                    dve.wait_ge(at(x_in, u), moved(i, u))
                    if begun(i - 4):
                        dve.wait_ge(at(x1_out, u), moved(i - 4, u))
                    if begun(i - 4):
                        dve.wait_ge(h1_ready, i - 3)
                    dve.tensor_tensor(at(x1, u)[:, :, :], at(leaky, u)[:, :, :], at(x, u)[:, :, :], ALU.add
                                      ).then_inc(x1_ready, 1)
                    dve.wait_ge(x1_ready, i + 1)
                    norm.moments_of(dve, at(x1, u), i, u)
            run_steps(dve, body, S, 1)

        @block.scalar
        def _(act):
            def body(i, u):
                j = i - 1
                if live(j, S):
                    if begun(j - 4):
                        act.wait_ge(at(h1_out, u - 1), moved(j - 4, u - 1))
                    norm.apply(act, at(h1, u - 1), at(x1, u - 1), ACT.Relu, j, u - 1).then_inc(h1_ready, 1)
                    act.wait_ge(x1_ready, j + 1)
                    act.dma_start(rows_of(scratch["x1"], j), flat(at(x1, u - 1))).then_inc(at(x1_out, u - 1), 16)
                if live(i, S):
                    norm.std_of(act, k, i, u)
                if live(i - 2, S):
                    act.wait_ge(h1_ready, i - 1)
                    act.dma_start(rows_of(scratch["h1"], i - 2), flat(at(h1, u - 2))).then_inc(at(h1_out, u - 2), 16)
            run_steps(act, body, S, 2)
            for u in range(SLOTS):
                act.wait_ge(x1_out[u], all_moved(S, u))
            for u in range(SLOTS):
                act.wait_ge(h1_out[u], all_moved(S, u))


def attention_edges(nc, size, a, scratch, k):
    S = size.steps
    with Phase(nc, "e1") as ph:
        idx, idx_in = ph.loaded("idx", [P, 2 * TILES], I32)
        col, col_in = ph.loaded("col", [1, 3, ROWS], BF16)
        row, row_in = ph.loaded("row", [P, 3 * TILES], I32)
        hs, hs_in = ph.loaded("hs", [P, TILES, D])
        hd, hd_in = ph.loaded("hd", [P, TILES, D])
        hst, hst_ready = ph.made("hst", [D, ROWS])
        hdt, hdt_ready = ph.made("hdt", [D, ROWS])
        kq, kq_ready = ph.made("kq", [D, ROWS])
        v, v_ready = ph.made("v", [D, ROWS], 4)
        drop, drop_ready = ph.made("drop", [D, ROWS])
        top, top_ready = ph.made("top", [D, ROWS + 1])
        fall, fall_ready = ph.made("fall", [D, ROWS])
        arg, arg_ready = ph.made("arg", [D, 2, ROWS])
        ex, ex_ready = ph.made("ex", [D, 2, ROWS])
        den, den_ready = ph.made("den", [D, ROWS])
        safe_den, safe_ready = ph.made("safe_den", [D, ROWS])
        inv_den, inv_ready = ph.made("inv_den", [D, ROWS])
        pv, pv_ready = ph.made("pv", [D, ROWS])
        run, run_ready = ph.made("run", [D, ROWS])
        att, att_ready = ph.made("att", [D, ROWS])
        res, res_ready = ph.made("res", [P, TILES, D], 4)
        scattered = ph.dma_sems("scattered")
        pool_turn, top_carried = ph.sem("pool_turn"), ph.sem("top_carried")
        hs_turned, hd_turned, drop_spread = ph.sem("hs_turned"), ph.sem("hd_turned"), ph.sem("drop_spread")
        k_done, v_done, score_done, out_done = (ph.sem(n) for n in ("k_done", "v_done", "score_done", "out_done"))
        ps_hs, ps_hd, ps_k, ps_v, ps_r, ps_f = (ph.ps(n) for n in ("hs", "hd", "k", "v", "r", "f"))
        ps_s = ph.banks("s")
        block = ph.ctx.enter_context(nc.Block())

        @block.sync
        def _(sp):
            def body(i, u):
                if live(i, S):
                    if begun(i - 4):
                        sp.wait_ge(at(hs_in, u), moved(i - 4, u, TILES))
                    if begun(i - 4):
                        sp.wait_ge(at(hd_in, u), moved(i - 4, u, TILES))
                    sp.dma_start(at(idx, u)[:, :], idx_of(a, i)).then_inc(at(idx_in, u), 16)
                    if begun(i - 4):
                        sp.wait_ge(drop_spread, i - 3)
                    sp.dma_start(flat(at(col, u)), col_values_of(scratch, i)).then_inc(at(col_in, u), 16)
                j = i - 3
                if live(j, S):
                    if begun(j - 4):
                        sp.wait_ge(at(scattered, u - 3), moved(j - 4, u - 3, TILES))
                    sp.dma_start(at(row, u - 3)[:, :], row_values_of(scratch, j)).then_inc(at(row_in, u - 3), 16)
            run_steps(sp, body, S, 3)

        @block.gpsimd
        def _(pool):
            def body(i, u):
                if live(i, S):
                    pool.wait_ge(at(idx_in, u), moved(i, u))
                    if begun(i - 4):
                        pool.wait_ge(hs_turned, i - 3)
                    pool.sem_inc(pool_turn, 1)
                    gather(pool, at(hs, u), scratch["h1"], at(idx, u), 0, at(hs_in, u))
                    if begun(i - 4):
                        pool.wait_ge(hd_turned, i - 3)
                    pool.sem_inc(pool_turn, 1)
                    gather(pool, at(hd, u), scratch["h1"], at(idx, u), TILES, at(hd_in, u))
                j = i - 5
                if live(j, S):
                    pool.wait_ge(at(row_in, u - 5), moved(j, u - 5))
                    pool.wait_ge(res_ready, j + 1)
                    pool.sem_inc(pool_turn, 1)
                    scatter(pool, scratch["agg"], at(res, u - 5), at(row, u - 5), size.rows - 1, at(scattered, u - 5))
            run_steps(pool, body, S, 5)
            for u in range(SLOTS):
                pool.wait_ge(scattered[u], all_moved(S, u, TILES))

        @block.vector
        def _(dve):
            dve.memset(top[0][:, 0:1], 0.0).then_inc(top_carried, 1)

            def body(i, u):
                j = i - 3
                if live(j, S):
                    dve.wait_ge(safe_ready, j + 1)
                    if begun(j - 2):
                        dve.wait_ge(att_ready, j - 1)
                    dve.reciprocal(at(inv_den, u - 3)[:, :], at(safe_den, u - 3)[:, :]).then_inc(inv_ready, 1)
                    dve.wait_ge(inv_ready, j + 1)
                    dve.wait_ge(run_ready, j + 1)
                    if begun(j - 2):
                        dve.wait_ge(out_done, j - 1)
                    dve.tensor_tensor(at(att, u - 3)[:, :], at(run, u - 3)[:, :], at(inv_den, u - 3)[:, :], ALU.mult
                                      ).then_inc(att_ready, 1)
                j = i - 1
                if live(j, S):
                    now, s = at(top, u - 1), flat(at(ps_s, u - 1))
                    if begun(j - 1):
                        dve.wait_ge(arg_ready, j)
                    if isinstance(j, int) and j == 0:
                        before = 0.0
                    else:
                        before = at(top, u)[:, ROWS:ROWS + 1]
                        dve.tensor_copy(now[:, 0:1], before).then_inc(top_carried, 1)
                    dve.wait_ge(top_carried, j + 1)
                    dve.wait_ge(score_done, j + 1)
                    dve.wait_ge(drop_ready, j + 1)
                    dve.tensor_tensor_scan(now[:, 1:ROWS + 1], at(drop, u - 1)[:, :], s, before, ALU.add, ALU.max
                                           ).then_inc(top_ready, 1)
                    dve.wait_ge(top_ready, j + 1)
                    if begun(j - 2):
                        dve.wait_ge(ex_ready, j - 1)
                    dve.tensor_tensor(at(fall, u - 1)[:, :], now[:, 0:ROWS], now[:, 1:ROWS + 1], ALU.subtract
                                      ).then_inc(fall_ready, 1)
                    dve.tensor_tensor(at(arg, u - 1)[:, 0, :], s, now[:, 1:ROWS + 1], ALU.subtract)
                    dve.wait_ge(fall_ready, j + 1)
                    dve.tensor_tensor(at(arg, u - 1)[:, 1, :], at(fall, u - 1)[:, :], at(drop, u - 1)[:, :], ALU.add
                                      ).then_inc(arg_ready, 1)
                j = i - 2
                if live(j, S):
                    e = at(ex, u)
                    dve.wait_ge(ex_ready, j + 1)
                    if begun(j - 2):
                        dve.wait_ge(safe_ready, j - 1)
                    if begun(j - 1):
                        dve.wait_ge(den_ready, j)
                    start = isinstance(j, int) and j == 0
                    dve.tensor_tensor_scan(at(den, u)[:, :], e[:, 1, :], e[:, 0, :],
                                           0.0 if start else at(den, u - 1)[:, ROWS - 1:ROWS], ALU.mult, ALU.add
                                           ).then_inc(den_ready, 1)
                    dve.wait_ge(v_ready, j + 1)
                    dve.tensor_tensor(at(pv, u)[:, :], at(v, u - 2)[:, :], e[:, 0, :], ALU.mult).then_inc(pv_ready, 1)
                    dve.wait_ge(pv_ready, j + 1)
                    if begun(j - 2):
                        dve.wait_ge(att_ready, j - 1)
                    if begun(j - 1):
                        dve.wait_ge(run_ready, j)
                    dve.tensor_tensor_scan(at(run, u)[:, :], e[:, 1, :], at(pv, u)[:, :],
                                           0.0 if start else at(run, u - 1)[:, ROWS - 1:ROWS], ALU.mult, ALU.add
                                           ).then_inc(run_ready, 1)
                if live(i, S):
                    dve.wait_ge(k_done, i + 1)
                    dve.wait_ge(hdt_ready, i + 1)
                    if begun(i - 2):
                        dve.wait_ge(score_done, i - 1)
                    dve.scalar_tensor_tensor(at(kq, u)[:, :], flat(ps_k), k.bk[:, :], at(hdt, u)[:, :], ALU.add,
                                             ALU.mult).then_inc(kq_ready, 1)
            run_steps(dve, body, S, 3)

        @block.scalar
        def _(act):
            def body(i, u):
                j = i - 4
                if live(j, S):
                    act.wait_ge(out_done, j + 1)
                    if begun(j - 4):
                        act.wait_ge(at(scattered, u - 4), moved(j - 4, u - 4, TILES))
                    act.activation(at(res, u - 4)[:, :, :], ps_r[:, :, :], ACT.Copy).then_inc(res_ready, 1)
                if live(i, S):
                    act.wait_ge(hs_turned, i + 1)
                    if begun(i - 2):
                        act.wait_ge(v_done, i - 1)
                    act.activation(at(hst, u)[:, :], flat(ps_hs), ACT.Copy).then_inc(hst_ready, 1)
                    act.wait_ge(hd_turned, i + 1)
                    if begun(i - 2):
                        act.wait_ge(kq_ready, i - 1)
                    act.activation(at(hdt, u)[:, :], flat(ps_hd), ACT.Copy).then_inc(hdt_ready, 1)
                    act.wait_ge(drop_spread, i + 1)
                    if begun(i - 2):
                        act.wait_ge(arg_ready, i - 1)
                    act.activation(at(drop, u)[:, :], flat(ps_f), ACT.Copy).then_inc(drop_ready, 1)
                    act.wait_ge(v_done, i + 1)
                    if begun(i - 4):
                        act.wait_ge(pv_ready, i - 3)
                    act.activation(at(v, u)[:, :], flat(ps_v), ACT.Identity, bias=k.bv[:, :]).then_inc(v_ready, 1)
                j = i - 1
                if live(j, S):
                    act.wait_ge(arg_ready, j + 1)
                    if begun(j - 2):
                        act.wait_ge(run_ready, j - 1)
                    act.activation(at(ex, u - 1)[:, :, :], at(arg, u - 1)[:, :, :], ACT.Exp).then_inc(ex_ready, 1)
                j = i - 2
                if live(j, S):
                    act.wait_ge(den_ready, j + 1)
                    if begun(j - 2):
                        act.wait_ge(inv_ready, j - 1)
                    act.activation(at(safe_den, u)[:, :], at(den, u)[:, :], ACT.Identity, bias=k.tiny[:, :]
                                   ).then_inc(safe_ready, 1)
            run_steps(act, body, S, 4)

        @block.tensor
        def _(pe):
            def body(i, u):
                j = i - 1
                if live(j, S):
                    pe.wait_ge(kq_ready, j + 1)
                    if begun(j - 2):
                        pe.wait_ge(arg_ready, j - 1)
                    pe.matmul(flat(at(ps_s, u - 1)), k.heads[:, :], at(kq, u - 1)[:, :], start=True, stop=True
                              ).then_inc(score_done, 1)
                if live(i, S):
                    pe.wait_ge(at(hs_in, u), moved(i, u, TILES))
                    if begun(i - 1):
                        pe.wait_ge(hst_ready, i)
                    for t in range(TILES):
                        ins = pe.transpose(ps_hs[:, t, :], at(hs, u)[:, t, :], k.ident[:, :])
                    ins.then_inc(hs_turned, 1)
                    pe.wait_ge(at(hd_in, u), moved(i, u, TILES))
                    if begun(i - 1):
                        pe.wait_ge(hdt_ready, i)
                    for t in range(TILES):
                        ins = pe.transpose(ps_hd[:, t, :], at(hd, u)[:, t, :], k.ident[:, :])
                    ins.then_inc(hd_turned, 1)
                    pe.wait_ge(at(col_in, u), moved(i, u))
                    if begun(i - 1):
                        pe.wait_ge(drop_ready, i)
                    pe.matmul(flat(ps_f), k.ones_row[:, :], at(col, u)[:, 2, :], start=True, stop=True
                              ).then_inc(drop_spread, 1)
                j = i - 3
                if live(j, S):
                    pe.wait_ge(att_ready, j + 1)
                    if begun(j - 1):
                        pe.wait_ge(res_ready, j)
                    for t in range(TILES):
                        ins = pe.matmul(ps_r[:, t, :], at(att, u - 3)[:, t * P:(t + 1) * P], k.wo[:, :], start=True,
                                        stop=True)
                    ins.then_inc(out_done, 1)
                if live(i, S):
                    pe.wait_ge(hst_ready, i + 1)
                    if begun(i - 1):
                        pe.wait_ge(kq_ready, i)
                    pe.matmul(flat(ps_k), k.wk[:, :], at(hst, u)[:, :], start=True, stop=True).then_inc(k_done, 1)
                    if begun(i - 1):
                        pe.wait_ge(v_ready, i)
                    pe.matmul(flat(ps_v), k.wv[:, :], at(hst, u)[:, :], start=True, stop=True).then_inc(v_done, 1)
            run_steps(pe, body, S, 3)


def valid_columns(size, tile, i):
    if not isinstance(i, int) or (i + 1) * ROWS <= size.nodes:
        return tile[:, :, :]
    per = (size.nodes - i * ROWS) // TILES
    return tile[:, :, 0:per] if per > 0 else None


def attention_nodes(nc, size, scratch, k):
    S = size.steps
    with Phase(nc, "n1") as ph:
        h1, h1_in = ph.loaded("h1", [P, TILES, D])
        agg, agg_in = ph.loaded("agg", [P, TILES, D])
        total, total_ready = ph.made("total", [P, TILES, D])
        tt, tt_ready = ph.made("tt", [D, TILES, P], 4)
        tt_out = ph.dma_sems("tt_out")
        turned, stats_done = ph.sem("turned"), ph.sem("stats_done")
        ps_t = ph.banks("t")
        block = ph.ctx.enter_context(nc.Block())

        @block.sync
        def _(sp):
            def body(i, u):
                if live(i, S):
                    if begun(i - 4):
                        sp.wait_ge(total_ready, i - 3)
                    sp.dma_start(flat(at(agg, u)), rows_of(scratch["agg"], i)).then_inc(at(agg_in, u), 16)
                    sp.dma_start(flat(at(h1, u)), rows_of(scratch["h1"], i)).then_inc(at(h1_in, u), 16)
            run_steps(sp, body, S, 0)

        @block.vector
        def _(dve):
            def body(i, u):
                if live(i, S):
                    dve.wait_ge(at(agg_in, u), moved(i, u))
                    dve.wait_ge(at(h1_in, u), moved(i, u))
                    if begun(i - 2):
                        dve.wait_ge(turned, i - 1)
                    dve.tensor_tensor(at(total, u)[:, :, :], at(agg, u)[:, :, :], at(h1, u)[:, :, :], ALU.add
                                      ).then_inc(total_ready, 1)
                j = i - 1
                if live(j, S):
                    cols = valid_columns(size, at(tt, u - 1), j)
                    if cols is not None:
                        dve.wait_ge(tt_ready, j + 1)
                        dve.bn_stats(k.bn_stats1[:, bass.ds(j, 1), :].rearrange("p a c -> p (a c)"), cols
                                     ).then_inc(stats_done, 1)
            run_steps(dve, body, S, 1)

        @block.tensor
        def _(pe):
            def body(i, u):
                if live(i, S):
                    pe.wait_ge(total_ready, i + 1)
                    if begun(i - 2):
                        pe.wait_ge(tt_ready, i - 1)
                    for t in range(TILES):
                        ins = pe.transpose(at(ps_t, u)[:, t, :], at(total, u)[:, t, :], k.ident[:, :])
                    ins.then_inc(turned, 1)
            run_steps(pe, body, S, 0)

        @block.scalar
        def _(act):
            def body(i, u):
                if live(i, S):
                    act.wait_ge(turned, i + 1)
                    if begun(i - 4):
                        act.wait_ge(at(tt_out, u), moved(i - 4, u))
                    if begun(i - 4):
                        act.wait_ge(stats_done, i - 3)
                    act.activation(at(tt, u)[:, :, :], at(ps_t, u)[:, :, :], ACT.Identity, bias=k.bo[:, :]
                                   ).then_inc(tt_ready, 1)
                j = i - 1
                if live(j, S):
                    act.wait_ge(tt_ready, j + 1)
                    act.dma_start(cols_of(scratch["tt"], j), flat(at(tt, u - 1))).then_inc(at(tt_out, u - 1), 16)
            run_steps(act, body, S, 1)
            for u in range(SLOTS):
                act.wait_ge(tt_out[u], all_moved(S, u))


class BatchNorm:

    def __init__(self, ph, size, stats, gamma_beta, scale, shift):
        self.mv, self.std = ph.sb("bn_mv", [D, 2]), ph.sb("bn_std", [D, 1])
        self.step, self.std_done = ph.sem("bn_step"), ph.sem("bn_std_done")
        self.stats = stats[:, 0:-(-size.nodes // ROWS), :].rearrange("p s c -> p (s c)")
        self.gamma_beta, self.scale, self.shift = gamma_beta, scale, shift

    def vector(self, dve):
        dve.bn_aggr(self.mv[:, :], self.stats).then_inc(self.step, 1)
        dve.wait_ge(self.std_done, 1)
        dve.reciprocal(self.scale[:, :], self.std[:, :]).then_inc(self.step, 1)
        dve.wait_ge(self.step, 2)
        dve.tensor_tensor(self.scale[:, :], self.scale[:, :], self.gamma_beta[:, 0:1], ALU.mult
                          ).then_inc(self.step, 1)
        dve.wait_ge(self.step, 3)
        dve.tensor_tensor(self.shift[:, :], self.mv[:, 0:1], self.scale[:, :], ALU.mult).then_inc(self.step, 1)
        dve.wait_ge(self.step, 4)
        dve.tensor_tensor(self.shift[:, :], self.gamma_beta[:, 1:2], self.shift[:, :], ALU.subtract
                          ).then_inc(self.step, 1)

    def scalar(self, act, k):
        act.wait_ge(self.step, 1)
        act.activation(self.std[:, :], self.mv[:, 1:2], ACT.Sqrt, bias=k.eps[:, :]).then_inc(self.std_done, 1)
        act.wait_ge(self.step, 5)


def feed_forward(nc, size, scratch, k):
    S = size.steps
    with Phase(nc, "ff") as ph:
        tt, tt_in = ph.loaded("tt", [D, ROWS])
        hb, hb_ready = ph.made("hb", [D, TILES, P], 4)
        mid, mid_ready = ph.made("mid", [D, 2, ROWS], 4)
        ut, ut_ready = ph.made("ut", [D, TILES, P], 4)
        ut_out = ph.dma_sems("ut_out")
        up_done, down_done, stats_done = ph.sem("up_done"), ph.sem("down_done"), ph.sem("stats_done")
        bn = BatchNorm(ph, size, k.bn_stats1, k.bn[:, 0:2], k.bn1_scale, k.bn1_shift)
        ps_m = [ph.banks(f"m{n}") for n in range(2)]
        ps_u = ph.banks("u")
        block = ph.ctx.enter_context(nc.Block())

        @block.sync
        def _(sp):
            def body(i, u):
                if live(i, S):
                    if begun(i - 4):
                        sp.wait_ge(hb_ready, i - 3)
                    sp.dma_start(at(tt, u)[:, :], cols_of(scratch["tt"], i)).then_inc(at(tt_in, u), 16)
                j = i - 4
                if live(j, S):
                    sp.wait_ge(ut_ready, j + 1)
                    sp.dma_start(cols_of(scratch["ut"], j), flat(at(ut, u))).then_inc(at(ut_out, u), 16)
            run_steps(sp, body, S, 4)
            for u in range(SLOTS):
                sp.wait_ge(ut_out[u], all_moved(S, u))

        @block.scalar
        def _(act):
            bn.scalar(act, k)

            def body(i, u):
                if live(i, S):
                    act.wait_ge(at(tt_in, u), moved(i, u))
                    if begun(i - 4):
                        act.wait_ge(up_done, i - 3)
                    if begun(i - 4):
                        act.wait_ge(ut_ready, i - 3)
                    act.activation(flat(at(hb, u)), at(tt, u)[:, :], ACT.Identity, bias=k.bn1_shift[:, :],
                                   scale=k.bn1_scale[:, :]).then_inc(hb_ready, 1)
                j = i - 1
                if live(j, S):
                    if begun(j - 4):
                        act.wait_ge(down_done, j - 3)
                    act.wait_ge(up_done, j + 1)
                    for n in range(2):
                        ins = act.activation(at(mid, u - 1)[:, n, :], flat(at(ps_m[n], u - 1)), ACT.Relu,
                                             bias=k.ff_b1[:, n:n + 1])
                    ins.then_inc(mid_ready, 1)
            run_steps(act, body, S, 1)

        @block.tensor
        def _(pe):
            def body(i, u):
                if live(i, S):
                    pe.wait_ge(hb_ready, i + 1)
                    if begun(i - 2):
                        pe.wait_ge(mid_ready, i - 1)
                    for n in range(2):
                        ins = pe.matmul(flat(at(ps_m[n], u)), k.ff1[:, n, :], flat(at(hb, u)), start=True, stop=True)
                    ins.then_inc(up_done, 1)
                j = i - 2
                if live(j, S):
                    pe.wait_ge(mid_ready, j + 1)
                    if begun(j - 2):
                        pe.wait_ge(ut_ready, j - 1)
                    for n in range(2):
                        ins = pe.matmul(flat(at(ps_u, u)), k.ff2[:, n, :], at(mid, u - 2)[:, n, :], start=(n == 0),
                                        stop=(n == 1))
                    ins.then_inc(down_done, 1)
            run_steps(pe, body, S, 2)

        @block.vector
        def _(dve):
            bn.vector(dve)

            def body(i, u):
                j = i - 2
                if live(j, S):
                    dve.wait_ge(down_done, j + 1)
                    if begun(j - 4):
                        dve.wait_ge(at(ut_out, u - 2), moved(j - 4, u - 2))
                    if begun(j - 4):
                        dve.wait_ge(stats_done, j - 3)
                    dve.scalar_tensor_tensor(at(ut, u - 2)[:, :, :], at(ps_u, u)[:, :, :], k.ff_b2[:, :],
                                             at(hb, u - 2)[:, :, :], ALU.add, ALU.add).then_inc(ut_ready, 1)
                    cols = valid_columns(size, at(ut, u - 2), j)
                    if cols is not None:
                        dve.wait_ge(ut_ready, j + 1)
                        dve.bn_stats(k.bn_stats2[:, bass.ds(j, 1), :].rearrange("p a c -> p (a c)"), cols
                                     ).then_inc(stats_done, 1)
            run_steps(dve, body, S, 2)


def second_norm_nodes(nc, size, scratch, k):
    S = size.steps
    with Phase(nc, "n3") as ph:
        ut, ut_in = ph.loaded("ut", [D, ROWS])
        x1, x1_in = ph.loaded("x1", [P, TILES, D])
        vt, vt_ready = ph.made("vt", [D, ROWS])
        x2, x2_ready = ph.made("x2", [P, TILES, D], 4)
        h2, h2_ready = ph.made("h2", [P, TILES, D], 4)
        h2t, h2t_ready = ph.made("h2t", [D, TILES, P])
        own, own_ready = ph.made("own", [P, TILES, D], 4)
        x2_out, h2_out, own_out = ph.dma_sems("x2_out"), ph.dma_sems("h2_out"), ph.dma_sems("own_out")
        turned_back, h2_turned, own_done = ph.sem("turned_back"), ph.sem("h2_turned"), ph.sem("own_done")
        norm = Norm(ph, "norm")
        bn = BatchNorm(ph, size, k.bn_stats2, k.bn[:, 2:4], k.bn2_scale, k.bn2_shift)
        ps_v, ps_h, ps_o = ph.banks("v"), ph.banks("h"), ph.banks("o")
        block = ph.ctx.enter_context(nc.Block())

        @block.sync
        def _(sp):
            def body(i, u):
                if live(i, S):
                    if begun(i - 4):
                        sp.wait_ge(vt_ready, i - 3)
                    sp.dma_start(at(ut, u)[:, :], cols_of(scratch["ut"], i)).then_inc(at(ut_in, u), 16)
                    if begun(i - 4):
                        sp.wait_ge(x2_ready, i - 3)
                    sp.dma_start(flat(at(x1, u)), rows_of(scratch["x1"], i)).then_inc(at(x1_in, u), 16)
                j = i - 5
                if live(j, S):
                    sp.wait_ge(own_ready, j + 1)
                    sp.dma_start(rows_of(scratch["sum"][0:size.rows, :], j), flat(at(own, u - 5))
                                 ).then_inc(at(own_out, u - 5), 16)
            run_steps(sp, body, S, 5)
            for u in range(SLOTS):
                sp.wait_ge(own_out[u], all_moved(S, u))

        @block.scalar
        def _(act):
            bn.scalar(act, k)

            def body(i, u):
                if live(i, S):
                    act.wait_ge(at(ut_in, u), moved(i, u))
                    if begun(i - 2):
                        act.wait_ge(turned_back, i - 1)
                    act.activation(at(vt, u)[:, :], at(ut, u)[:, :], ACT.Identity, bias=k.bn2_shift[:, :],
                                   scale=k.bn2_scale[:, :]).then_inc(vt_ready, 1)
                j = i - 3
                if live(j, S):
                    act.wait_ge(h2_ready, j + 1)
                    act.dma_start(rows_of(scratch["h2"], j), flat(at(h2, u - 3))).then_inc(at(h2_out, u - 3), 16)
                    act.wait_ge(h2_turned, j + 1)
                    if begun(j - 2):
                        act.wait_ge(own_done, j - 1)
                    act.activation(at(h2t, u - 3)[:, :, :], at(ps_h, u - 3)[:, :, :], ACT.Copy).then_inc(h2t_ready, 1)
                j = i - 2
                if live(j, S):
                    act.wait_ge(x2_ready, j + 1)
                    act.dma_start(rows_of(scratch["x2"], j), flat(at(x2, u - 2))).then_inc(at(x2_out, u - 2), 16)
                    if begun(j - 4):
                        act.wait_ge(at(h2_out, u - 2), moved(j - 4, u - 2))
                    if begun(j - 4):
                        act.wait_ge(h2_turned, j - 3)
                    norm.apply(act, at(h2, u - 2), at(x2, u - 2), ACT.Relu, j, u - 2).then_inc(h2_ready, 1)
                j = i - 1
                if live(j, S):
                    norm.std_of(act, k, j, u - 1)
            run_steps(act, body, S, 3)
            for u in range(SLOTS):
                act.wait_ge(x2_out[u], all_moved(S, u))
            for u in range(SLOTS):
                act.wait_ge(h2_out[u], all_moved(S, u))

        @block.tensor
        def _(pe):
            def body(i, u):
                if live(i, S):
                    pe.wait_ge(vt_ready, i + 1)
                    if begun(i - 2):
                        pe.wait_ge(x2_ready, i - 1)
                    for t in range(TILES):
                        ins = pe.transpose(at(ps_v, u)[:, t, :], at(vt, u)[:, t * P:(t + 1) * P], k.ident[:, :])
                    ins.then_inc(turned_back, 1)
                j = i - 3
                if live(j, S):
                    pe.wait_ge(h2t_ready, j + 1)
                    if begun(j - 2):
                        pe.wait_ge(own_ready, j - 1)
                    for t in range(TILES):
                        ins = pe.matmul(at(ps_o, u - 3)[:, t, :], at(h2t, u - 3)[:, t, :], k.w_center_cat[:, :],
                                        start=True, stop=True)
                    ins.then_inc(own_done, 1)
                j = i - 2
                if live(j, S):
                    pe.wait_ge(h2_ready, j + 1)
                    if begun(j - 2):
                        pe.wait_ge(h2t_ready, j - 1)
                    for t in range(TILES):
                        ins = pe.transpose(at(ps_h, u)[:, t, :], at(h2, u - 2)[:, t, :], k.ident[:, :])
                    ins.then_inc(h2_turned, 1)
            run_steps(pe, body, S, 3)

        @block.vector
        def _(dve):
            bn.vector(dve)

            def body(i, u):
                if live(i - 2, S):
                    norm.scale_of(dve, i - 2, u - 2, h2_ready)
                j = i - 1
                if live(j, S):
                    dve.wait_ge(turned_back, j + 1)
                    dve.wait_ge(at(x1_in, u - 1), moved(j, u - 1))
                    if begun(j - 4):
                        dve.wait_ge(at(x2_out, u - 1), moved(j - 4, u - 1))
                    if begun(j - 4):
                        dve.wait_ge(h2_ready, j - 3)
                    dve.tensor_tensor(at(x2, u - 1)[:, :, :], at(ps_v, u - 1)[:, :, :], at(x1, u - 1)[:, :, :],
                                      ALU.add).then_inc(x2_ready, 1)
                    dve.wait_ge(x2_ready, j + 1)
                    norm.moments_of(dve, at(x2, u - 1), j, u - 1)
                j = i - 4
                if live(j, S):
                    dve.wait_ge(own_done, j + 1)
                    if begun(j - 4):
                        dve.wait_ge(at(own_out, u), moved(j - 4, u))
                    dve.tensor_copy(at(own, u)[:, :, :], at(ps_o, u)[:, :, :]).then_inc(own_ready, 1)
            run_steps(dve, body, S, 4)


def gated_edges(nc, size, a, scratch, k):
    S = size.steps
    with Phase(nc, "e2") as ph:
        idx, idx_in = ph.loaded("idx", [P, 2 * TILES], I32)
        edge, edge_in = ph.loaded("edge", [EDGE_DIM, ROWS])
        keys, keys_in = ph.loaded("keys", [P, ROWS], I32)
        hd, hd_in = ph.loaded("hd", [P, TILES, D])
        mine, mine_ready = ph.made("mine", [P, TILES])
        keys_f, keys_ready = ph.made("keys_f", [P, ROWS])
        hdt, hdt_ready = ph.made("hdt", [D, TILES, P])
        gate, gate_ready = ph.made("gate", [P, TILES, D])
        msg, msg_ready = ph.made("msg", [P, TILES, D])
        same, same_ready = ph.made("same", [P, TILES, ROWS])
        spare = ph.slots(TILES, "spare", [P, ROWS])
        last_place, last_ready = ph.made("last_place", [P, TILES])
        chosen, chosen_ready = ph.made("chosen", [P, TILES])
        gap, gap_ready = ph.made("gap", [P, TILES])
        shift, shift_ready = ph.made("shift", [P, TILES])
        target, target_ready = ph.made("target", [P, TILES], 4, I32)
        sums, sums_ready = ph.made("sums", [D, TILES, P])
        res, res_ready = ph.made("res", [P, TILES, D], 4)
        added = ph.dma_sems("added")
        pool_turn, sp_turn, dve_turn = ph.sem("pool_turn"), ph.sem("sp_turn"), ph.sem("dve_turn")
        turned, proj_done, gate_done = ph.sem("turned"), ph.sem("proj_done"), ph.sem("gate_done")
        sums_done, out_done = ph.sem("sums_done"), ph.sem("out_done")
        ps_t, ps_s, ps_r = ph.banks("t"), ph.banks("s"), ph.banks("r")
        ps_p, ps_g = ph.ps("p"), ph.ps("g")
        block = ph.ctx.enter_context(nc.Block())

        @block.sync
        def _(sp):
            def body(i, u):
                if live(i, S):
                    if begun(i - 4):
                        sp.wait_ge(at(hd_in, u), moved(i - 4, u, TILES))
                    sp.sem_inc(sp_turn, 1)
                    if begun(i - 4):
                        sp.wait_ge(mine_ready, i - 3)
                    sp.dma_start(at(idx, u)[:, :], idx_of(a, i)).then_inc(at(idx_in, u), 16)
                    if begun(i - 4):
                        sp.wait_ge(gate_done, i - 3)
                    sp.dma_start(at(edge, u)[:, :], cols_of(a["edge32T"], i)).then_inc(at(edge_in, u), 16)
                    if begun(i - 4):
                        sp.wait_ge(keys_ready, i - 3)
                    sp.dma_start(at(keys, u)[:, :], a["src_lin"][bass.ds(i, 1), :].rearrange(
                        "a c -> (a c)").partition_broadcast(P)).then_inc(at(keys_in, u), 16)
            run_steps(sp, body, S, 0)

        @block.gpsimd
        def _(pool):
            def body(i, u):
                if live(i, S):
                    pool.wait_ge(at(idx_in, u), moved(i, u))
                    if begun(i - 4):
                        pool.wait_ge(turned, i - 3)
                    pool.sem_inc(pool_turn, 1)
                    gather(pool, at(hd, u), scratch["h2"], at(idx, u), TILES, at(hd_in, u))
                j = i - 4
                if live(j, S):
                    pool.wait_ge(target_ready, j + 1)
                    pool.wait_ge(res_ready, j + 1)
                    if begun(j - 1):
                        pool.wait_ge(at(added, u - 1), moved(j - 1, u - 1, TILES))
                    pool.sem_inc(pool_turn, 1)
                    for t in range(TILES):
                        pool.indirect_dma_start(out=scratch["sum"], out_offset=bass.IndirectOffsetOnAxis(
                            ap=at(target, u)[:, t:t + 1], axis=0), in_=at(res, u)[:, t, :], in_offset=None,
                            compute_op=ALU.add).then_inc(at(added, u), 16)
            run_steps(pool, body, S, 4)
            for u in range(SLOTS):
                pool.wait_ge(added[u], all_moved(S, u, TILES))

        @block.vector
        def _(dve):
            def body(i, u):
                if live(i, S):
                    dve.wait_ge(at(idx_in, u), moved(i, u))
                    if begun(i - 2):
                        dve.wait_ge(shift_ready, i - 1)
                    dve.tensor_copy(at(mine, u)[:, :], at(idx, u)[:, 0:TILES]).then_inc(mine_ready, 1)
                    dve.wait_ge(at(keys_in, u), moved(i, u))
                    if begun(i - 2):
                        dve.wait_ge(same_ready, i - 1)
                    dve.tensor_copy(at(keys_f, u)[:, :], at(keys, u)[:, :]).then_inc(keys_ready, 1)
                    dve.wait_ge(mine_ready, i + 1)
                    dve.wait_ge(keys_ready, i + 1)
                    if begun(i - 2):
                        dve.wait_ge(sums_done, i - 1)
                    for t in range(TILES):
                        ins = dve.tensor_scalar(at(same, u)[:, t, :], at(keys_f, u)[:, :], at(mine, u)[:, t:t + 1],
                                                None, ALU.is_equal)
                    ins.then_inc(same_ready, 1)
                j = i - 1
                if live(j, S):
                    dve.wait_ge(proj_done, j + 1)
                    dve.wait_ge(gate_ready, j + 1)
                    if begun(j - 2):
                        dve.wait_ge(sums_done, j - 1)
                    dve.tensor_tensor(at(msg, u - 1)[:, :, :], ps_p[:, :, :], at(gate, u - 1)[:, :, :], ALU.mult
                                      ).then_inc(msg_ready, 1)
                if live(i, S):
                    dve.wait_ge(same_ready, i + 1)
                    if begun(i - 1):
                        dve.wait_ge(last_ready, i)
                    dve.sem_inc(dve_turn, 1)
                    for t in range(TILES):
                        ins = dve.tensor_tensor_reduce(spare[t][:, :], at(same, u)[:, t, :], k.place_row[:, :], 1.0,
                                                       0.0, ALU.mult, ALU.max, at(last_place, u)[:, t:t + 1])
                    ins.then_inc(last_ready, 1)
                    dve.tensor_tensor(at(gap, u)[:, :], at(mine, u)[:, :], k.dump_row[:, :], ALU.subtract
                                      ).then_inc(gap_ready, 1)
                    dve.wait_ge(last_ready, i + 1)
                    dve.tensor_tensor(at(chosen, u)[:, :], at(last_place, u)[:, :], k.place[:, :], ALU.is_equal
                                      ).then_inc(chosen_ready, 1)
                    dve.wait_ge(gap_ready, i + 1)
                    dve.wait_ge(chosen_ready, i + 1)
                    dve.tensor_tensor(at(shift, u)[:, :], at(gap, u)[:, :], at(chosen, u)[:, :], ALU.mult
                                      ).then_inc(shift_ready, 1)
                    dve.wait_ge(shift_ready, i + 1)
                    if begun(i - 4):
                        dve.wait_ge(at(added, u), moved(i - 4, u, TILES))
                    dve.tensor_tensor(at(target, u)[:, :], at(shift, u)[:, :], k.dump_row[:, :], ALU.add
                                      ).then_inc(target_ready, 1)
            run_steps(dve, body, S, 1)

        @block.scalar
        def _(act):
            def body(i, u):
                j = i - 1
                if live(j, S):
                    act.wait_ge(gate_done, j + 1)
                    if begun(j - 2):
                        act.wait_ge(msg_ready, j - 1)
                    act.activation(at(gate, u - 1)[:, :, :], ps_g[:, :, :], ACT.Copy).then_inc(gate_ready, 1)
                j = i - 2
                if live(j, S):
                    act.wait_ge(out_done, j + 1)
                    if begun(j - 4):
                        act.wait_ge(at(added, u - 2), moved(j - 4, u - 2, TILES))
                    act.activation(at(res, u - 2)[:, :, :], at(ps_r, u)[:, :, :], ACT.Copy).then_inc(res_ready, 1)
                if live(i, S):
                    act.wait_ge(turned, i + 1)
                    if begun(i - 2):
                        act.wait_ge(proj_done, i - 1)
                    act.activation(at(hdt, u)[:, :, :], at(ps_t, u)[:, :, :], ACT.Copy).then_inc(hdt_ready, 1)
                j = i - 1
                if live(j, S):
                    act.wait_ge(sums_done, j + 1)
                    if begun(j - 2):
                        act.wait_ge(out_done, j - 1)
                    act.activation(at(sums, u - 1)[:, :, :], at(ps_s, u - 1)[:, :, :], ACT.Copy
                                   ).then_inc(sums_ready, 1)
            run_steps(act, body, S, 2)

        @block.tensor
        def _(pe):
            def body(i, u):
                j = i - 1
                if live(j, S):
                    pe.wait_ge(at(edge_in, u - 1), moved(j, u - 1))
                    if begun(j - 1):
                        pe.wait_ge(gate_ready, j)
                    for t in range(TILES):
                        ins = pe.matmul(ps_g[:, t, :], at(edge, u - 1)[:, t * P:(t + 1) * P], k.w_edge[:, :],
                                        start=True, stop=True)
                    ins.then_inc(gate_done, 1)
                    pe.wait_ge(hdt_ready, j + 1)
                    if begun(j - 1):
                        pe.wait_ge(msg_ready, j)
                    for t in range(TILES):
                        ins = pe.matmul(ps_p[:, t, :], at(hdt, u - 1)[:, t, :], k.w_node[:, :], start=True, stop=True)
                    ins.then_inc(proj_done, 1)
                j = i - 2
                if live(j, S):
                    pe.wait_ge(sums_ready, j + 1)
                    if begun(j - 2):
                        pe.wait_ge(res_ready, j - 1)
                    for t in range(TILES):
                        ins = pe.matmul(at(ps_r, u)[:, t, :], at(sums, u)[:, t, :], k.w_cat_sum[:, :], start=True,
                                        stop=True)
                    ins.then_inc(out_done, 1)
                if live(i, S):
                    pe.wait_ge(at(hd_in, u), moved(i, u, TILES))
                    if begun(i - 2):
                        pe.wait_ge(hdt_ready, i - 1)
                    for t in range(TILES):
                        ins = pe.transpose(at(ps_t, u)[:, t, :], at(hd, u)[:, t, :], k.ident[:, :])
                    ins.then_inc(turned, 1)
                j = i - 1
                if live(j, S):
                    pe.wait_ge(msg_ready, j + 1)
                    pe.wait_ge(same_ready, j + 1)
                    if begun(j - 2):
                        pe.wait_ge(sums_ready, j - 1)
                    for t in range(TILES):
                        ins = pe.matmul(flat(at(ps_s, u - 1)), at(msg, u - 1)[:, t, :], at(same, u - 1)[:, t, :],
                                        start=(t == 0), stop=(t == TILES - 1))
                    ins.then_inc(sums_done, 1)
            run_steps(pe, body, S, 2)


def gated_nodes(nc, size, scratch, k):
    S = size.steps
    with Phase(nc, "n4") as ph:
        z, z_in = ph.loaded("z", [P, TILES, D])
        x2, x2_in = ph.loaded("x2", [P, TILES, D])
        zn, zn_ready = ph.made("zn", [P, TILES, D])
        zw, zw_ready = ph.made("zw", [P, TILES, D])
        xb, xb_ready = ph.made("xb", [P, TILES, D], 4)
        x3, x3_ready = ph.made("x3", [P, TILES, D], 4)
        h3, h3_ready = ph.made("h3", [P, TILES, D], 4)
        x3_out, h3_out = ph.dma_sems("x3_out"), ph.dma_sems("h3_out")
        pool_turn = ph.sem("pool_turn")
        first, second = Norm(ph, "first"), Norm(ph, "second")
        block = ph.ctx.enter_context(nc.Block())

        @block.sync
        def _(sp):
            def body(i, u):
                if live(i, S):
                    if begun(i - 4):
                        sp.wait_ge(zn_ready, i - 3)
                    sp.dma_start(flat(at(z, u)), rows_of(scratch["sum"][0:size.rows, :], i)).then_inc(at(z_in, u), 16)
                    if begun(i - 4):
                        sp.wait_ge(xb_ready, i - 3)
                    sp.dma_start(flat(at(x2, u)), rows_of(scratch["x2"], i)).then_inc(at(x2_in, u), 16)
            run_steps(sp, body, S, 0)

        @block.gpsimd
        def _(pool):
            def body(i, u):
                if live(i, S):
                    pool.wait_ge(at(x2_in, u), moved(i, u))
                    if begun(i - 4):
                        pool.wait_ge(x3_ready, i - 3)
                    pool.sem_inc(pool_turn, 1)
                    pool.tensor_tensor(at(xb, u)[:, :, :], at(x2, u)[:, :, :], k.ln_b_rep[:, :, :], ALU.add
                                       ).then_inc(xb_ready, 1)
                j = i - 1
                if live(j, S):
                    pool.wait_ge(zn_ready, j + 1)
                    if begun(j - 2):
                        pool.wait_ge(x3_ready, j - 1)
                    pool.sem_inc(pool_turn, 1)
                    pool.tensor_tensor(at(zw, u - 1)[:, :, :], at(zn, u - 1)[:, :, :], k.ln_w_rep[:, :, :], ALU.mult
                                       ).then_inc(zw_ready, 1)
            run_steps(pool, body, S, 1)

        @block.vector
        def _(dve):
            def body(i, u):
                if live(i - 1, S):
                    first.scale_of(dve, i - 1, u - 1, zn_ready)
                if live(i - 3, S):
                    second.scale_of(dve, i - 3, u - 3, h3_ready)
                if live(i, S):
                    dve.wait_ge(at(z_in, u), moved(i, u))
                    first.moments_of(dve, at(z, u), i, u)
                j = i - 2
                if live(j, S):
                    dve.wait_ge(zw_ready, j + 1)
                    dve.wait_ge(xb_ready, j + 1)
                    if begun(j - 4):
                        dve.wait_ge(at(x3_out, u - 2), moved(j - 4, u - 2))
                    if begun(j - 4):
                        dve.wait_ge(h3_ready, j - 3)
                    dve.tensor_tensor(at(x3, u - 2)[:, :, :], at(zw, u)[:, :, :], at(xb, u - 2)[:, :, :], ALU.add
                                      ).then_inc(x3_ready, 1)
                    dve.wait_ge(x3_ready, j + 1)
                    second.moments_of(dve, at(x3, u - 2), j, u - 2)
            run_steps(dve, body, S, 3)

        @block.scalar
        def _(act):
            def body(i, u):
                if live(i - 1, S):
                    if begun(i - 3):
                        act.wait_ge(zw_ready, i - 2)
                    first.apply(act, at(zn, u - 1), at(z, u - 1), ACT.Identity, i - 1, u - 1).then_inc(zn_ready, 1)
                j = i - 3
                if live(j, S):
                    act.wait_ge(x3_ready, j + 1)
                    act.dma_start(rows_of(scratch["x3"], j), flat(at(x3, u - 3))).then_inc(at(x3_out, u - 3), 16)
                    if begun(j - 4):
                        act.wait_ge(at(h3_out, u - 3), moved(j - 4, u - 3))
                    second.apply(act, at(h3, u - 3), at(x3, u - 3), ACT.Relu, j, u - 3).then_inc(h3_ready, 1)
                if live(i, S):
                    first.std_of(act, k, i, u)
                if live(i - 2, S):
                    second.std_of(act, k, i - 2, u - 2)
                j = i - 4
                if live(j, S):
                    act.wait_ge(h3_ready, j + 1)
                    act.dma_start(rows_of(scratch["h3"], j), flat(at(h3, u))).then_inc(at(h3_out, u), 16)
            run_steps(act, body, S, 4)
            for u in range(SLOTS):
                act.wait_ge(x3_out[u], all_moved(S, u))
            for u in range(SLOTS):
                act.wait_ge(h3_out[u], all_moved(S, u))


def relation_edges(nc, size, a, scratch, k):
    S = size.steps
    with Phase(nc, "e3") as ph:
        idx, idx_in = ph.loaded("idx", [P, 2 * TILES], I32)
        col, col_in = ph.loaded("col", [1, 3, ROWS], BF16)
        row, row_in = ph.loaded("row", [P, 3 * TILES], I32)
        again, again_in = ph.loaded("again", [P, 3 * TILES], I32)
        hs, hs_in = ph.loaded("hs", [P, TILES, D])
        part, part_ready = ph.made("part", [P, TILES, D])
        hst, hst_ready = ph.made("hst", [D, ROWS])
        by_rel, by_rel_ready = ph.made("by_rel", [D, RELS, ROWS])
        msg, msg_ready = ph.made("msg", [D, ROWS])
        run, run_ready = ph.made("run", [D, ROWS])
        res, res_ready = ph.made("res", [P, TILES, D], 4)
        scattered = ph.dma_sems("scattered")
        pool_turn = ph.sem("pool_turn")
        turned, type_done, keep_done = ph.sem("turned"), ph.sem("type_done"), ph.sem("keep_done")
        msg_done, out_done = ph.sem("msg_done"), ph.sem("out_done")
        ps_t, ps_y = ph.ps("t"), ph.ps("y")
        ps_k, ps_m, ps_r = ph.banks("k"), ph.banks("m"), ph.banks("r")
        block = ph.ctx.enter_context(nc.Block())

        @block.sync
        def _(sp):
            def body(i, u):
                if live(i, S):
                    if begun(i - 4):
                        sp.wait_ge(at(hs_in, u), moved(i - 4, u, TILES))
                    sp.dma_start(at(idx, u)[:, :], idx_of(a, i)).then_inc(at(idx_in, u), 16)
                    if begun(i - 4):
                        sp.wait_ge(keep_done, i - 3)
                    sp.dma_start(flat(at(col, u)), col_values_of(scratch, i)).then_inc(at(col_in, u), 16)
                    if begun(i - 4):
                        sp.wait_ge(part_ready, i - 3)
                    sp.dma_start(at(row, u)[:, :], row_values_of(scratch, i)).then_inc(at(row_in, u), 16)
                j = i - 2
                if live(j, S):
                    if begun(j - 4):
                        sp.wait_ge(at(scattered, u - 2), moved(j - 4, u - 2, TILES))
                    sp.dma_start(at(again, u - 2)[:, :], row_values_of(scratch, j)).then_inc(at(again_in, u - 2), 16)
            run_steps(sp, body, S, 2)

        @block.gpsimd
        def _(pool):
            def body(i, u):
                if live(i, S):
                    pool.wait_ge(at(idx_in, u), moved(i, u))
                    if begun(i - 4):
                        pool.wait_ge(part_ready, i - 3)
                    pool.sem_inc(pool_turn, 1)
                    gather(pool, at(hs, u), scratch["h3"], at(idx, u), 0, at(hs_in, u))
                j = i - 4
                if live(j, S):
                    pool.wait_ge(at(again_in, u), moved(j, u))
                    pool.wait_ge(res_ready, j + 1)
                    pool.sem_inc(pool_turn, 1)
                    scatter(pool, scratch["agg"], at(res, u), at(again, u), size.rows - 1, at(scattered, u))
            run_steps(pool, body, S, 4)
            for u in range(SLOTS):
                pool.wait_ge(scattered[u], all_moved(S, u, TILES))

        @block.vector
        def _(dve):
            def body(i, u):
                if live(i, S):
                    dve.wait_ge(at(hs_in, u), moved(i, u, TILES))
                    dve.wait_ge(at(row_in, u), moved(i, u))
                    if begun(i - 2):
                        dve.wait_ge(turned, i - 1)
                    dve.tensor_tensor(at(part, u)[:, :, :], at(hs, u)[:, :, :],
                                      spread(at(row, u)[:, 2 * TILES:3 * TILES].bitcast(F32), D), ALU.mult
                                      ).then_inc(part_ready, 1)
                j = i - 2
                if live(j, S):
                    dve.wait_ge(msg_ready, j + 1)
                    dve.wait_ge(keep_done, j + 1)
                    if begun(j - 2):
                        dve.wait_ge(out_done, j - 1)
                    if begun(j - 1):
                        dve.wait_ge(run_ready, j)
                    before = 0.0 if isinstance(j, int) and j == 0 else at(run, u - 1)[:, ROWS - 1:ROWS]
                    dve.tensor_tensor_scan(at(run, u)[:, :], flat(at(ps_k, u)), at(msg, u)[:, :], before, ALU.mult,
                                           ALU.add).then_inc(run_ready, 1)
                if live(i, S):
                    dve.wait_ge(hst_ready, i + 1)
                    dve.wait_ge(type_done, i + 1)
                    if begun(i - 2):
                        dve.wait_ge(msg_done, i - 1)
                    for r in range(RELS):
                        ins = dve.scalar_tensor_tensor(at(by_rel, u)[:, r, :], flat(ps_y), float(r), at(hst, u)[:, :],
                                                       ALU.is_equal, ALU.mult)
                    ins.then_inc(by_rel_ready, 1)
            run_steps(dve, body, S, 2)

        @block.scalar
        def _(act):
            def body(i, u):
                if live(i, S):
                    act.wait_ge(turned, i + 1)
                    if begun(i - 2):
                        act.wait_ge(by_rel_ready, i - 1)
                    act.activation(at(hst, u)[:, :], flat(ps_t), ACT.Copy).then_inc(hst_ready, 1)
                j = i - 3
                if live(j, S):
                    act.wait_ge(out_done, j + 1)
                    if begun(j - 4):
                        act.wait_ge(at(scattered, u - 3), moved(j - 4, u - 3, TILES))
                    act.activation(at(res, u - 3)[:, :, :], at(ps_r, u - 3)[:, :, :], ACT.Copy).then_inc(res_ready, 1)
                j = i - 1
                if live(j, S):
                    act.wait_ge(msg_done, j + 1)
                    if begun(j - 2):
                        act.wait_ge(run_ready, j - 1)
                    act.activation(at(msg, u - 1)[:, :], flat(at(ps_m, u - 1)), ACT.Copy).then_inc(msg_ready, 1)
            run_steps(act, body, S, 3)

        @block.tensor
        def _(pe):
            def body(i, u):
                if live(i, S):
                    pe.wait_ge(at(col_in, u), moved(i, u))
                    if begun(i - 1):
                        pe.wait_ge(by_rel_ready, i)
                    pe.matmul(flat(ps_y), k.ones_row[:, :], at(col, u)[:, 1, :], start=True, stop=True
                              ).then_inc(type_done, 1)
                    pe.wait_ge(part_ready, i + 1)
                    if begun(i - 1):
                        pe.wait_ge(hst_ready, i)
                    for t in range(TILES):
                        ins = pe.transpose(ps_t[:, t, :], at(part, u)[:, t, :], k.ident[:, :])
                    ins.then_inc(turned, 1)
                j = i - 1
                if live(j, S):
                    pe.wait_ge(by_rel_ready, j + 1)
                    if begun(j - 2):
                        pe.wait_ge(msg_ready, j - 1)
                    for r in range(RELS):
                        ins = pe.matmul(flat(at(ps_m, u - 1)), k.rel_w[:, r, :], at(by_rel, u - 1)[:, r, :],
                                        start=(r == 0), stop=(r == RELS - 1))
                    ins.then_inc(msg_done, 1)
                    if begun(j - 2):
                        pe.wait_ge(run_ready, j - 1)
                    pe.matmul(flat(at(ps_k, u - 1)), k.ones_row[:, :], at(col, u - 1)[:, 0, :], start=True, stop=True
                              ).then_inc(keep_done, 1)
                j = i - 2
                if live(j, S):
                    pe.wait_ge(run_ready, j + 1)
                    if begun(j - 2):
                        pe.wait_ge(res_ready, j - 1)
                    for t in range(TILES):
                        ins = pe.transpose(at(ps_r, u)[:, t, :], at(run, u)[:, t * P:(t + 1) * P], k.ident[:, :])
                    ins.then_inc(out_done, 1)
            run_steps(pe, body, S, 2)


def relation_nodes(nc, size, scratch, out, k):
    S = size.steps
    with Phase(nc, "n5") as ph:
        x3, x3_in = ph.loaded("x3", [P, TILES, D])
        agg, agg_in = ph.loaded("agg", [P, TILES, D])
        xb, xb_ready = ph.made("xb", [P, TILES, D])
        res, res_ready = ph.made("res", [P, TILES, D], 4)
        res_out = ph.dma_sems("res_out")
        block = ph.ctx.enter_context(nc.Block())

        @block.sync
        def _(sp):
            def body(i, u):
                if live(i, S):
                    if begun(i - 4):
                        sp.wait_ge(xb_ready, i - 3)
                    sp.dma_start(flat(at(x3, u)), rows_of(scratch["x3"], i)).then_inc(at(x3_in, u), 16)
                    if begun(i - 4):
                        sp.wait_ge(res_ready, i - 3)
                    sp.dma_start(flat(at(agg, u)), rows_of(scratch["agg"], i)).then_inc(at(agg_in, u), 16)
            run_steps(sp, body, S, 0)

        @block.vector
        def _(dve):
            def body(i, u):
                if live(i, S):
                    dve.wait_ge(at(x3_in, u), moved(i, u))
                    if begun(i - 2):
                        dve.wait_ge(res_ready, i - 1)
                    dve.tensor_tensor(at(xb, u)[:, :, :], at(x3, u)[:, :, :], k.rel_b_rep[:, :, :], ALU.add
                                      ).then_inc(xb_ready, 1)
                    dve.wait_ge(xb_ready, i + 1)
                    dve.wait_ge(at(agg_in, u), moved(i, u))
                    if begun(i - 4):
                        dve.wait_ge(at(res_out, u), moved(i - 4, u))
                    dve.tensor_tensor(at(res, u)[:, :, :], at(xb, u)[:, :, :], at(agg, u)[:, :, :], ALU.add
                                      ).then_inc(res_ready, 1)
            run_steps(dve, body, S, 0)

        @block.scalar
        def _(act):
            def body(i, u):
                if live(i, S):
                    act.wait_ge(res_ready, i + 1)
                    act.dma_start(rows_of(out, i), flat(at(res, u))).then_inc(at(res_out, u), 16)
            run_steps(act, body, S, 0)
            for u in range(SLOTS):
                act.wait_ge(res_out[u], all_moved(S, u))


def padded(a, rows, fill):
    out = np.full((rows, *a.shape[1:]), fill, a.dtype)
    out[:a.shape[0]] = a
    return out


def kernel(**inputs):
    from concourse import bacc
    from concourse.bass_utils import run_bass_kernel_spmd

    g = {n: np.asarray(v) for n, v in inputs.items()}
    nodes, edges = g["x"].shape[0], g["src"].shape[0]
    size = Sizes(nodes, edges)
    S, R = size.steps, size.rows
    i32 = np.int32

    src = padded(g["src"].astype(i32, copy=False), R, nodes)
    dst = padded(g["dst"].astype(i32, copy=False), R, nodes)
    kind = padded(g["edge_type_8"].astype(i32, copy=False), R, 0)
    before = np.concatenate([np.full(1, -1, i32), dst[:-1]])
    behind = np.concatenate([dst[1:], np.full(1, -1, i32)])

    def by_place(v):
        return v.reshape(S, TILES, P).transpose(2, 0, 1)

    col = lambda v: v.reshape(-1, 1)
    row = lambda v: v.reshape(1, -1)
    arrays = {
        "x": padded(g["x"], R, 0),
        "edge128T": padded(g["edge_attr_128"], R, 0).T,
        "edge32T": padded(g["edge_attr_32"], R, 0).T,
        "idx": np.concatenate([by_place(src), by_place(dst)], axis=2).reshape(P, S * 2 * TILES),
        "edge_lin": np.stack([v.reshape(S, ROWS) for v in (dst, before, behind, kind)]),
        "src_lin": src.reshape(S, ROWS),
        "edge_rows": np.stack([by_place(dst).reshape(P, -1), by_place(behind).reshape(P, -1)], axis=1),
        "L0_W1": g["L0_gnn_W1"], "L0_W2": g["L0_gnn_W2"], "L0_b1": col(g["L0_gnn_b1"]), "L0_b2": row(g["L0_gnn_b2"]),
        "L1_WkT": g["L1_gnn_Wk"].T, "L1_WvT": g["L1_gnn_Wv"].T, "L1_WoT": g["L1_gnn_Wo"].T,
        "L1_bk": col(g["L1_gnn_bk"]), "L1_bv": col(g["L1_gnn_bv"]), "L1_bo": col(g["L1_gnn_bo"]),
        "L1_W1T": g["L1_gnn_W1"].T, "L1_W2T": g["L1_gnn_W2"].T,
        "L1_b1": g["L1_gnn_b1"].reshape(2, D).T, "L1_b2": col(g["L1_gnn_b2"]),
        "L1_bn": np.stack([g["L1_gnn_bn1_g"], g["L1_gnn_bn1_b"], g["L1_gnn_bn2_g"], g["L1_gnn_bn2_b"]], axis=1),
        "L2_W_node": g["L2_gnn_W_node"], "L2_W_centerT": g["L2_gnn_W_center_node"].T,
        "L2_W_cat": g["L2_gnn_W_concat_node"], "L2_W_edge": g["L2_gnn_W_edge"],
        "L2_ln_w": row(g["L2_gnn_ln_weight"]), "L2_ln_b": row(g["L2_gnn_ln_bias"]),
        "L3_W": g["L3_gnn_weight"], "L3_b": row(g["L3_gnn_bias"]),
    }
    arrays = {n: np.ascontiguousarray(v) for n, v in arrays.items()}

    nc = bacc.Bacc("TRN2", target_bir_lowering=False, num_devices=1)
    a = {n: nc.dram_tensor(n, v.shape, mybir.dt.from_np(v.dtype), kind="ExternalInput").ap() for n, v in arrays.items()}
    out = nc.dram_tensor("out", (R, D), F32, kind="ExternalOutput").ap()

    def table(name, shape, dt=F32):
        return nc.dram_tensor(f"{name}_table", shape, dt).ap()

    scratch = {n: table(n, (R, D)) for n in ("agg", "x1", "h1", "x2", "h2", "x3", "h3")}
    scratch["sum"] = table("sum", (R + ROWS, D))
    scratch["tt"] = table("tt", (D, R))
    scratch["ut"] = table("ut", (D, R))
    scratch["col_tab"] = table("col_tab", (S, 3, ROWS), BF16)
    scratch["row_tab"] = table("row_tab", (P, S, 12), I32)
    build(nc, size, a, out, scratch)
    r = run_bass_kernel_spmd(nc, [arrays], core_ids=[0])
    return r.results[0]["out"][:nodes]
```
